# Optimizing a Trainium2 kernel written in Bass

```python
import numpy as np
import jax
import jax.numpy as jnp

def _softmax(x, axis=-1):
    return jax.nn.softmax(x, axis=axis)

def _gelu(x):
    return jax.nn.gelu(x, approximate=True)

def _silu(x):
    return jax.nn.silu(x)

def _sigmoid(x):
    return jax.nn.sigmoid(x)

def _layernorm(x, axis=-1, eps=1e-05):
    m = jnp.mean(x, axis=axis, keepdims=True)
    v = jnp.var(x, axis=axis, keepdims=True)
    return (x - m) / jnp.sqrt(v + eps)

def _scatter_add(tgt, idx, src, axis=0):
    return tgt.at[idx].add(src)

def _segment_sum(src, seg, n):
    return jax.ops.segment_sum(src, seg, n)
kernel_name = 'mk_xattn_seq_d4_seqx_r8_8b941d'

def setup_inputs(seed: int=0):
    np.random.seed(seed)
    _w = jnp.asarray

    def _rec_inputs():
        import jax
        import jax.numpy as jnp
        _rk = jax.random.key(seed)
        x = 7.22e-05 + 1 * jax.random.normal(jax.random.fold_in(_rk, 1), (8, 256, 256), jnp.float32)
        _lenS = 256 - jax.random.randint(jax.random.fold_in(_rk, 7), (8,), 0, max(1, 256 // 4) + 1, jnp.int32)
        _lenS2 = 1601 - jax.random.randint(jax.random.fold_in(_rk, 8), (8,), 0, max(1, 1601 // 4) + 1, jnp.int32)
        _ctx_1024P = jax.random.normal(jax.random.fold_in(_rk, 11), (8, 16, 128), jnp.float32)
        _ctx_1024c = jax.random.dirichlet(jax.random.fold_in(_rk, 511), 0.3 * jnp.ones((16,), jnp.float32), (8, 1601))
        _ctx_1024t = jnp.einsum('bsk,bkd->bsd', _ctx_1024c, _ctx_1024P)
        _ctx_1024t = _ctx_1024t * jax.lax.rsqrt(jnp.mean(jnp.square(_ctx_1024t)) + 1e-12) * 0.953939
        ctx_1024 = -0.000514642 + 1.00011 * (_ctx_1024t + 0.3 * jax.random.normal(jax.random.fold_in(_rk, 611), (8, 1601, 128), jnp.float32))
        pos_1xS = jnp.broadcast_to(jnp.arange(256, dtype=jnp.int32), (1, 256))
        _validS = jnp.arange(256)[None, :] < _lenS[:, None]
        _validS2 = jnp.arange(1601)[None, :] < _lenS2[:, None]
        _causal = jnp.tril(jnp.ones((256, 256), dtype=bool))
        mask_BxS_ik0 = jnp.where(jnp.broadcast_to(_validS[:, :], (8, 256)), 0, 1).astype(jnp.int32)
        mask_BxS2_bk0 = jnp.logical_not(jnp.broadcast_to(_validS2[:, :], (8, 1601)))
        return (x, ctx_1024, pos_1xS, mask_BxS_ik0, mask_BxS2_bk0)
    x, ctx_1024, pos_1xS, mask_BxS_ik0, mask_BxS2_bk0 = _rec_inputs()

    def _L0_xattn_setup():
        import jax, jax.numpy as jnp
        import numpy as np
        H = 256
        NH = 16
        HD = H // NH
        CH = 128
        CC = 128
        CHD = CC // NH
        I = 688
        B = 2
        L = 256
        LE = 128
        EPS = 1e-06

        def rms_norm(x, w):
            xf = x.astype(jnp.float32)
            var = jnp.mean(xf * xf, axis=-1, keepdims=True)
            return (w * (xf * jax.lax.rsqrt(var + EPS))).astype(x.dtype)

        def expert_mask(tt):
            vm = jnp.zeros(tt.shape, dtype=bool)
            vm = vm.at[:, :-1].set((tt[:, :-1] == 1) & (tt[:, 1:] == 1))
            return vm

        def rotate_half(x):
            d = x.shape[-1] // 2
            return jnp.concatenate([-x[..., d:], x[..., :d]], axis=-1)

        def apply_rotary(q, k, position_ids, seq_len):
            inv = 1.0 / 10000.0 ** (jnp.arange(0, HD, 2, dtype=jnp.float32) / HD)
            t = jnp.arange(seq_len, dtype=jnp.float32)
            freqs = jnp.outer(t, inv)
            emb = jnp.concatenate([freqs, freqs], axis=-1)
            cos = jnp.cos(emb)[position_ids][:, None].astype(q.dtype)
            sin = jnp.sin(emb)[position_ids][:, None].astype(q.dtype)
            return (q * cos + rotate_half(q) * sin, k * cos + rotate_half(k) * sin)

        def sdpa(q, k, v, causal):
            scale = 1.0 / np.sqrt(q.shape[-1])
            scores = jnp.einsum('bhqd,bhkd->bhqk', q * scale, k)
            if causal:
                mask = jnp.tril(jnp.ones((q.shape[-2], k.shape[-2]), dtype=bool))
                scores = jnp.where(mask, scores, jnp.finfo(jnp.float32).min)
            p = jax.nn.softmax(scores.astype(jnp.float32), axis=-1).astype(q.dtype)
            return jnp.einsum('bhqk,bhkd->bhqd', p, v)

        def heads(x, nh, hd):
            b, l, _ = x.shape
            return x.reshape(b, l, nh, hd).transpose(0, 2, 1, 3)
        key = jax.random.key(seed)
        ks = jax.random.split(key, 20)
        s = 0.02
        f32 = jnp.float32
        return {'hidden_states': jax.random.normal(ks[0], (B, L, H), f32), 'encoder_outputs': jax.random.normal(ks[1], (B, LE, CH), f32), 'token_type_ids': jax.random.randint(ks[2], (B, L), 0, 2, jnp.int32), 'position_ids': jnp.arange(L, dtype=jnp.int32)[None, :], 'ln_in_w': jnp.ones((H,), f32), 'ln_post_attn_w': jnp.ones((H,), f32), 'ln_post_cross_w': jnp.ones((H,), f32), 'v_qkv': jax.random.normal(ks[3], (H, 3 * H), f32) * s, 'l_qkv': jax.random.normal(ks[4], (H, 3 * H), f32) * s, 'v_dense': jax.random.normal(ks[5], (H, H), f32) * s, 'l_dense': jax.random.normal(ks[6], (H, H), f32) * s, 'cq_w': jax.random.normal(ks[7], (H, CC), f32) * s, 'ckv_w': jax.random.normal(ks[8], (CH, 2 * CC), f32) * s, 'cdense_w': jax.random.normal(ks[9], (CC, H), f32) * s, 'v_gate': jax.random.normal(ks[10], (H, I), f32) * s, 'v_up': jax.random.normal(ks[11], (H, I), f32) * s, 'v_down': jax.random.normal(ks[12], (I, H), f32) * s, 'l_gate': jax.random.normal(ks[13], (H, I), f32) * s, 'l_up': jax.random.normal(ks[14], (H, I), f32) * s, 'l_down': jax.random.normal(ks[15], (I, H), f32) * s}
    _L0_xattn_all = _L0_xattn_setup()
    _L0_xattn_in = {k: v for k, v in _L0_xattn_all.items() if k in ('ln_in_w', 'ln_post_attn_w', 'ln_post_cross_w', 'v_qkv', 'l_qkv', 'v_dense', 'l_dense', 'cq_w', 'ckv_w', 'cdense_w', 'v_gate', 'v_up', 'v_down', 'l_gate', 'l_up', 'l_down')}
    del _L0_xattn_all

    def _L1_xattn_setup():
        import jax, jax.numpy as jnp
        import numpy as np
        DIM = 256
        DIM_MEDIA = 128
        HEADS = 16
        DIM_HEAD = 64
        INNER = HEADS * DIM_HEAD
        FF_INNER = 4 * DIM
        B, N_TOK, N_LAT = (4, 256, 64)
        EPS = 1e-05

        def layernorm(x, g, b):
            mu = jnp.mean(x, axis=-1, keepdims=True)
            var = jnp.var(x, axis=-1, keepdims=True)
            return (x - mu) * jax.lax.rsqrt(var + EPS) * g + b
        key = jax.random.key(seed)
        ks = jax.random.split(key, 12)
        x = jax.random.normal(ks[0], (B, N_TOK, DIM), dtype=jnp.float32)
        media = jax.random.normal(ks[1], (B, N_LAT, DIM_MEDIA), dtype=jnp.float32)
        media_mask = jax.random.randint(ks[2], (B, N_LAT), 0, 2).astype(bool)
        media_mask = media_mask.at[:, 0].set(True)
        s = lambda d: 1.0 / np.sqrt(d)
        Wq = jax.random.normal(ks[3], (DIM, INNER), dtype=jnp.float32) * s(DIM)
        Wkv = jax.random.normal(ks[4], (DIM_MEDIA, 2 * INNER), dtype=jnp.float32) * s(DIM_MEDIA)
        Wo = jax.random.normal(ks[5], (INNER, DIM), dtype=jnp.float32) * s(INNER)
        W1 = jax.random.normal(ks[6], (DIM, FF_INNER), dtype=jnp.float32) * s(DIM)
        W2 = jax.random.normal(ks[7], (FF_INNER, DIM), dtype=jnp.float32) * s(FF_INNER)
        return {'x': x, 'media': media, 'media_mask': media_mask, 'ln_q_g': jnp.ones((DIM,), jnp.float32), 'ln_q_b': jnp.zeros((DIM,), jnp.float32), 'Wq': Wq, 'Wkv': Wkv, 'Wo': Wo, 'attn_gate': jax.random.normal(ks[8], (1,), jnp.float32) * 0.5, 'ln_ff_g': jnp.ones((DIM,), jnp.float32), 'ln_ff_b': jnp.zeros((DIM,), jnp.float32), 'W1': W1, 'W2': W2, 'ff_gate': jax.random.normal(ks[9], (1,), jnp.float32) * 0.5}
    _L1_xattn_all = _L1_xattn_setup()
    _L1_xattn_in = {k: v for k, v in _L1_xattn_all.items() if k in ('ln_q_g', 'ln_q_b', 'Wq', 'Wkv', 'Wo', 'attn_gate', 'ln_ff_g', 'ln_ff_b', 'W1', 'W2', 'ff_gate')}
    del _L1_xattn_all

    def _L2_xattn_setup():
        import jax, jax.numpy as jnp
        import numpy as np
        EPS = 1e-06

        def _rmsnorm(x, w):
            var = jnp.mean(jnp.square(x), axis=-1, keepdims=True)
            return x * jax.lax.rsqrt(var + EPS) * w
        key = jax.random.key(seed)
        ks = jax.random.split(key, 6)
        B, N, M = (4, 512, 256)
        d_model, memory_dim = (256, 128)
        hidden_states = jax.random.normal(ks[0], (B, N, d_model), dtype=jnp.float32)
        memory = jax.random.normal(ks[1], (B, M, memory_dim), dtype=jnp.float32)
        W_mem = jax.random.normal(ks[2], (d_model, memory_dim), dtype=jnp.float32) / np.sqrt(memory_dim)
        W_gate = jax.random.normal(ks[3], (d_model, 2 * d_model), dtype=jnp.float32) / np.sqrt(2 * d_model)
        b_gate = jax.random.normal(ks[4], (d_model,), dtype=jnp.float32) * 0.01
        norm_w = jnp.ones((d_model,), dtype=jnp.float32)
        return {'hidden_states': hidden_states, 'memory': memory, 'W_mem': W_mem, 'W_gate': W_gate, 'b_gate': b_gate, 'norm_w': norm_w}
    _L2_xattn_all = _L2_xattn_setup()
    _L2_xattn_in = {k: v for k, v in _L2_xattn_all.items() if k in ('W_mem', 'W_gate', 'b_gate', 'norm_w')}
    del _L2_xattn_all

    def _L3_xattn_setup():
        import jax, jax.numpy as jnp
        import numpy as np
        EPS = 1e-06

        def _rmsnorm(x, w):
            var = jnp.mean(jnp.square(x), axis=-1, keepdims=True)
            return x * jax.lax.rsqrt(var + EPS) * w
        key = jax.random.key(seed)
        ks = jax.random.split(key, 6)
        B, N, M = (4, 512, 256)
        d_model, memory_dim = (256, 128)
        hidden_states = jax.random.normal(ks[0], (B, N, d_model), dtype=jnp.float32)
        memory = jax.random.normal(ks[1], (B, M, memory_dim), dtype=jnp.float32)
        W_mem = jax.random.normal(ks[2], (d_model, memory_dim), dtype=jnp.float32) / np.sqrt(memory_dim)
        W_gate = jax.random.normal(ks[3], (d_model, 2 * d_model), dtype=jnp.float32) / np.sqrt(2 * d_model)
        b_gate = jax.random.normal(ks[4], (d_model,), dtype=jnp.float32) * 0.01
        norm_w = jnp.ones((d_model,), dtype=jnp.float32)
        return {'hidden_states': hidden_states, 'memory': memory, 'W_mem': W_mem, 'W_gate': W_gate, 'b_gate': b_gate, 'norm_w': norm_w}
    _L3_xattn_all = _L3_xattn_setup()
    _L3_xattn_in = {k: v for k, v in _L3_xattn_all.items() if k in ('W_mem', 'W_gate', 'b_gate', 'norm_w')}
    del _L3_xattn_all
    return {'x': x, 'ctx_1024': ctx_1024, 'pos_1xS': pos_1xS, 'mask_BxS_ik0': mask_BxS_ik0, 'mask_BxS2_bk0': mask_BxS2_bk0, 'L0_xattn_ln_in_w': _L0_xattn_in['ln_in_w'], 'L0_xattn_ln_post_attn_w': _L0_xattn_in['ln_post_attn_w'], 'L0_xattn_ln_post_cross_w': _L0_xattn_in['ln_post_cross_w'], 'L0_xattn_v_qkv': _L0_xattn_in['v_qkv'], 'L0_xattn_l_qkv': _L0_xattn_in['l_qkv'], 'L0_xattn_v_dense': _L0_xattn_in['v_dense'], 'L0_xattn_l_dense': _L0_xattn_in['l_dense'], 'L0_xattn_cq_w': _L0_xattn_in['cq_w'], 'L0_xattn_ckv_w': _L0_xattn_in['ckv_w'], 'L0_xattn_cdense_w': _L0_xattn_in['cdense_w'], 'L0_xattn_v_gate': _L0_xattn_in['v_gate'], 'L0_xattn_v_up': _L0_xattn_in['v_up'], 'L0_xattn_v_down': _L0_xattn_in['v_down'], 'L0_xattn_l_gate': _L0_xattn_in['l_gate'], 'L0_xattn_l_up': _L0_xattn_in['l_up'], 'L0_xattn_l_down': _L0_xattn_in['l_down'], 'L1_xattn_ln_q_g': _L1_xattn_in['ln_q_g'], 'L1_xattn_ln_q_b': _L1_xattn_in['ln_q_b'], 'L1_xattn_Wq': _L1_xattn_in['Wq'], 'L1_xattn_Wkv': _L1_xattn_in['Wkv'], 'L1_xattn_Wo': _L1_xattn_in['Wo'], 'L1_xattn_attn_gate': _L1_xattn_in['attn_gate'], 'L1_xattn_ln_ff_g': _L1_xattn_in['ln_ff_g'], 'L1_xattn_ln_ff_b': _L1_xattn_in['ln_ff_b'], 'L1_xattn_W1': _L1_xattn_in['W1'], 'L1_xattn_W2': _L1_xattn_in['W2'], 'L1_xattn_ff_gate': _L1_xattn_in['ff_gate'], 'L2_xattn_W_mem': _L2_xattn_in['W_mem'], 'L2_xattn_W_gate': _L2_xattn_in['W_gate'], 'L2_xattn_b_gate': _L2_xattn_in['b_gate'], 'L2_xattn_norm_w': _L2_xattn_in['norm_w'], 'L3_xattn_W_mem': _L3_xattn_in['W_mem'], 'L3_xattn_W_gate': _L3_xattn_in['W_gate'], 'L3_xattn_b_gate': _L3_xattn_in['b_gate'], 'L3_xattn_norm_w': _L3_xattn_in['norm_w']}

def reference(x, ctx_1024, pos_1xS, mask_BxS_ik0, mask_BxS2_bk0, L0_xattn_ln_in_w, L0_xattn_ln_post_attn_w, L0_xattn_ln_post_cross_w, L0_xattn_v_qkv, L0_xattn_l_qkv, L0_xattn_v_dense, L0_xattn_l_dense, L0_xattn_cq_w, L0_xattn_ckv_w, L0_xattn_cdense_w, L0_xattn_v_gate, L0_xattn_v_up, L0_xattn_v_down, L0_xattn_l_gate, L0_xattn_l_up, L0_xattn_l_down, L1_xattn_ln_q_g, L1_xattn_ln_q_b, L1_xattn_Wq, L1_xattn_Wkv, L1_xattn_Wo, L1_xattn_attn_gate, L1_xattn_ln_ff_g, L1_xattn_ln_ff_b, L1_xattn_W1, L1_xattn_W2, L1_xattn_ff_gate, L2_xattn_W_mem, L2_xattn_W_gate, L2_xattn_b_gate, L2_xattn_norm_w, L3_xattn_W_mem, L3_xattn_W_gate, L3_xattn_b_gate, L3_xattn_norm_w):
    import jax
    import jax.numpy as jnp

    def _L0_xattn_ref(hidden_states, encoder_outputs, token_type_ids, position_ids, ln_in_w, ln_post_attn_w, ln_post_cross_w, v_qkv, l_qkv, v_dense, l_dense, cq_w, ckv_w, cdense_w, v_gate, v_up, v_down, l_gate, l_up, l_down):
        import jax, jax.numpy as jnp
        import numpy as np
        H = 256
        NH = 16
        HD = H // NH
        CH = 128
        CC = 128
        CHD = CC // NH
        I = 688
        B = 2
        L = 256
        LE = 128
        EPS = 1e-06

        def rms_norm(x, w):
            xf = x.astype(jnp.float32)
            var = jnp.mean(xf * xf, axis=-1, keepdims=True)
            return (w * (xf * jax.lax.rsqrt(var + EPS))).astype(x.dtype)

        def expert_mask(tt):
            vm = jnp.zeros(tt.shape, dtype=bool)
            vm = vm.at[:, :-1].set((tt[:, :-1] == 1) & (tt[:, 1:] == 1))
            return vm

        def rotate_half(x):
            d = x.shape[-1] // 2
            return jnp.concatenate([-x[..., d:], x[..., :d]], axis=-1)

        def apply_rotary(q, k, position_ids, seq_len):
            inv = 1.0 / 10000.0 ** (jnp.arange(0, HD, 2, dtype=jnp.float32) / HD)
            t = jnp.arange(seq_len, dtype=jnp.float32)
            freqs = jnp.outer(t, inv)
            emb = jnp.concatenate([freqs, freqs], axis=-1)
            cos = jnp.cos(emb)[position_ids][:, None].astype(q.dtype)
            sin = jnp.sin(emb)[position_ids][:, None].astype(q.dtype)
            return (q * cos + rotate_half(q) * sin, k * cos + rotate_half(k) * sin)

        def sdpa(q, k, v, causal):
            scale = 1.0 / np.sqrt(q.shape[-1])
            scores = jnp.einsum('bhqd,bhkd->bhqk', q * scale, k)
            if causal:
                mask = jnp.tril(jnp.ones((q.shape[-2], k.shape[-2]), dtype=bool))
                scores = jnp.where(mask, scores, jnp.finfo(jnp.float32).min)
            p = jax.nn.softmax(scores.astype(jnp.float32), axis=-1).astype(q.dtype)
            return jnp.einsum('bhqk,bhkd->bhqd', p, v)

        def heads(x, nh, hd):
            b, l, _ = x.shape
            return x.reshape(b, l, nh, hd).transpose(0, 2, 1, 3)
        b, l, _ = hidden_states.shape
        vm = expert_mask(token_type_ids)[..., None]
        residual = hidden_states
        x = rms_norm(hidden_states, ln_in_w)
        mixed = jnp.where(vm, x @ v_qkv, x @ l_qkv)
        q, k, v = jnp.split(mixed, 3, axis=-1)
        q, k, v = (heads(q, NH, HD), heads(k, NH, HD), heads(v, NH, HD))
        q, k = apply_rotary(q, k, position_ids, l)
        ctx = sdpa(q, k, v, causal=True)
        ctx = ctx.transpose(0, 2, 1, 3).reshape(b, l, H)
        attn_out = jnp.where(vm, ctx @ v_dense, ctx @ l_dense)
        hidden_states = residual + attn_out
        ci = rms_norm(hidden_states, ln_post_cross_w)
        cq = heads(ci @ cq_w, NH, CHD)
        ckv = encoder_outputs @ ckv_w
        ck, cv = jnp.split(ckv, 2, axis=-1)
        ck, cv = (heads(ck, NH, CHD), heads(cv, NH, CHD))
        cctx = sdpa(cq, ck, cv, causal=False)
        cctx = cctx.transpose(0, 2, 1, 3).reshape(b, l, CC)
        hidden_states = hidden_states + cctx @ cdense_w
        mi = rms_norm(hidden_states, ln_post_attn_w)
        v_out = jax.nn.silu(mi @ v_gate) * (mi @ v_up) @ v_down
        l_out = jax.nn.silu(mi @ l_gate) * (mi @ l_up) @ l_down
        hidden_states = hidden_states + jnp.where(vm, v_out, l_out)
        return hidden_states

    def _L1_xattn_ref(x, media, media_mask, ln_q_g, ln_q_b, Wq, Wkv, Wo, attn_gate, ln_ff_g, ln_ff_b, W1, W2, ff_gate):
        import jax, jax.numpy as jnp
        import numpy as np
        DIM = 256
        DIM_MEDIA = 128
        HEADS = 16
        DIM_HEAD = 64
        INNER = HEADS * DIM_HEAD
        FF_INNER = 4 * DIM
        B, N_TOK, N_LAT = (4, 256, 64)
        EPS = 1e-05

        def layernorm(x, g, b):
            mu = jnp.mean(x, axis=-1, keepdims=True)
            var = jnp.var(x, axis=-1, keepdims=True)
            return (x - mu) * jax.lax.rsqrt(var + EPS) * g + b
        scale = DIM_HEAD ** (-0.5)
        qn = layernorm(x, ln_q_g, ln_q_b)
        q = qn @ Wq * scale
        kv = media @ Wkv
        k, v = jnp.split(kv, 2, axis=-1)
        split_heads = lambda t: t.reshape(t.shape[0], t.shape[1], HEADS, DIM_HEAD).transpose(0, 2, 1, 3)
        q, k, v = (split_heads(q), split_heads(k), split_heads(v))
        sim = jnp.einsum('bhid,bhjd->bhij', q, k)
        neg_inf = jnp.finfo(sim.dtype).min
        sim = jnp.where(media_mask[:, None, None, :], sim, neg_inf)
        attn = jax.nn.softmax(sim, axis=-1)
        out = jnp.einsum('bhij,bhjd->bhid', attn, v)
        out = out.transpose(0, 2, 1, 3).reshape(x.shape[0], x.shape[1], INNER)
        attn_out = out @ Wo
        x = x + jnp.tanh(attn_gate) * attn_out
        h = layernorm(x, ln_ff_g, ln_ff_b)
        h = jax.nn.gelu(h @ W1, approximate=False) @ W2
        x = x + jnp.tanh(ff_gate) * h
        return x

    def _L2_xattn_ref(hidden_states, memory, W_mem, W_gate, b_gate, norm_w):
        import jax, jax.numpy as jnp
        import numpy as np
        EPS = 1e-06

        def _rmsnorm(x, w):
            var = jnp.mean(jnp.square(x), axis=-1, keepdims=True)
            return x * jax.lax.rsqrt(var + EPS) * w
        D = hidden_states.shape[-1]
        memory_proj = jnp.einsum('bme,de->bmd', memory, W_mem)
        scores = jnp.einsum('bnd,bmd->bnm', hidden_states, memory_proj) / jnp.sqrt(jnp.float32(D))
        attn = jax.nn.softmax(scores, axis=-1)
        memory_context = jnp.einsum('bnm,bmd->bnd', attn, memory_proj)
        gate_input = jnp.concatenate([hidden_states, memory_context], axis=-1)
        gate = jax.nn.sigmoid(jnp.einsum('bnf,df->bnd', gate_input, W_gate) + b_gate)
        fused = hidden_states + gate * memory_context
        return _rmsnorm(fused, norm_w)

    def _L3_xattn_ref(hidden_states, memory, W_mem, W_gate, b_gate, norm_w):
        import jax, jax.numpy as jnp
        import numpy as np
        EPS = 1e-06

        def _rmsnorm(x, w):
            var = jnp.mean(jnp.square(x), axis=-1, keepdims=True)
            return x * jax.lax.rsqrt(var + EPS) * w
        D = hidden_states.shape[-1]
        memory_proj = jnp.einsum('bme,de->bmd', memory, W_mem)
        scores = jnp.einsum('bnd,bmd->bnm', hidden_states, memory_proj) / jnp.sqrt(jnp.float32(D))
        attn = jax.nn.softmax(scores, axis=-1)
        memory_context = jnp.einsum('bnm,bmd->bnd', attn, memory_proj)
        gate_input = jnp.concatenate([hidden_states, memory_context], axis=-1)
        gate = jax.nn.sigmoid(jnp.einsum('bnf,df->bnd', gate_input, W_gate) + b_gate)
        fused = hidden_states + gate * memory_context
        return _rmsnorm(fused, norm_w)
    x = _L0_xattn_ref(x, ctx_1024, mask_BxS_ik0, pos_1xS, L0_xattn_ln_in_w, L0_xattn_ln_post_attn_w, L0_xattn_ln_post_cross_w, L0_xattn_v_qkv, L0_xattn_l_qkv, L0_xattn_v_dense, L0_xattn_l_dense, L0_xattn_cq_w, L0_xattn_ckv_w, L0_xattn_cdense_w, L0_xattn_v_gate, L0_xattn_v_up, L0_xattn_v_down, L0_xattn_l_gate, L0_xattn_l_up, L0_xattn_l_down)
    x = _L1_xattn_ref(x, ctx_1024, mask_BxS2_bk0, L1_xattn_ln_q_g, L1_xattn_ln_q_b, L1_xattn_Wq, L1_xattn_Wkv, L1_xattn_Wo, L1_xattn_attn_gate, L1_xattn_ln_ff_g, L1_xattn_ln_ff_b, L1_xattn_W1, L1_xattn_W2, L1_xattn_ff_gate)
    x = _L2_xattn_ref(x, ctx_1024, L2_xattn_W_mem, L2_xattn_W_gate, L2_xattn_b_gate, L2_xattn_norm_w)
    x = _L3_xattn_ref(x, ctx_1024, L3_xattn_W_mem, L3_xattn_W_gate, L3_xattn_b_gate, L3_xattn_norm_w)
    return x

_drawn_inputs = setup_inputs


def setup_inputs(seed=0):
    import zlib

    import numpy as np

    out = dict(_drawn_inputs(seed))
    spreads = {'L0_xattn_ln_in_w': (1.0, 0.6),
     'L0_xattn_ln_post_attn_w': (1.0, 0.6),
     'L0_xattn_ln_post_cross_w': (1.0, 0.6),
     'L1_xattn_ln_q_g': (1.0, 0.6),
     'L1_xattn_ln_q_b': (0.0, 0.8),
     'L1_xattn_ln_ff_g': (1.0, 0.6),
     'L1_xattn_ln_ff_b': (0.0, 0.8),
     'L2_xattn_norm_w': (1.0, 0.2),
     'L3_xattn_norm_w': (1.0, 0.2)}
    factors = {'L0_xattn_v_qkv': 8.0,
     'L0_xattn_l_qkv': 3.782,
     'L0_xattn_v_dense': 8.0,
     'L0_xattn_l_dense': 3.913,
     'L0_xattn_cq_w': 64.0,
     'L0_xattn_v_gate': 5.712,
     'L0_xattn_v_up': 5.621,
     'L0_xattn_v_down': 5.602,
     'L1_xattn_W1': 2.815,
     'L2_xattn_b_gate': 64.0,
     'L3_xattn_b_gate': 47.534,
     'L0_xattn_ckv_w': 3.444,
     'L0_xattn_cdense_w': 3.407}
    for name, (base, spread) in spreads.items():
        noise = np.random.default_rng([zlib.crc32(name.encode()), seed]).standard_normal(out[name].shape)
        drawn = base * np.exp(spread * noise) if base else spread * noise
        out[name] = jnp.asarray(drawn.astype(out[name].dtype))
    for name, factor in factors.items():
        out[name] = (out[name] * factor).astype(out[name].dtype)
    return out
```

```python
import numpy as np

import concourse.bass as bass
from concourse import mybir
from contextlib import ExitStack

F32, F32R, BF16 = mybir.dt.float32, mybir.dt.float32r, mybir.dt.bfloat16
I32, U8 = mybir.dt.int32, mybir.dt.uint8
ACT, ALU, AX = mybir.ActivationFunctionType, mybir.AluOpType, mybir.AxisListType

P = 128
B, S, D = 8, 256, 256
DC = D // P
C = 128
NK = 1601
KT = -(-NK // P)
KLAST = NK - (KT - 1) * P
NKP = NK + NK % 2
MW = -(-NKP // 4)
KCH = [(k, min(512, NKP - k)) for k in range(0, NKP, 512)]
NH = 16
SHD, CHD, XHD = D // NH, C // NH, 64
FF0, FF1 = 688, 1024
NG = NH // 4
NP = NH // 2
BIG = 1e30
EXP_LN = "natural_log_exp_and_others"


class Phase:

    def __init__(self, nc, name):
        self.nc, self.name, self.stack, self.sems = nc, name, ExitStack(), []

    def __enter__(self):
        return self

    def __exit__(self, *error):
        self.stack.close()
        if error[0] is None:
            self.nc.clear_and_free_semaphores(self.sems)
            self.nc.all_engine_barrier()

    def sem(self, name):
        self.sems.append(self.nc.alloc_semaphore(f"{self.name}_{name}"))
        return self.sems[-1]

    def sems2(self, name):
        return [self.sem(f"{name}{k}") for k in range(2)]

    def sb(self, name, shape, dt=F32):
        return self.stack.enter_context(self.nc.sbuf_tensor(f"{self.name}_{name}", shape, dt))

    def banks(self, name, n, width=512):
        return [self.stack.enter_context(self.nc.psum_tensor(f"{self.name}_{name}{k}", [P, width], F32))
                for k in range(n)]


def batches(eng, ahead, main):
    ahead(0, 0)
    with eng.Fori(0, B // 2 - 1) as i:
        ahead(i * 2 + 1, 1)
        main(i * 2, 0)
        ahead(i * 2 + 2, 0)
        main(i * 2 + 1, 1)
    ahead(B - 1, 1)
    main(B - 2, 0)
    main(B - 1, 1)


def first(b):
    return isinstance(b, int) and b == 0


def half(b, p):
    return b // 2 if isinstance(b, int) else (b - p) // 2


class Chain:

    def __init__(self, eng, sem, before):
        self.eng, self.sem, self.n = eng, sem, before

    def link(self, instruction):
        self.n = self.n + 1
        instruction.then_inc(self.sem, 1)
        self.eng.wait_ge(self.sem, self.n)


def load_constants(nc, src, c):
    with Phase(nc, "setup") as ph:
        names = list(c["loads"])
        loaded, built, pe_done = ph.sem("loaded"), ph.sem("built"), ph.sem("pe_done")
        tok = ph.sb("tok", [P, B, S], I32)
        is_one = ph.sb("is_one", [P, B, S])
        pos_i = ph.sb("pos_i", [P, S], I32)
        pos = ph.sb("pos", [P, 3, S])
        onehot = ph.sb("onehot", [P, 2, S])
        iota = ph.sb("iota", [P, 2])
        tables = ph.sb("tables", [P, 2, 2, P])
        stage = ph.sb("stage", [P, 2, S])
        causal = ph.sb("causal", [P, 2, S])
        sel = ph.sb("sel", [P, 4, P])
        rope_ps = ph.banks("rope", 2)
        with nc.Block() as block:
            n_loads = len(names) + 6

            @block.sync
            def _(sp):
                for name in names:
                    sp.dma_start(c[name][:], c["loads"][name]).then_inc(loaded, 16)
                sp.dma_start(tok[:], src["tok_mask"].partition_broadcast(P)).then_inc(loaded, 16)
                sp.dma_start(pos_i[:], src["pos"][0].partition_broadcast(P)).then_inc(loaded, 16)
                sp.dma_start(iota[:], src["c_iota"]).then_inc(loaded, 16)
                sp.dma_start(tables[:], src["c_rope"]).then_inc(loaded, 16)
                sp.dma_start(causal[:], src["c_causal"]).then_inc(loaded, 16)
                sp.dma_start(sel[:], src["c_sel"]).then_inc(loaded, 16)

            @block.vector
            def _(dve):
                dve.wait_ge(loaded, 16 * n_loads)
                ch = Chain(dve, built, 0)
                ch.link(nc.vector.tensor_scalar(is_one[:], tok[:], 1.0, None, ALU.is_equal))
                ch.link(nc.vector.tensor_tensor(c["vm"][:, :, 0:S - 1], is_one[:, :, 0:S - 1],
                                                is_one[:, :, 1:S], ALU.mult))
                ch.link(nc.vector.memset(c["vm"][:, :, S - 1:S], 0.0))
                ch.link(nc.vector.tensor_copy(pos[:, 0, :], pos_i[:]))
                ch.link(nc.vector.tensor_scalar(pos[:, 1, :], pos[:, 0, :], 0.0, float(S), ALU.is_lt, ALU.mult))
                ch.link(nc.vector.tensor_tensor(pos[:, 2, :], pos[:, 0, :], pos[:, 1, :], ALU.add))
                ch.link(nc.vector.tensor_scalar(pos[:, 0, :], pos[:, 2, :], 0.0, float(S - 1), ALU.max, ALU.min))
                for k in range(2):
                    ch.link(nc.vector.tensor_scalar(onehot[:, k, :], pos[:, 0, :], iota[:, k:k + 1], None,
                                                    ALU.is_equal))
                dve.wait_ge(pe_done, 1)
                ch.link(nc.vector.tensor_copy(c["cos"][:], rope_ps[0][:, 0:S]))
                ch.link(nc.vector.tensor_copy(c["sin"][:], rope_ps[1][:, 0:S]))
                ch.link(nc.vector.tensor_copy(c["causal"][:], causal[:]))
                ch.link(nc.vector.tensor_copy(c["causal_tb"][:], c["causal_t"][:]))
                ch.link(nc.vector.tensor_copy(c["ident_b"][:], c["ident"][:]))
                ch.link(nc.vector.memset(c["eps6"][:], 1e-6))
                ch.link(nc.vector.memset(c["eps5"][:], 1e-5))
                ch.link(nc.vector.tensor_copy(c["ones_r"][:], c["ones"][:]))
                ch.link(nc.vector.tensor_copy(c["sel_r"][:], sel[:]))
                ch.link(nc.vector.tensor_scalar(c["mean"][:], c["ones"][:], 1.0 / D, None, ALU.mult))

            @block.scalar
            def _(act):
                act.wait_ge(loaded, 16 * n_loads)
                for k, name in enumerate(("attn_gate", "ff_gate")):
                    nc.scalar.activation(c["tanh_gate"][:, k:k + 1], c[name][:], ACT.Tanh)

            @block.tensor
            def _(pe):
                pe.wait_ge(built, 9)
                for k in range(2):
                    for t in range(2):
                        last = nc.tensor.matmul(rope_ps[k][:, 0:S], tables[:, k, t, :], onehot[:, t, :],
                                                start=(t == 0), stop=(t == 1))
                last.then_inc(pe_done, 1)


def mask_context(nc, src, c, masked_d):
    with Phase(nc, "maskctx") as ph:
        in_ready, out_stored = ph.sems2("in_ready"), ph.sems2("out_stored")
        in_free, out_free, out_ready = ph.sem("in_free"), ph.sem("out_free"), ph.sem("out_ready")
        steps, mt_ready = ph.sem("steps"), ph.sem("mt_ready")
        ct = ph.sb("ct", [P, 2, NKP])
        mk_words = ph.sb("mk", [P, 2, MW], I32)
        mk = mk_words.bitcast(U8)
        valid = ph.sb("valid", [P, NKP])
        invalid = ph.sb("invalid", [P, NKP])
        kept = ph.sb("kept", [P, NKP])
        out = ph.sb("out", [P, 2, NKP])
        stat = ph.sb("stat", [P, 6])
        mt_words = ph.sb("mt", [P, B * KT // 4], I32)
        mt = mt_words.bitcast(U8).rearrange("p (b t) -> p b t", b=B)
        with nc.Block() as block:
            @block.sync
            def _(sp):
                sp.dma_start(mt_words[:], src["key_mask_t"]).then_inc(mt_ready, 16)
                with sp.Fori(0, B // 2) as i:
                    for p in range(2):
                        sp.wait_ge(in_free, i * 2 + p + 1)
                        sp.dma_start(ct[:, p, :], src["ctx_t"][i * 2 + p]).then_inc(in_ready[p], 16)
                        sp.dma_start(mk_words[:, p, :], src["key_mask"][i * 2 + p].partition_broadcast(P)
                                     ).then_inc(in_ready[p], 16)

            @block.gpsimd
            def _(pool):
                pool.sem_inc(out_free, 2)
                with pool.Fori(0, B // 2) as i:
                    for p in range(2):
                        pool.wait_ge(out_ready, i * 2 + p + 1)
                        pool.dma_start(masked_d[i * 2 + p], out[:, p, :]).then_inc(out_stored[p], 16)
                        pool.wait_ge(out_stored[p], i * 16 + 16)
                        pool.sem_inc(out_free, 1)

            @block.vector
            def _(dve):
                dve.sem_inc(in_free, 2)
                dve.wait_ge(mt_ready, 16)
                per = 8
                with dve.Fori(0, B // 2) as i:
                    for p in range(2):
                        b = i * 2 + p
                        ch = Chain(dve, steps, b * per)
                        dve.wait_ge(in_ready[p], i * 32 + 32)
                        ch.link(nc.vector.tensor_scalar(invalid[:], mk[:, p, 0:NKP], 0.0, None, ALU.is_equal))
                        ch.link(nc.vector.tensor_scalar(valid[:], invalid[:], -1.0, 1.0, ALU.mult, ALU.add))
                        ch.link(nc.vector.tensor_reduce(stat[:, 0:1], valid[:, 0:NK], AX.X, ALU.add))
                        ch.link(nc.vector.tensor_tensor(kept[:], ct[:, p, :], valid[:], ALU.mult))
                        dve.sem_inc(in_free, 1)
                        nc.vector.tensor_reduce(stat[:, 1:2], kept[:, 0:NK], AX.X, ALU.add)
                        ch.link(nc.vector.tensor_scalar(stat[:, 2:3], stat[:, 0:1], 1.0, None, ALU.max))
                        ch.link(nc.vector.reciprocal(stat[:, 3:4], stat[:, 2:3]))
                        nc.vector.tensor_scalar(stat[:, 4:5], stat[:, 0:1], 1.0, -BIG, ALU.min, ALU.mult)
                        ch.link(nc.vector.tensor_tensor(stat[:, 5:6], stat[:, 1:2], stat[:, 3:4], ALU.mult))
                        dve.wait_ge(out_free, b + 1)
                        nc.vector.scalar_tensor_tensor(out[:, p, :], invalid[:], stat[:, 5:6], kept[:],
                                                       ALU.mult, ALU.add).then_inc(out_ready, 1)
                        ch.link(nc.vector.tensor_scalar(c["key_bias"][:, b, :], mt[:, b, :], 0.0, stat[:, 4:5],
                                                        ALU.is_equal, ALU.mult))
def self_projections(nc, src, c, q_d, k_d, v_d):
    with Phase(nc, "selfproj") as ph:
        x = ph.sb("x", [P, 2, DC, S])
        sq = ph.sb("sq", [P, DC, S])
        ln = ph.sb("ln", [P, S])
        rs = ph.sb("rs", [P, 2, S])
        xn = ph.sb("xn", [P, DC, S])
        xe = ph.sb("xe", [P, 2, 2, DC, S])
        w = ph.sb("w", [P, 2, DC, 3 * D])
        raw = ph.sb("raw", [P, 2, S])
        by_cos = ph.sb("by_cos", [P, 2, S])
        by_sin = ph.sb("by_sin", [P, 2, S])
        qk = ph.sb("qk", [P, 2, 4, S])
        v = ph.sb("v", [P, 2, 2, NH, 32])
        var_ps, qk_ps, rot_ps, v_ps = (ph.banks(n, k) for n, k in (("var", 1), ("qk", 2), ("rot", 2), ("v", 2)))
        x_ready, q_stored, v_stored = ph.sems2("x_ready"), ph.sems2("q_stored"), ph.sems2("v_stored")
        w_ready, x_free, sq_ready, sq_free = (ph.sem(n) for n in ("w_ready", "x_free", "sq_ready", "sq_free"))
        var_ready, ln_ready, rs_ready = ph.sem("var_ready"), ph.sem("ln_ready"), ph.sem("rs_ready")
        xe_ready, steps = ph.sem("xe_ready"), ph.sem("steps")
        qk_ready, raw_ready, rot_ready, turned = (ph.sem(n) for n in ("qk_ready", "raw_ready", "rot_ready", "turned"))
        rot_used = ph.sem("rot_used")
        v_ready, v_copied, v_set, out_free = (ph.sem(n) for n in ("v_ready", "v_copied", "v_set", "out_free"))
        with nc.Block() as block:
            @block.sync
            def _(sp):
                for e, name in enumerate(("v_qkv", "l_qkv")):
                    sp.dma_start(w[:, e], src[name]).then_inc(w_ready, 16)
                with sp.Fori(0, B // 2) as i:
                    for p in range(2):
                        sp.wait_ge(x_free, i * 2 + p + 1)
                        sp.dma_start(x[:, p], src["x_t"][i * 2 + p]).then_inc(x_ready[p], 16)

            @block.gpsimd
            def _(pool):
                nc.gpsimd.memset(v[:], 0.0).then_inc(v_set, 1)
                pool.wait_ge(v_set, 1)
                nc.gpsimd.memset(v[:, :, :, :, SHD:SHD + 1], 1.0).then_inc(v_set, 1)
                pool.sem_inc(out_free, 2)
                with pool.Fori(0, B // 2) as i:
                    for p in range(2):
                        b = i * 2 + p
                        counted(pool, turned, b * 4 + 4)
                        pool.dma_start(q_d[b], qk[:, p, 0:2]).then_inc(q_stored[p], 16)
                        pool.dma_start(k_d[b], qk[:, p, 2:4]).then_inc(q_stored[p], 16)
                        counted(pool, v_copied, b * 2 + 2)
                        pool.dma_start(v_d[b], v[:, p]).then_inc(v_stored[p], 16)
                        pool.wait_ge(q_stored[p], i * 32 + 32)
                        pool.wait_ge(v_stored[p], i * 16 + 16)
                        pool.sem_inc(out_free, 1)

            @block.scalar
            def _(act):
                act.preload_act_table_set(EXP_LN)
                prime(act, raw_ready, v_copied)

                def ahead(b, p):
                    act.wait_ge(x_ready[p], half(b, p) * 16 + 16)
                    act.wait_ge(var_ready, b)
                    nc.scalar.activation(sq[:], x[:, p], ACT.Square).then_inc(sq_ready, 1)
                    act.wait_ge(var_ready, b + 1)
                    nc.scalar.activation(ln[:], var_ps[0][:, 0:S], ACT.Ln, bias=c["eps6"][:, 0:1]).then_inc(ln_ready, 1)
                    act.wait_ge(ln_ready, b + 1)
                    nc.scalar.activation(rs[:, p], ln[:], ACT.Exp, scale=-0.5).then_inc(rs_ready, 1)

                def main(b, p):
                    for m in range(4):
                        act.wait_ge(qk_ready, b * 4 + m + 1)
                        counted(act, turned, b * 4 + m - 1)
                        nc.scalar.activation(raw[:, m % 2], qk_ps[m % 2][:, 0:S], ACT.Copy).then_inc(raw_ready, 1)
                    act.wait_ge(out_free, b + 1)
                    act.wait_ge(v_set, 2)
                    for t in range(2):
                        counted(act, v_ready, b * 2 + t + 1)
                        nc.scalar.activation(v[:, p, t, :, 0:SHD],
                                             v_ps[t][:, 0:D].rearrange("p (h d) -> p h d", h=NH),
                                             ACT.Copy).then_inc(v_copied, 1)
                batches(act, ahead, main)

            @block.vector
            def _(dve):
                dve.sem_inc(x_free, 2)
                prime(dve, turned, rot_used)

                def ahead(b, p):
                    ch = Chain(dve, steps, b * 4)
                    dve.wait_ge(rs_ready, b + 1)
                    for k in range(DC):
                        ins = nc.vector.scalar_tensor_tensor(xn[:, k], x[:, p, k], c["ln_in_w"][:, k:k + 1], rs[:, p],
                                                             ALU.mult, ALU.mult)
                        ch.link(ins)
                    dve.sem_inc(x_free, 1)
                    counted(dve, v_ready, b * 2 - 2)
                    for k in range(DC):
                        ch.link(nc.vector.tensor_tensor(xe[:, p, 0, k], xn[:, k], c["vm"][:, b, :], ALU.mult))
                    nc.vector.tensor_tensor(xe[:, p, 1], xn[:], xe[:, p, 0], ALU.subtract).then_inc(xe_ready, 1)
                    dve.wait_ge(xe_ready, b + 1)

                def main(b, p):
                    dve.wait_ge(out_free, b + 1)
                    for m in range(4):
                        ch = m % 2
                        counted(dve, raw_ready, b * 4 + m + 1)
                        nc.vector.tensor_tensor(by_cos[:, ch], raw[:, ch], c["cos"][:], ALU.mult)
                        dve.wait_ge(rot_ready, b * 4 + m + 1)
                        nc.vector.tensor_tensor(by_sin[:, ch], rot_ps[ch][:, 0:S], c["sin"][:], ALU.mult).then_inc(
                            rot_used, 1)
                        counted(dve, rot_used, b * 4 + m + 1)
                        nc.vector.tensor_tensor(qk[:, p, m], by_cos[:, ch], by_sin[:, ch], ALU.add).then_inc(turned, 1)
                batches(dve, ahead, main)

            @block.tensor
            def _(pe):
                prime(pe, v_ready)
                def ahead(b, p):
                    pe.wait_ge(sq_ready, b + 1)
                    if not first(b):
                        pe.wait_ge(ln_ready, b)
                    for k in range(DC):
                        last = nc.tensor.matmul(var_ps[0][:, 0:S], c["mean"][:], sq[:, k], start=(k == 0), stop=(k == DC - 1))
                    last.then_inc(var_ready, 1)

                def turn(b, m):
                    counted(pe, raw_ready, b * 4 + m + 1)
                    counted(pe, rot_used, b * 4 + m - 1)
                    nc.tensor.matmul(rot_ps[m % 2][:, 0:S], c["rot"][:], raw[:, m % 2], start=True, stop=True
                                     ).then_inc(rot_ready, 1)

                def main(b, p):
                    pe.wait_ge(w_ready, 32)
                    pe.wait_ge(xe_ready, b + 1)
                    for m in range(4):
                        counted(pe, raw_ready, b * 4 + m - 1)
                        for n in range(4):
                            e, k = divmod(n, 2)
                            last = nc.tensor.matmul(qk_ps[m % 2][:, 0:S], w[:, e, k, m * P:(m + 1) * P], xe[:, p, e, k],
                                                    start=(n == 0), stop=(n == 3))
                        last.then_inc(qk_ready, 1)
                        if m:
                            turn(b, m - 1)
                    for t in range(2):
                        counted(pe, v_copied, b * 2 + t - 1)
                        for n in range(4):
                            e, k = divmod(n, 2)
                            last = nc.tensor.matmul(v_ps[t][:, 0:D], xe[:, p, e, k, t * P:(t + 1) * P],
                                                    w[:, e, k, 2 * D:3 * D], start=(n == 0), stop=(n == 3))
                        last.then_inc(v_ready, 1)
                        if t == 0:
                            turn(b, 3)
                batches(pe, ahead, main)


PRIME = 4


def prime(eng, *sems):
    for s in sems:
        eng.sem_inc(s, PRIME)


def counted(eng, sem, n):
    if isinstance(n, int) and n <= 0:
        return
    eng.wait_ge(sem, n + PRIME)


def units(eng, per, ahead, step):
    ahead((0, 0, 0, 0))

    def batch(b, p, last=False):
        for g in range(per):
            if g + 1 < per:
                step((b, p, g, b * per + g), (b, p, g + 1, b * per + g + 1))
            elif not last:
                step((b, p, g, b * per + g), (b + 1, 1 - p, 0, b * per + per))
            else:
                step((b, p, g, b * per + g), None)

    with eng.Fori(0, B // 2 - 1) as i:
        batch(i * 2, 0)
        batch(i * 2 + 1, 1)
    batch(B - 2, 0)
    batch(B - 1, 1, last=True)


def self_attention(nc, c, q_d, k_d, v_d, out_d):
    with Phase(nc, "self") as ph:
        q, k = ph.sb("q", [P, 2, 2, S]), ph.sb("k", [P, 2, 2, S])
        k_r = ph.sb("k_r", [P, 2, 2, S], F32R)
        v = ph.sb("v", [P, 2, 2, NH, 32])
        qd = ph.sb("qd", [P, 2, 4, S])
        qd_r = ph.sb("qd_r", [P, 4, S], F32R)
        negmax = ph.sb("negmax", [P, 2, 4, 2])
        diag = ph.sb("diag", [P, 2, 4, S], F32R)
        p0, p1 = ph.sb("p0", [P, 2, 4, S]), ph.sb("p1", [P, 2, 4, P])
        av, rsum, out = ph.sb("av", [P, S]), ph.sb("rsum", [P, S]), ph.sb("out", [P, 2, S])
        max_ps, s0_ps, s1_ps, av_ps, sum_ps = (ph.banks(n, m) for n, m in (("max", 2), ("s0", 2), ("s1", 1), ("av", 1), ("sum", 1)))
        loaded, stored = ph.sems2("loaded"), ph.sems2("stored")
        kr_ready, qd_ready, qdr_ready, max_ready, maxed, diag_ready = (
            ph.sem(n) for n in ("kr_ready", "qd_ready", "qdr_ready", "max_ready", "maxed", "diag_ready"))
        s0_ready, s1_ready, p0_ready, p1_ready = (ph.sem(n) for n in ("s0_ready", "s1_ready", "p0_ready", "p1_ready"))
        av_ready, av_copied, sum_ready, rsum_ready, out_ready = (
            ph.sem(n) for n in ("av_ready", "av_copied", "sum_ready", "rsum_ready", "out_ready"))
        with nc.Block() as block:
            @block.sync
            def _(sp):
                def load(b, p):
                    counted(sp, av_ready, b * NG - NG)
                    for dst, s in ((q, q_d), (k, k_d), (v, v_d)):
                        sp.dma_start(dst[:, p], s[b]).then_inc(loaded[p], 16)

                def step(u, nxt):
                    b, p, g, n = u
                    if nxt and g == 0:
                        pass
                    if g == 0 and (nxt and not (isinstance(b, int) and b == B - 1)):
                        load(b + 1, 1 - p)
                    counted(sp, out_ready, n + 1)
                    sp.dma_start(out_d[b, :, g, :], out[:, g % 2]).then_inc(stored[g % 2], 16)

                units(sp, NG, lambda u: load(0, 0), step)
                for s in stored:
                    sp.wait_ge(s, 16 * B * NG // 2)

            @block.gpsimd
            def _(pool):
                prime(pool, qd_ready)

                def ahead(u):
                    b, p, g, n = u
                    pool.wait_ge(loaded[p], half(b, p) * 48 + 48)
                    counted(pool, s1_ready, n - 1)
                    for j in range(4):
                        h = g % 2 * 4 + j
                        last = nc.gpsimd.tensor_tensor(qd[:, g % 2, j], q[:, p, g // 2],
                                                       c["headmask"][:, h:h + 1].to_broadcast([P, S]), ALU.mult)
                    last.then_inc(qd_ready, 1)

                units(pool, NG, ahead, lambda u, nxt: nxt and ahead(nxt))

            @block.scalar
            def _(act):
                act.preload_act_table_set(EXP_LN)
                prime(act, kr_ready, qdr_ready, p0_ready, p1_ready, av_copied)

                def ahead(u):
                    b, p, g, n = u
                    if g == 0:
                        act.wait_ge(loaded[p], half(b, p) * 48 + 48)
                        nc.scalar.activation(k_r[:, p], k[:, p], ACT.Copy).then_inc(kr_ready, 1)
                    counted(act, qd_ready, n + 1)
                    counted(act, max_ready, n * 4)
                    nc.scalar.activation(qd_r[:], qd[:, g % 2], ACT.Copy).then_inc(qdr_ready, 1)

                def step(u, nxt):
                    b, p, g, n = u
                    counted(act, av_ready, n - 1)
                    counted(act, s0_ready, n + 1)
                    for h in range(2):
                        last = nc.scalar.activation(p0[:, g % 2, 2 * h:2 * h + 2], s0_ps[h][:].rearrange("p (h s) -> p h s", h=2),
                                                    ACT.Exp, scale=SHD ** -0.5)
                    last.then_inc(p0_ready, 1)
                    counted(act, s1_ready, n + 1)
                    nc.scalar.activation(p1[:, g % 2], s1_ps[0][:].rearrange("p (h s) -> p h s", h=4), ACT.Exp,
                                         scale=SHD ** -0.5).then_inc(p1_ready, 1)
                    if nxt:
                        ahead(nxt)
                    counted(act, av_ready, n + 1)
                    counted(act, out_ready, n)
                    nc.scalar.activation(av[:], av_ps[0][:, 0:S], ACT.Copy).then_inc(av_copied, 1)

                units(act, NG, ahead, step)

            @block.vector
            def _(dve):
                prime(dve, maxed, diag_ready, rsum_ready, out_ready)

                def ahead(u):
                    b, p, g, n = u
                    for j in range(4):
                        counted(dve, max_ready, n * 4 + j + 1)
                        nc.vector.tensor_reduce(negmax[:, g % 2, j], max_ps[j % 2][:].rearrange("p (t s) -> p t s", t=2),
                                                AX.X, ALU.max, negate=True).then_inc(maxed, 1)
                    counted(dve, maxed, n * 4 + 4)
                    counted(dve, s1_ready, n - 1)
                    for j in range(4):
                        for t in range(2):
                            last = nc.vector.tensor_scalar(diag[:, g % 2, j, t * P:(t + 1) * P], c["ident"][:],
                                                           negmax[:, g % 2, j, t:t + 1], None, ALU.mult)
                    last.then_inc(diag_ready, 1)

                def step(u, nxt):
                    b, p, g, n = u
                    if nxt:
                        ahead(nxt)
                    counted(dve, sum_ready, n + 1)
                    nc.vector.reciprocal(rsum[:], sum_ps[0][:, 0:S]).then_inc(rsum_ready, 1)
                    counted(dve, rsum_ready, n + 1)
                    dve.wait_ge(stored[g % 2], (b * 2 + g // 2) * 16)
                    nc.vector.tensor_tensor(out[:, g % 2], av[:], rsum[:], ALU.mult).then_inc(out_ready, 1)

                units(dve, NG, ahead, step)

            @block.tensor
            def _(pe):
                prime(pe, max_ready, s0_ready, s1_ready, av_ready, sum_ready)

                def maxima(u, heads):
                    b, p, g, n = u
                    if 0 in heads:
                        counted(pe, kr_ready, b + 1)
                        counted(pe, qdr_ready, n + 1)
                    for j in heads:
                        counted(pe, maxed, n * 4 + j - 1)
                        for t in range(2):
                            o = max_ps[j % 2][:, t * S:(t + 1) * S]
                            nc.tensor.matmul(o, qd_r[:, j, t * P:(t + 1) * P], k_r[:, p, g // 2], start=True, stop=False)
                            last = nc.tensor.matmul(o, c["ident_b"][:], c["causal"][:, t], start=False, stop=True)
                        last.then_inc(max_ready, 1)

                def scores(u, t):
                    b, p, g, n = u
                    lo = t * P
                    for h in range(2):
                        if t == 0:
                            o = s0_ps[h][:].rearrange("p (h s) -> p h s", h=2)
                        else:
                            o = s1_ps[0][:, h * 2 * P:(h + 1) * 2 * P].rearrange("p (h s) -> p h s", h=2)
                        two = slice(2 * h, 2 * h + 2)
                        nc.tensor.matmul(o, k[:, p, g // 2, t * P:(t + 1) * P], qd[:, g % 2, two, lo:S], start=True, stop=False)
                        nc.tensor.matmul(o[:, :, 0:P], c["ident_b"][:],
                                         c["causal_tb"][:, t, lo:lo + P].unsqueeze(1).to_broadcast([P, 2, P]),
                                         start=False, stop=False)
                        last = nc.tensor.matmul(o, c["ones_r"][:], diag[:, g % 2, two, lo:S], start=False, stop=True)
                    last.then_inc(s1_ready if t else s0_ready, 1)

                def step(u, nxt):
                    b, p, g, n = u
                    counted(pe, diag_ready, n + 1)
                    counted(pe, qd_ready, n + 1)
                    counted(pe, p0_ready, n)
                    scores(u, 0)
                    counted(pe, p1_ready, n)
                    scores(u, 1)
                    if nxt:
                        maxima(nxt, (0, 1))
                    counted(pe, p0_ready, n + 1)
                    counted(pe, av_copied, n)
                    for j in range(4):
                        nc.tensor.matmul(av_ps[0][32 * j:32 * j + 32, 0:S], v[:, p, 0, 4 * g + j], p0[:, g % 2, j],
                                         start=True, stop=False)
                    counted(pe, p1_ready, n + 1)
                    for j in range(4):
                        last = nc.tensor.matmul(av_ps[0][32 * j:32 * j + 32, P:S], v[:, p, 1, 4 * g + j], p1[:, g % 2, j],
                                                start=False, stop=True)
                    last.then_inc(av_ready, 1)
                    if nxt:
                        maxima(nxt, (2, 3))
                    counted(pe, av_copied, n + 1)
                    counted(pe, rsum_ready, n)
                    nc.tensor.matmul(sum_ps[0][:, 0:S], c["sum16"][:], av[:], start=True, stop=True).then_inc(sum_ready, 1)

                units(pe, NG, lambda u: maxima(u, (0, 1, 2, 3)), step)


def residual_norm(nc, c, name, x_d, norm, w_norm, b_norm=None, attn_d=None, w_attn=None, experts=False, gate=None,
                  x_out_d=None, normed_d=None, w_proj=None, proj_d=None, split=False):
    NE = 2 if experts else 1
    with Phase(nc, name) as ph:
        ka = attn_d.shape[2] if attn_d is not None else 0
        kp = proj_d.shape[2] if proj_d is not None else 0
        x, x1 = ph.sb("x", [P, 2, DC, S]), ph.sb("x1", [P, 2, DC, S])
        xc, sq, ln = ph.sb("xc", [P, DC, S]), ph.sb("sq", [P, DC, S]), ph.sb("ln", [P, S])
        rs, xs = ph.sb("rs", [P, S]), ph.sb("xs", [P, DC, S])
        xn = ph.sb("xn", [P, 2, DC, S])
        if ka:
            at = ph.sb("at", [P, 2, ka, S])
            ae = ph.sb("ae", [P, 2, 2, ka, S]) if experts else None
            wa = ph.sb("wa", [P, NE * ka, D])
        if kp:
            wp = ph.sb("wp", [P, DC, kp * P])
            high = ph.sb("high", [P, kp, S], F32R) if split else None
            pr = ph.sb("pr", [P, 2, kp, S], F32R if split else F32)
        at_ps, mean_ps, var_ps, pr_ps = (ph.banks(n, m) for n, m in (("at", 2), ("mean", 1), ("var", 1), ("pr", 4)))
        loaded, w_ready = ph.sems2("loaded"), ph.sem("w_ready")
        stored, pr_stored = ph.sems2("stored"), ph.sems2("pr_stored")
        ae_ready, at_ready, x1_ready, mean_ready, xc_ready = (
            ph.sem(n) for n in ("ae_ready", "at_ready", "x1_ready", "mean_ready", "xc_ready"))
        sq_ready, var_ready, ln_ready, rs_ready, xs_ready, xn_ready = (
            ph.sem(n) for n in ("sq_ready", "var_ready", "ln_ready", "rs_ready", "xs_ready", "xn_ready"))
        pr_ready, high_ready, pr_copied = ph.sem("pr_ready"), ph.sem("high_ready"), ph.sem("pr_copied")
        n_loads = 1 + (ka > 0)
        n_stored = (x_out_d is not None) + (normed_d is not None)
        n_weights = (NE if ka else 0) + (kp > 0)
        kpp = max(1, kp // 2)
        pair = min(kp, 2)
        with nc.Block() as block:
            @block.sync
            def _(sp):
                if ka:
                    for e, w in enumerate(w_attn):
                        sp.dma_start(wa[:, e * ka:(e + 1) * ka], w).then_inc(w_ready, 16)
                if kp:
                    sp.dma_start(wp[:], w_proj).then_inc(w_ready, 16)

                def load(u):
                    b, p, _, _ = u
                    counted(sp, xn_ready, b - 1)
                    sp.dma_start(x[:, p], x_d[b]).then_inc(loaded[p], 16)
                    if ka:
                        sp.dma_start(at[:, p], attn_d[b]).then_inc(loaded[p], 16)

                def step(u, nxt):
                    if nxt:
                        load(nxt)
                    b, p, _, _ = u
                    if x_out_d is not None:
                        counted(sp, x1_ready, b + 1)
                        sp.dma_start(x_out_d[b], x1[:, p]).then_inc(stored[p], 16)
                    if normed_d is not None:
                        counted(sp, xn_ready, b + 1)
                        sp.dma_start(normed_d[b], xn[:, p]).then_inc(stored[p], 16)
                    if kp:
                        counted(sp, pr_copied, (b + 1) * kpp)
                        sp.dma_start(proj_d[b], pr[:, p].bitcast(F32) if split else pr[:, p]).then_inc(pr_stored[p], 16)

                units(sp, 1, load, step)
                for p in range(2):
                    if n_stored:
                        sp.wait_ge(stored[p], B // 2 * n_stored * 16)
                    if kp:
                        sp.wait_ge(pr_stored[p], B // 2 * 16)

            @block.scalar
            def _(act):
                act.preload_act_table_set(EXP_LN)
                prime(act, sq_ready, ln_ready, rs_ready, high_ready)
                if kp and not split:
                    prime(act, pr_copied)

                def ahead(u):
                    b, p, _, _ = u
                    counted(act, xc_ready, b + 1)
                    counted(act, var_ready, b)
                    nc.scalar.activation(sq[:], xc[:], ACT.Square).then_inc(sq_ready, 1)

                def statistics(u):
                    b, p, _, _ = u
                    counted(act, var_ready, b + 1)
                    eps = c["eps5"] if norm == "layer" else c["eps6"]
                    nc.scalar.activation(ln[:], var_ps[0][:, 0:S], ACT.Ln, bias=eps[:, 0:1]).then_inc(ln_ready, 1)
                    counted(act, ln_ready, b + 1)
                    counted(act, xs_ready, b)
                    nc.scalar.activation(rs[:], ln[:], ACT.Exp, scale=-0.5).then_inc(rs_ready, 1)

                def project(u):
                    b, p, _, _ = u
                    if not kp:
                        return
                    act.wait_ge(pr_stored[p], half(b, p) * 16)
                    for m in range(kpp):
                        counted(act, pr_ready, b * kpp + m + 1)
                        src = pr_ps[m % 4][:, 0:pair * S].rearrange("p (m s) -> p m s", m=pair)
                        if split:
                            if m == 0:
                                counted(act, pr_copied, b * kpp)
                            nc.scalar.activation(high[:, 2 * m:2 * m + 2], src, ACT.Copy, scale=c["low"][:, 3:4]
                                                 ).then_inc(high_ready, 1)
                        else:
                            nc.scalar.activation(pr[:, p, pair * m:pair * m + pair], src, ACT.Copy).then_inc(pr_copied, 1)

                def first_unit(u):
                    ahead(u)
                    statistics(u)

                def step(u, nxt):
                    if nxt:
                        ahead(nxt)
                    project(u)
                    if nxt:
                        statistics(nxt)

                units(act, 1, first_unit, step)

            @block.vector
            def _(dve):
                prime(dve, ae_ready, x1_ready, xc_ready, xs_ready, xn_ready)
                if kp and split:
                    prime(dve, pr_copied)

                def residual(u):
                    b, p, _, _ = u
                    dve.wait_ge(loaded[p], (half(b, p) + 1) * 16 * n_loads)
                    if experts:
                        counted(dve, at_ready, b - 1)
                        for g in range(ka):
                            last = nc.vector.tensor_tensor(ae[:, p, 0, g], at[:, p, g], c["vm"][:, b, :], ALU.mult)
                        last.then_inc(ae_ready, 1)
                        counted(dve, ae_ready, b * 2 + 1)
                        nc.vector.tensor_tensor(ae[:, p, 1], at[:, p], ae[:, p, 0], ALU.subtract).then_inc(ae_ready, 1)
                    if n_stored:
                        dve.wait_ge(stored[p], half(b, p) * 16 * n_stored)
                    if ka:
                        counted(dve, at_ready, b + 1)
                        src = at_ps[p][:].rearrange("p (m s) -> p m s", m=DC)
                        if gate is not None:
                            nc.vector.scalar_tensor_tensor(x1[:, p], src, gate, x[:, p], ALU.mult, ALU.add
                                                           ).then_inc(x1_ready, 1)
                        else:
                            nc.vector.tensor_tensor(x1[:, p], src, x[:, p], ALU.add).then_inc(x1_ready, 1)
                    else:
                        nc.vector.tensor_copy(x1[:, p], x[:, p]).then_inc(x1_ready, 1)
                    counted(dve, x1_ready, b + 1)
                    counted(dve, sq_ready, b)
                    if norm == "layer":
                        counted(dve, mean_ready, b + 1)
                        for k in range(DC):
                            last = nc.vector.tensor_tensor(xc[:, k], x1[:, p, k], mean_ps[0][:, 0:S], ALU.subtract)
                    else:
                        last = nc.vector.tensor_copy(xc[:], x1[:, p])
                    last.then_inc(xc_ready, 1)

                def normalise(u):
                    b, p, _, _ = u
                    counted(dve, rs_ready, b + 1)
                    if kp:
                        counted(dve, pr_ready, (b - 1) * kpp)
                    dst = xs if norm == "layer" else xn[:, p]
                    for k in range(DC):
                        last = nc.vector.scalar_tensor_tensor(dst[:, k], xc[:, k], w_norm[:, k:k + 1], rs[:],
                                                              ALU.mult, ALU.mult)
                    last.then_inc(xs_ready, 1)
                    counted(dve, xs_ready, b + 1)
                    if norm == "layer":
                        for k in range(DC):
                            last = nc.vector.tensor_scalar(xn[:, p, k], xs[:, k], b_norm[:, k:k + 1], None, ALU.add)
                        last.then_inc(xn_ready, 1)
                    else:
                        dve.sem_inc(xn_ready, 1)

                def low_parts(u):
                    b, p, _, _ = u
                    dve.wait_ge(pr_stored[p], half(b, p) * 16)
                    for m in range(kpp):
                        counted(dve, high_ready, b * kpp + m + 1)
                        src = pr_ps[m % 4][:].rearrange("p (m s) -> p m s", m=2)
                        nc.vector.scalar_tensor_tensor(pr[:, p, 2 * m:2 * m + 2], src, c["low"][:, 0:1],
                                                       high[:, 2 * m:2 * m + 2], ALU.mult, ALU.add).then_inc(pr_copied, 1)

                def first_unit(u):
                    residual(u)
                    normalise(u)

                def step(u, nxt):
                    if nxt:
                        residual(nxt)
                    if kp and split:
                        low_parts(u)
                    if nxt:
                        normalise(nxt)

                units(dve, 1, first_unit, step)

            @block.tensor
            def _(pe):
                prime(pe, at_ready, mean_ready, var_ready, pr_ready)
                if n_weights:
                    pe.wait_ge(w_ready, n_weights * 16)

                def attend(u):
                    b, p, _, _ = u
                    if not ka:
                        return
                    if experts:
                        counted(pe, ae_ready, b * 2 + 2)
                    else:
                        pe.wait_ge(loaded[p], (half(b, p) + 1) * 16 * n_loads)
                    counted(pe, x1_ready, b - 1)
                    for m in range(DC):
                        for n in range(NE * ka):
                            rhs = ae[:, p, n // ka, n % ka] if experts else at[:, p, n]
                            last = nc.tensor.matmul(at_ps[p][:, m * S:(m + 1) * S], wa[:, n, m * P:(m + 1) * P], rhs,
                                                    start=(n == 0), stop=(n == NE * ka - 1))
                    last.then_inc(at_ready, 1)

                def statistics(u):
                    b, p, _, _ = u
                    if norm == "layer":
                        counted(pe, x1_ready, b + 1)
                        counted(pe, xc_ready, b)
                        for k in range(DC):
                            last = nc.tensor.matmul(mean_ps[0][:, 0:S], c["mean"][:], x1[:, p, k], start=(k == 0), stop=(k == DC - 1))
                        last.then_inc(mean_ready, 1)
                    counted(pe, sq_ready, b + 1)
                    counted(pe, ln_ready, b)
                    for k in range(DC):
                        last = nc.tensor.matmul(var_ps[0][:, 0:S], c["mean"][:], sq[:, k], start=(k == 0), stop=(k == DC - 1))
                    last.then_inc(var_ready, 1)

                def project(u):
                    b, p, _, _ = u
                    if not kp:
                        return
                    counted(pe, xn_ready, b + 1)
                    for m in range(kpp):
                        counted(pe, pr_copied, b * kpp + m - 3 if kpp >= 4 else (b - 1) * kpp + m + 1)
                        for h in range(pair):
                            t = pair * m + h
                            for k in range(DC):
                                last = nc.tensor.matmul(pr_ps[m % 4][:, h * S:(h + 1) * S], wp[:, k, t * P:(t + 1) * P],
                                                        xn[:, p, k], start=(k == 0), stop=(k == DC - 1))
                        last.then_inc(pr_ready, 1)

                def first_unit(u):
                    attend(u)
                    statistics(u)

                def step(u, nxt):
                    if nxt:
                        attend(nxt)
                    project(u)
                    if nxt:
                        statistics(nxt)

                units(pe, 1, first_unit, step)


def width(t):
    return P if t < KT - 1 else KLAST


def cross_attention_0(nc, src, c, q_d, out_d):
    with Phase(nc, "cross0") as ph:
        ct = ph.sb("ct", [P, 2, NKP])
        wk, wv = ph.sb("wk", [P, NG * P]), ph.sb("wv", [P, C])
        k_high = ph.sb("k_high", [P, 2, 512], F32R)
        ks = ph.sb("ks", [P, 2, NKP], F32R)
        qd = ph.sb("qd", [P, 2, 4, S], F32R)
        cv = ph.sb("cv", [P, 2, KT, C])
        v = ph.sb("v", [P, 2, KT, 4, 32])
        partmax, negmax = ph.sb("partmax", [P, 8, len(KCH)]), ph.sb("negmax", [P, 8])
        diag = ph.sb("diag", [P, 4, S], F32R)
        probs = ph.sb("probs", [P, 3, 4, S])
        av, rsum, out = ph.sb("av", [P, S]), ph.sb("rsum", [P, S]), ph.sb("out", [P, 2, S])
        max_ps, s_ps = ph.banks("max", 2), ph.banks("s", 2, 1024)
        av_ps, misc_ps = ph.banks("av", 1)[0], ph.banks("misc", 1)[0]
        loaded, stored, w_ready = ph.sems2("loaded"), ph.sems2("stored"), ph.sem("w_ready")
        q_loaded, v_set, qd_set = ph.sems2("q_loaded"), ph.sem("v_set"), ph.sem("qd_set")
        kp_ready, k_high_ready, k_ready, vp_ready, cv_ready, v_ready = (
            ph.sem(n) for n in ("kp_ready", "k_high_ready", "k_ready", "vp_ready", "cv_ready", "v_ready"))
        max_ready, maxed, negmax_ready, diag_ready, shift_ready, shifted = (
            ph.sem(n) for n in ("max_ready", "maxed", "negmax_ready", "diag_ready", "shift_ready", "shifted"))
        s_ready, probs_ready, probs_used, av_copied, sum_ready, rsum_ready, out_ready = (
            ph.sem(n) for n in ("s_ready", "probs_ready", "probs_used", "av_copied", "sum_ready", "rsum_ready", "out_ready"))
        NC = len(KCH)
        NM = 8 * NC

        with nc.Block() as block:
            @block.sync
            def _(sp):
                sp.wait_ge(qd_set, 1)
                sp.dma_start(wk[:], src["ck_stack"]).then_inc(w_ready, 16)
                sp.dma_start(wv[:], src["cv"]).then_inc(w_ready, 16)

                def load(b, p):
                    counted(sp, probs_used, (b - 1) * NG * KT)
                    sp.dma_start(ct[:, p], src["ctx_t"][b]).then_inc(loaded[p], 16)

                def load_q(u):
                    b, p, g, n = u
                    counted(sp, probs_used, (n - 1) * KT)
                    for j in range(4):
                        r = slice(32 * j, 32 * j + 32)
                        sp.dma_start(qd[r, g % 2, j].bitcast(F32), q_d[b, r, g, :]).then_inc(q_loaded[g % 2], 16)

                def ahead(u):
                    load(0, 0)
                    load_q(u)

                def step(u, nxt):
                    b, p, g, n = u
                    if g == 0 and not (isinstance(b, int) and b == B - 1):
                        load(b + 1, 1 - p)
                    if nxt:
                        load_q(nxt)
                    counted(sp, out_ready, n + 1)
                    sp.dma_start(out_d[b, :, g, :], out[:, g % 2]).then_inc(stored[g % 2], 16)

                units(sp, NG, ahead, step)
                for s in stored:
                    sp.wait_ge(s, 16 * B * NG // 2)

            @block.gpsimd
            def _(pool):
                nc.gpsimd.memset(qd[:].bitcast(F32), 0.0).then_inc(qd_set, 1)
                nc.gpsimd.memset(v[:], 0.0).then_inc(v_set, 1)
                pool.wait_ge(v_set, 1)
                nc.gpsimd.memset(v[:, :, :, :, CHD:CHD + 1], 1.0).then_inc(v_set, 1)


            def copy_shift(eng, u, heads):
                b, p, g, n = u
                counted(eng, shift_ready, n + 1)
                for j in heads:
                    r = slice(32 * j, 32 * j + 1)
                    if eng is nc.scalar:
                        nc.scalar.activation(qd[r, g % 2, j], av_ps[r, S:2 * S], ACT.Copy).then_inc(shifted, 1)
                    else:
                        nc.vector.tensor_copy(qd[r, g % 2, j], av_ps[r, S:2 * S]).then_inc(shifted, 1)

            @block.scalar
            def _(act):
                act.preload_act_table_set(EXP_LN)
                prime(act, k_high_ready, cv_ready, probs_ready, av_copied)

                def k_chunk(u, i):
                    b, p, g, n = u
                    w = KCH[i][1]
                    counted(act, kp_ready, n * NC + i + 1)
                    counted(act, k_ready, n * NC + i - 1)
                    nc.scalar.activation(k_high[:, i % 2, 0:w], misc_ps[:, 0:w], ACT.Identity, scale=c["low"][:, 4:5],
                                         bias=c["low"][:, 2:3]).then_inc(k_high_ready, 1)

                def v_chunk(u, i):
                    b, p, g, n = u
                    counted(act, vp_ready, b * NC + i + 1)
                    if i == 0:
                        counted(act, v_ready, (b - 1) * NG)
                    rows, tiles = (P, 4) if i < NC - 1 else (KLAST, 1)
                    nc.scalar.activation(cv[0:rows, p, 4 * i:4 * i + tiles], misc_ps[0:rows, 0:tiles * C]
                                         .rearrange("p (t d) -> p t d", t=tiles), ACT.Copy).then_inc(cv_ready, 1)

                def ahead(u):
                    for i in range(NC):
                        k_chunk(u, i)
                    for i in range(NC):
                        v_chunk(u, i)
                    copy_shift(nc.scalar, u, (0, 2))

                def step(u, nxt):
                    b, p, g, n = u
                    for t in range(KT):
                        w = width(t)
                        counted(act, s_ready, n * KT + t + 1)
                        counted(act, probs_used, n * KT + max(t - 2, 0))
                        nc.scalar.activation(probs[0:w, t % 3], s_ps[t % 2][0:w].rearrange("p (h s) -> p h s", h=4),
                                             ACT.Exp, scale=CHD ** -0.5).then_inc(probs_ready, 1)
                        if nxt and t < NC:
                            k_chunk(nxt, t)
                        elif nxt and nxt[2] == 0 and t < 2 * NC:
                            v_chunk(nxt, t - NC)
                    counted(act, probs_used, (n + 1) * KT)
                    counted(act, out_ready, n)
                    nc.scalar.activation(av[:], av_ps[:, 0:S], ACT.Copy).then_inc(av_copied, 1)
                    if nxt:
                        copy_shift(nc.scalar, nxt, (0, 2))

                units(act, NG, ahead, step)

            @block.vector
            def _(dve):
                prime(dve, k_ready, v_ready, maxed, negmax_ready, diag_ready, rsum_ready, out_ready)
                prime(dve, shifted)

                def ahead(u):
                    b, p, g, n = u
                    counted(dve, s_ready, (n - 1) * KT)
                    for i, (k0, w) in enumerate(KCH):
                        counted(dve, k_high_ready, n * NC + i + 1)
                        nc.vector.scalar_tensor_tensor(ks[:, g % 2, k0:k0 + w], misc_ps[:, 0:w], c["low"][:, 1:2],
                                                       k_high[:, i % 2, 0:w], ALU.mult, ALU.add).then_inc(k_ready, 1)
                    counted(dve, negmax_ready, n)
                    for m in range(NM):
                        w = KCH[m % NC][1]
                        counted(dve, max_ready, n * NM + m + 1)
                        nc.vector.tensor_reduce(partmax[:, m // NC, m % NC:m % NC + 1], max_ps[m % 2][:, 0:w], AX.X, ALU.max
                                                ).then_inc(maxed, 1)
                    if isinstance(n, int) and n == 0:
                        dve.wait_ge(v_set, 2)
                    counted(dve, cv_ready, (b + 1) * NC)
                    counted(dve, probs_used, (n - 1) * KT)
                    nc.vector.tensor_copy(v[:, g % 2, 0:KT - 1, :, 0:CHD],
                                          cv[:, p, 0:KT - 1, g * 32:g * 32 + 32].rearrange("p t (j d) -> p t j d", j=4))
                    nc.vector.tensor_copy(v[0:KLAST, g % 2, KT - 1, :, 0:CHD],
                                          cv[0:KLAST, p, KT - 1, g * 32:g * 32 + 32].rearrange("p (j d) -> p j d", j=4)
                                          ).then_inc(v_ready, 1)
                    counted(dve, maxed, (n + 1) * NM)
                    counted(dve, diag_ready, n)
                    nc.vector.tensor_reduce(negmax[:], partmax[:], AX.X, ALU.max, negate=True).then_inc(negmax_ready, 1)
                    counted(dve, negmax_ready, n + 1)
                    counted(dve, shift_ready, n)
                    for m in range(8):
                        last = nc.vector.tensor_scalar(diag[:, m // 2, m % 2 * P:m % 2 * P + P], c["ident"][:],
                                                       negmax[:, m:m + 1], None, ALU.mult)
                    last.then_inc(diag_ready, 1)
                    copy_shift(nc.vector, u, (1, 3))

                def step(u, nxt):
                    b, p, g, n = u
                    if nxt:
                        ahead(nxt)
                    counted(dve, sum_ready, n + 1)
                    nc.vector.reciprocal(rsum[:], misc_ps[:, 0:S]).then_inc(rsum_ready, 1)
                    counted(dve, rsum_ready, n + 1)
                    dve.wait_ge(stored[g % 2], (b * 2 + g // 2) * 16)
                    nc.vector.tensor_tensor(out[:, g % 2], av[:], rsum[:], ALU.mult).then_inc(out_ready, 1)

                units(dve, NG, ahead, step)

            @block.tensor
            def _(pe):
                prime(pe, kp_ready, vp_ready, max_ready, shift_ready, s_ready, probs_used, sum_ready)
                pe.wait_ge(w_ready, 32)

                def k_chunk(u, i):
                    b, p, g, n = u
                    k0, w = KCH[i]
                    if i == 0:
                        pe.wait_ge(loaded[p], half(b, p) * 16 + 16)
                        counted(pe, rsum_ready, n - 1)
                    counted(pe, k_ready, n * NC + i)
                    nc.tensor.matmul(misc_ps[:, 0:w], wk[:, g * P:(g + 1) * P], ct[:, p, k0:k0 + w], start=True, stop=True
                                     ).then_inc(kp_ready, 1)

                def v_chunk(u, i):
                    b, p, g, n = u
                    if i == 0:
                        counted(pe, k_ready, (n + 1) * NC)
                    counted(pe, cv_ready, b * NC + i)
                    for t in range(4 * i, min(4 * i + 4, KT)):
                        w = width(t)
                        last = nc.tensor.matmul(misc_ps[0:w, t % 4 * C:(t % 4 + 1) * C], ct[:, p, t * P:t * P + w], wv[:],
                                                start=True, stop=True)
                    last.then_inc(vp_ready, 1)

                def maxima(u, m):
                    b, p, g, n = u
                    if m == 0:
                        counted(pe, k_ready, (n + 1) * NC)
                        pe.wait_ge(q_loaded[g % 2], (b * 2 + g // 2 + 1) * 64)
                    for i, (k0, w) in enumerate(KCH):
                        counted(pe, maxed, n * NM + m * NC + i - 1)
                        nc.tensor.matmul(max_ps[i % 2][:, 0:w], qd[:, g % 2, m // 2, m % 2 * P:m % 2 * P + P],
                                         ks[:, g % 2, k0:k0 + w], start=True, stop=True).then_inc(max_ready, 1)

                def shift(u):
                    b, p, g, n = u
                    counted(pe, diag_ready, n + 1)
                    counted(pe, av_copied, n)
                    for j in range(4):
                        last = nc.tensor.matmul(av_ps[:, S:2 * S], c["sel_r"][:, j], diag[:, j], start=(j == 0), stop=(j == 3))
                    last.then_inc(shift_ready, 1)

                def scores(u, t):
                    b, p, g, n = u
                    w = width(t)
                    counted(pe, probs_ready, n * KT + t - 1)
                    if t == 0:
                        counted(pe, probs_ready, n * KT)
                    for h in range(2):
                        last = nc.tensor.matmul(s_ps[t % 2][0:w, h * 512:(h + 1) * 512], ks[:, g % 2, t * P:t * P + w],
                                                qd[:, g % 2, 2 * h:2 * h + 2, :], start=True, stop=True)
                    last.then_inc(s_ready, 1)

                def values(u, t):
                    b, p, g, n = u
                    w = width(t)
                    counted(pe, probs_ready, n * KT + t + 1)
                    if t == 0:
                        counted(pe, v_ready, n + 1)
                    for j in range(4):
                        last = nc.tensor.matmul(av_ps[32 * j:32 * j + 32, 0:S], v[0:w, g % 2, t, j], probs[0:w, t % 3, j],
                                                start=(t == 0), stop=(t == KT - 1))
                    last.then_inc(probs_used, 1)

                def ahead(u):
                    for i in range(NC):
                        k_chunk(u, i)
                    for i in range(NC):
                        v_chunk(u, i)
                    for m in range(8):
                        maxima(u, m)
                    shift(u)

                def step(u, nxt):
                    b, p, g, n = u
                    counted(pe, shifted, (n + 1) * 4)
                    scores(u, 0)
                    for t in range(KT):
                        if t + 1 < KT:
                            scores(u, t + 1)
                        if nxt and t < NC:
                            k_chunk(nxt, t)
                        elif nxt and nxt[2] == 0 and t < 2 * NC:
                            v_chunk(nxt, t - NC)
                        if nxt and NC <= t < NC + 8:
                            maxima(nxt, t - NC)
                        values(u, t)
                    if nxt:
                        shift(nxt)
                    counted(pe, av_copied, n + 1)
                    if nxt:
                        counted(pe, k_ready, (n + 2) * NC)
                        if nxt[2] == 0:
                            counted(pe, cv_ready, (b + 2) * NC)
                    else:
                        counted(pe, rsum_ready, n)
                    nc.tensor.matmul(misc_ps[:, 0:S], c["sum8"][:], av[:], start=True, stop=True).then_inc(sum_ready, 1)

                units(pe, NG, ahead, step)


def v_share(g):
    lo = (0, 4, 7, 10, 13)
    return range(lo[g % 4], lo[g % 4 + 1])


def cross_attention_1(nc, src, c, masked_d, q_d, out_d):
    with Phase(nc, "cross1") as ph:
        ct, cm = ph.sb("ct", [P, 2, NKP]), ph.sb("cm", [P, 2, NKP])
        wk, wv = ph.sb("wk", [P, NP, P]), ph.sb("wv", [P, 2, 512])
        qp = ph.sb("qp", [P, 2, S])
        ka, kb = ph.sb("ka", [P, 2, 2, NKP], F32R), ph.sb("kb", [P, 2, 2, NKP], F32R)
        qa, qb = ph.sb("qa", [P, 2, 2, S], F32R), ph.sb("qb", [P, 2, 2, S], F32R)
        v = ph.sb("v", [P, 2, KT, 512])
        partmax, negmax = ph.sb("partmax", [P, 4, len(KCH)]), ph.sb("negmax", [P, 4])
        diag = ph.sb("diag", [P, 2, S], F32R)
        bias = ph.sb("bias", [P, 2, KT])
        NPB = 4
        probs, acc = ph.sb("probs", [P, NPB, 2, S]), ph.sb("acc", [P, 2, S])
        av, rsum, out = ph.sb("av", [P, S]), ph.sb("rsum", [P, S]), ph.sb("out", [P, 2, S])
        k_ps, max_ps, s_ps = ph.banks("k", 2), ph.banks("max", 2), ph.banks("s", 2)
        av_ps, misc_ps = ph.banks("av", 1)[0], ph.banks("misc", 1)[0]
        loaded, q_loaded, stored = ph.sems2("loaded"), ph.sems2("q_loaded"), ph.sems2("stored")
        bias_ready, w_ready, kb_set, qb_set = ph.sem("bias_ready"), ph.sem("w_ready"), ph.sem("kb_set"), ph.sem("qb_set")
        kp_ready, ka_ready, kb_ready, vp_ready, v_ready, qb_ready, q_ready = (
            ph.sem(n) for n in ("kp_ready", "ka_ready", "kb_ready", "vp_ready", "v_ready", "qb_ready", "q_ready"))
        max_ready, maxed, negmax_ready, diag_ready, shift_ready, shifted = (
            ph.sem(n) for n in ("max_ready", "maxed", "negmax_ready", "diag_ready", "shift_ready", "shifted"))
        s_ready, probs_ready, probs_used, added, av_copied, sum_ready, rsum_ready, out_ready = (
            ph.sem(n) for n in ("s_ready", "probs_ready", "probs_used", "added", "av_copied", "sum_ready", "rsum_ready", "out_ready"))
        NC = len(KCH)
        NM = 4 * NC
        once = (slice(0, 64), slice(64, P))
        other = (slice(64, P), slice(0, 64))
        row = (slice(64, 65), slice(0, 1))

        def next_half(u):
            b, p, g, n = u
            if g < NP // 2:
                return b, p, 1
            return None if isinstance(b, int) and b == B - 1 else (b + 1, 1 - p, 0)

        with nc.Block() as block:
            @block.sync
            def _(sp):
                sp.dma_start(wk[:], src["Wkv"][:, 0:NP * P].rearrange("p (h d) -> p h d", h=NP)).then_inc(w_ready, 16)
                sp.dma_start(wv[:], src["Wkv"][:, NP * P:].rearrange("p (h d) -> p h d", h=2)).then_inc(w_ready, 16)

                def load(b, p):
                    counted(sp, probs_used, (b - 1) * NP * KT)
                    sp.dma_start(ct[:, p], src["ctx_t"][b]).then_inc(loaded[p], 16)
                    sp.dma_start(cm[:, p], masked_d[b]).then_inc(loaded[p], 16)

                def load_q(u):
                    b, p, g, n = u
                    counted(sp, q_ready, n - 1)
                    sp.dma_start(qp[:, g % 2], q_d[b, :, g, :]).then_inc(q_loaded[g % 2], 16)

                def ahead(u):
                    load(0, 0)
                    load_q(u)

                def step(u, nxt):
                    b, p, g, n = u
                    if nxt:
                        load_q(nxt)
                    if g == 0 and not (isinstance(b, int) and b == B - 1):
                        load(b + 1, 1 - p)
                    counted(sp, out_ready, n + 1)
                    sp.dma_start(out_d[b, :, g, :], out[:, g % 2]).then_inc(stored[g % 2], 16)

                units(sp, NP, ahead, step)
                for s in stored:
                    sp.wait_ge(s, 16 * B * NP // 2)

            @block.gpsimd
            def _(pool):
                prime(pool, added)
                nc.gpsimd.memset(kb[:].bitcast(F32), 0.0).then_inc(kb_set, 1)
                pool.wait_ge(kb_set, 1)
                nc.gpsimd.memset(qb[:].bitcast(F32), 0.0).then_inc(qb_set, 1)
                pool.wait_ge(qb_set, 1)
                for h in range(2):
                    nc.gpsimd.memset(kb[row[h], :, h].bitcast(F32), 1.0).then_inc(kb_set, 1)
                    pool.wait_ge(kb_set, h + 2)

                def step(u, nxt):
                    b, p, g, n = u
                    for t in range(1, KT):
                        w = width(t)
                        counted(pool, probs_ready, n * KT + t + 1)
                        if t == 1:
                            counted(pool, sum_ready, n)
                        else:
                            counted(pool, added, n * (KT - 1) + t - 1)
                        left = probs[:, 0] if t == 1 else acc[0:w]
                        nc.gpsimd.tensor_tensor(acc[0:w], left, probs[0:w, t % NPB], ALU.add).then_inc(added, 1)

                units(pool, NP, lambda u: None, step)

            @block.scalar
            def _(act):
                act.preload_act_table_set(EXP_LN)
                prime(act, ka_ready, v_ready, probs_ready, av_copied)

                def k_chunk(u, i):
                    b, p, g, n = u
                    k0, w = KCH[i]
                    counted(act, kp_ready, n * NC + i + 1)
                    if i == 0:
                        counted(act, s_ready, (n - 1) * KT)
                    for h in range(2):
                        for half_rows in (once[h], other[h]):
                            last = nc.scalar.activation(ka[half_rows, g % 2, h, k0:k0 + w], k_ps[i % 2][once[h], 0:w], ACT.Copy)
                    last.then_inc(ka_ready, 1)

                def v_tile(hb, t):
                    b, p, h = hb
                    w = width(t)
                    n = (b * 2 + h) * KT + t
                    counted(act, vp_ready, n + 1)
                    if t == 0:
                        counted(act, probs_used, (b * 2 + h - 1) * 4 * KT)
                    nc.scalar.activation(v[0:w, h, t], misc_ps[0:w, :], ACT.Copy).then_inc(v_ready, 1)

                def ahead(u):
                    for i in range(NC):
                        k_chunk(u, i)
                    for t in range(KT):
                        v_tile((0, 0, 0), t)

                def step(u, nxt):
                    b, p, g, n = u
                    share = list(v_share(g)) if next_half(u) else []
                    if g == 0:
                        act.wait_ge(bias_ready, b + 1)
                    for t in range(KT):
                        w = width(t)
                        counted(act, s_ready, n * KT + t + 1)
                        counted(act, probs_used, n * KT + max(t - NPB + 1, 0))
                        counted(act, added, n * (KT - 1) + (max(t - NPB, 1) if t >= NPB else 0))
                        nc.scalar.activation(probs[0:w, t % NPB], s_ps[t % 2][0:w].rearrange("p (h s) -> p h s", h=2), ACT.Exp,
                                             scale=XHD ** -0.5, bias=bias[0:w, p, t:t + 1]).then_inc(probs_ready, 1)
                        if nxt and t < NC:
                            k_chunk(nxt, t)
                        elif NC <= t < NC + len(share):
                            v_tile(next_half(u), share[t - NC])
                    counted(act, probs_used, (n + 1) * KT)
                    counted(act, out_ready, n)
                    nc.scalar.activation(av[:], av_ps[:, 0:S], ACT.Copy).then_inc(av_copied, 1)

                units(act, NP, ahead, step)

            @block.vector
            def _(dve):
                prime(dve, kb_ready, qb_ready, q_ready, maxed, negmax_ready, diag_ready, shifted, rsum_ready, out_ready)
                dve.wait_ge(kb_set, 3)
                dve.wait_ge(qb_set, 1)

                def ahead(u):
                    b, p, g, n = u
                    q2 = g % 2
                    if g == 0:
                        counted(dve, probs_ready, (b - 1) * NP * KT)
                        nc.vector.tensor_scalar(bias[:, p], c["key_bias"][:, b, :], 1.0, None, ALU.mult).then_inc(bias_ready, 1)
                    dve.wait_ge(q_loaded[q2], (b * (NP // 2) + g // 2 + 1) * 16)
                    counted(dve, s_ready, (n - 1) * KT)
                    for h in range(2):
                        nc.vector.tensor_copy(qb[once[h], q2, h], qp[once[h], q2]).then_inc(qb_ready, 1)
                    counted(dve, qb_ready, (n + 1) * 2)
                    for h in range(2):
                        nc.vector.tensor_copy(qa[once[h], q2, h], qb[once[h], q2, h])
                        last = nc.vector.tensor_tensor(qa[other[h], q2, h], qp[once[h], q2], qb[once[h], q2, h], ALU.subtract)
                    last.then_inc(q_ready, 1)
                    for i, (k0, w) in enumerate(KCH):
                        counted(dve, ka_ready, n * NC + i + 1)
                        for h in range(2):
                            last = nc.vector.tensor_tensor(kb[once[h], q2, h, k0:k0 + w], k_ps[i % 2][once[h], 0:w],
                                                           ka[once[h], q2, h, k0:k0 + w], ALU.subtract)
                        last.then_inc(kb_ready, 1)
                    counted(dve, negmax_ready, n)
                    for m in range(NM):
                        w = KCH[m % NC][1]
                        counted(dve, max_ready, n * NM + m + 1)
                        nc.vector.tensor_reduce(partmax[:, m // NC, m % NC:m % NC + 1], max_ps[m % 2][:, 0:w], AX.X, ALU.max
                                                ).then_inc(maxed, 1)
                    counted(dve, maxed, (n + 1) * NM)
                    counted(dve, diag_ready, n)
                    nc.vector.tensor_reduce(negmax[:], partmax[:], AX.X, ALU.max, negate=True).then_inc(negmax_ready, 1)
                    counted(dve, negmax_ready, n + 1)
                    counted(dve, shift_ready, n)
                    for m in range(4):
                        last = nc.vector.tensor_scalar(diag[:, m // 2, m % 2 * P:m % 2 * P + P], c["ident"][:],
                                                       negmax[:, m:m + 1], None, ALU.mult)
                    last.then_inc(diag_ready, 1)
                    counted(dve, shift_ready, n + 1)
                    for h in range(2):
                        last = nc.vector.tensor_copy(qb[row[h], q2, h], misc_ps[row[h], h * S:(h + 1) * S])
                    last.then_inc(shifted, 1)

                def step(u, nxt):
                    b, p, g, n = u
                    if nxt:
                        ahead(nxt)
                    counted(dve, sum_ready, n + 1)
                    counted(dve, out_ready, n)
                    nc.vector.reciprocal(rsum[:], misc_ps[:, 0:S]).then_inc(rsum_ready, 1)
                    counted(dve, rsum_ready, n + 1)
                    counted(dve, av_copied, n + 1)
                    dve.wait_ge(stored[g % 2], (b * (NP // 2) + g // 2) * 16)
                    nc.vector.tensor_tensor(out[:, g % 2], av[:], rsum[:], ALU.mult).then_inc(out_ready, 1)

                units(dve, NP, ahead, step)

            @block.tensor
            def _(pe):
                prime(pe, kp_ready, vp_ready, max_ready, shift_ready, s_ready, probs_used, sum_ready)
                pe.wait_ge(w_ready, 32)

                def k_chunk(u, i):
                    b, p, g, n = u
                    k0, w = KCH[i]
                    if i == 0:
                        pe.wait_ge(loaded[p], half(b, p) * 32 + 32)
                    counted(pe, kb_ready, n * NC + i - 1)
                    nc.tensor.matmul(k_ps[i % 2][:, 0:w], wk[:, g], cm[:, p, k0:k0 + w], start=True, stop=True).then_inc(kp_ready, 1)

                def v_tile(hb, t, before):
                    b, p, h = hb
                    w = width(t)
                    n = (b * 2 + h) * KT + t
                    pe.wait_ge(loaded[p], half(b, p) * 32 + 32)
                    counted(pe, rsum_ready, before)
                    counted(pe, v_ready, n)
                    nc.tensor.matmul(misc_ps[0:w, :], ct[:, p, t * P:t * P + w], wv[:, h], start=True, stop=True).then_inc(vp_ready, 1)

                def maxima(u, m):
                    b, p, g, n = u
                    if m == 0:
                        counted(pe, kb_ready, (n + 1) * NC)
                        counted(pe, q_ready, n + 1)
                    for i, (k0, w) in enumerate(KCH):
                        counted(pe, maxed, n * NM + m * NC + i - 1)
                        nc.tensor.matmul(max_ps[i % 2][:, 0:w], qa[:, g % 2, m // 2, m % 2 * P:m % 2 * P + P],
                                         ka[:, g % 2, m // 2, k0:k0 + w], start=True, stop=True).then_inc(max_ready, 1)

                def shift(u):
                    b, p, g, n = u
                    counted(pe, diag_ready, n + 1)
                    nc.tensor.matmul(misc_ps[:], c["ones_r"][:], diag[:], start=True, stop=True).then_inc(shift_ready, 1)

                def scores(u, t):
                    b, p, g, n = u
                    w = width(t)
                    counted(pe, probs_ready, n * KT + t - (t > 0))
                    for h in range(2):
                        o = s_ps[t % 2][0:w, h * S:(h + 1) * S]
                        nc.tensor.matmul(o, ka[:, g % 2, h, t * P:t * P + w], qa[:, g % 2, h], start=True, stop=False)
                        last = nc.tensor.matmul(o, kb[:, g % 2, h, t * P:t * P + w], qb[:, g % 2, h], start=False, stop=True)
                    last.then_inc(s_ready, 1)

                def values(u, t):
                    b, p, g, n = u
                    w = width(t)
                    counted(pe, probs_ready, n * KT + t + 1)
                    if t == 0:
                        counted(pe, v_ready, (b * 2 + g // 4 + 1) * KT)
                        counted(pe, av_copied, n)
                    for h in range(2):
                        d0 = g % 4 * P + h * XHD
                        last = nc.tensor.matmul(av_ps[h * XHD:(h + 1) * XHD, 0:S], v[0:w, g // 4, t, d0:d0 + XHD],
                                                probs[0:w, t % NPB, h], start=(t == 0), stop=(t == KT - 1))
                    last.then_inc(probs_used, 1)

                def ahead(u):
                    for i in range(NC):
                        k_chunk(u, i)
                    for t in range(KT):
                        v_tile((0, 0, 0), t, 0)
                    for m in range(4):
                        maxima(u, m)
                    counted(pe, v_ready, KT)
                    shift(u)

                def step(u, nxt):
                    b, p, g, n = u
                    share = list(v_share(g)) if next_half(u) else []
                    counted(pe, shifted, n + 1)
                    scores(u, 0)
                    for t in range(KT):
                        if t + 1 < KT:
                            scores(u, t + 1)
                        if nxt and t < NC:
                            k_chunk(nxt, t)
                        elif NC <= t < NC + len(share):
                            v_tile(next_half(u), share[t - NC], n)
                        if nxt and t >= KT - 6 and t < KT - 2:
                            maxima(nxt, t - (KT - 6))
                        values(u, t)
                    if nxt:
                        if not share:
                            counted(pe, rsum_ready, n)
                        else:
                            hb = next_half(u)
                            counted(pe, v_ready, (hb[0] * 2 + hb[2]) * KT + share[-1] + 1)
                        shift(nxt)
                        counted(pe, shifted, n + 2)
                    else:
                        counted(pe, rsum_ready, n)
                    counted(pe, added, (n + 1) * (KT - 1))
                    for h in range(2):
                        last = nc.tensor.matmul(misc_ps[h * XHD:(h + 1) * XHD, 0:S], c["ones"][:, 0:XHD], acc[:, h],
                                                start=True, stop=True)
                    last.then_inc(sum_ready, 1)

                units(pe, NP, ahead, step)


def feed_forward(nc, src, c, name, x_d, normed_d, w_in, w_out, out_d, silu, gate=None, w_proj=None, proj_d=None):
    NE = 2 if silu else 1
    kh = w_out[0].shape[1]
    with Phase(nc, name) as ph:
        x, xn = ph.sb("x", [P, 2, DC, S]), ph.sb("xn", [P, 2, DC, S])
        xe = ph.sb("xe", [P, 2, 2, DC, S]) if silu else None
        wi = [ph.sb(f"wi{k}", [P, DC, kh * P]) for k in range(len(w_in))]
        wo = ph.sb("wo", [P, NE * kh, D])
        act_g = ph.sb("act_g", [P, 2, S])
        hid = ph.sb("hid", [P, 2, NE * kh, S])
        out = ph.sb("out", [P, 2, DC, S])
        wp = ph.sb("wp", [P, DC, C]) if proj_d is not None else None
        pr = ph.sb("pr", [P, 2, S])
        in_ps, out_ps, pr_ps = ph.banks("in", 4), ph.banks("out", 2), ph.banks("pr", 1)
        loaded, stored, pr_stored, w_ready = ph.sems2("loaded"), ph.sems2("stored"), ph.sems2("pr_stored"), ph.sem("w_ready")
        xe_ready, in_ready, act_ready, hid_ready, down_ready, out_ready, pr_ready, pr_copied = (
            ph.sem(n) for n in ("xe_ready", "in_ready", "act_ready", "hid_ready", "down_ready", "out_ready", "pr_ready", "pr_copied"))
        NB_ = NE * kh if silu else kh // 2
        n_weights = len(w_in) + NE + (proj_d is not None)

        with nc.Block() as block:
            @block.sync
            def _(sp):
                for k, w in enumerate(w_in):
                    sp.dma_start(wi[k][:], w).then_inc(w_ready, 16)
                for e, w in enumerate(w_out):
                    sp.dma_start(wo[:, e * kh:(e + 1) * kh], w).then_inc(w_ready, 16)
                if proj_d is not None:
                    sp.dma_start(wp[:], w_proj).then_inc(w_ready, 16)

                def load(u):
                    b, p, _, _ = u
                    counted(sp, out_ready, b - 1)
                    sp.dma_start(x[:, p], x_d[b]).then_inc(loaded[p], 16)
                    sp.dma_start(xn[:, p], normed_d[b]).then_inc(loaded[p], 16)

                def step(u, nxt):
                    if nxt:
                        load(nxt)
                    b, p, _, _ = u
                    counted(sp, out_ready, b + 1)
                    sp.dma_start(out_d[b], out[:, p]).then_inc(stored[p], 16)
                    if proj_d is not None:
                        counted(sp, pr_copied, b + 1)
                        sp.dma_start(proj_d[b], pr[:, p]).then_inc(pr_stored[p], 16)

                units(sp, 1, load, step)
                for p in range(2):
                    sp.wait_ge(stored[p], B // 2 * 16)
                    if proj_d is not None:
                        sp.wait_ge(pr_stored[p], B // 2 * 16)

            @block.scalar
            def _(act):
                prime(act, act_ready, pr_copied)
                if not silu:
                    prime(act, hid_ready)

                def hidden(u):
                    b, p, _, _ = u
                    for m in range(NB_):
                        n = b * NB_ + m
                        counted(act, in_ready, n + 1)
                        if silu:
                            counted(act, hid_ready, n - 1)
                            nc.scalar.activation(act_g[:, m % 2], in_ps[m % 4][:, 0:S], ACT.Silu).then_inc(act_ready, 1)
                        else:
                            if m == 0:
                                counted(act, down_ready, b - 1)
                            nc.scalar.activation(hid[:, p, 2 * m:2 * m + 2], in_ps[m % 4][:].rearrange("p (m s) -> p m s", m=2),
                                                 ACT.Gelu).then_inc(hid_ready, 1)

                def step(u, nxt):
                    b, p, _, _ = u
                    if nxt:
                        hidden(nxt)
                    if proj_d is not None:
                        counted(act, pr_ready, b + 1)
                        act.wait_ge(pr_stored[p], half(b, p) * 16)
                        nc.scalar.activation(pr[:, p], pr_ps[0][:, 0:S], ACT.Copy).then_inc(pr_copied, 1)

                units(act, 1, hidden, step)

            @block.vector
            def _(dve):
                prime(dve, xe_ready, out_ready)
                if silu:
                    prime(dve, hid_ready)

                def hidden(u):
                    b, p, _, _ = u
                    if not silu:
                        return
                    dve.wait_ge(loaded[p], half(b, p) * 32 + 32)
                    counted(dve, in_ready, (b - 1) * NB_)
                    for k in range(DC):
                        last = nc.vector.tensor_tensor(xe[:, p, 0, k], xn[:, p, k], c["vm"][:, b, :], ALU.mult)
                    last.then_inc(xe_ready, 1)
                    counted(dve, xe_ready, b * 2 + 1)
                    nc.vector.tensor_tensor(xe[:, p, 1], xn[:, p], xe[:, p, 0], ALU.subtract).then_inc(xe_ready, 1)
                    for m in range(NB_):
                        counted(dve, act_ready, b * NB_ + m + 1)
                        if m == 0:
                            counted(dve, down_ready, b - 1)
                        nc.vector.tensor_tensor(hid[:, p, m], in_ps[m % 4][:, S:2 * S], act_g[:, m % 2], ALU.mult
                                                ).then_inc(hid_ready, 1)

                def step(u, nxt):
                    b, p, _, _ = u
                    if nxt:
                        hidden(nxt)
                    dve.wait_ge(loaded[p], half(b, p) * 32 + 32)
                    dve.wait_ge(stored[p], half(b, p) * 16)
                    counted(dve, pr_ready, b - 1) if proj_d is not None else None
                    counted(dve, down_ready, b + 1)
                    src_ = out_ps[p][:].rearrange("p (m s) -> p m s", m=DC)
                    if gate is not None:
                        nc.vector.scalar_tensor_tensor(out[:, p], src_, gate, x[:, p], ALU.mult, ALU.add).then_inc(out_ready, 1)
                    else:
                        nc.vector.tensor_tensor(out[:, p], src_, x[:, p], ALU.add).then_inc(out_ready, 1)

                units(dve, 1, hidden, step)

            @block.tensor
            def _(pe):
                prime(pe, in_ready, down_ready, pr_ready)
                pe.wait_ge(w_ready, n_weights * 16)

                def hidden(u):
                    b, p, _, _ = u
                    if silu:
                        counted(pe, xe_ready, b * 2 + 2)
                    else:
                        pe.wait_ge(loaded[p], half(b, p) * 32 + 32)
                    for m in range(NB_):
                        counted(pe, hid_ready, b * NB_ + (m - 3 if m >= 4 or NB_ % 4 == 0 else 0))
                        e, t = divmod(m, kh)
                        for h in range(2):
                            w = wi[2 * e + h] if silu else wi[0]
                            mt = t if silu else 2 * m + h
                            for k in range(DC):
                                rhs = xe[:, p, e, k] if silu else xn[:, p, k]
                                last = nc.tensor.matmul(in_ps[m % 4][:, h * S:(h + 1) * S], w[:, k, mt * P:(mt + 1) * P], rhs,
                                                        start=(k == 0), stop=(k == DC - 1))
                        last.then_inc(in_ready, 1)

                def step(u, nxt):
                    b, p, _, _ = u
                    if nxt:
                        hidden(nxt)
                    counted(pe, hid_ready, (b + 1) * NB_)
                    counted(pe, out_ready, b - 1)
                    for m in range(DC):
                        for k in range(NE * kh):
                            last = nc.tensor.matmul(out_ps[p][:, m * S:(m + 1) * S], wo[:, k, m * P:(m + 1) * P], hid[:, p, k],
                                                    start=(k == 0), stop=(k == NE * kh - 1))
                    last.then_inc(down_ready, 1)
                    if proj_d is not None:
                        counted(pe, out_ready, b + 1)
                        counted(pe, pr_copied, b)
                        for k in range(DC):
                            last = nc.tensor.matmul(pr_ps[0][:, 0:S], wp[:, k], out[:, p, k], start=(k == 0), stop=(k == DC - 1))
                        last.then_inc(pr_ready, 1)

                units(pe, 1, hidden, step)


def memory_attention(nc, src, c, name, q_d, out_d):
    with Phase(nc, name) as ph:
        ct, cn = ph.sb("ct", [P, 2, NKP]), ph.sb("cn", [P, 2, KT, C])
        q = ph.sb("q", [P, 2, S])
        ct_r, q_r = ph.sb("ct_r", [P, 2, NKP], F32R), ph.sb("q_r", [P, 2, S], F32R)
        partmax, negmax = ph.sb("partmax", [P, 2, len(KCH)]), ph.sb("negmax", [P, 2])
        diag = ph.sb("diag", [P, 2, S], F32R)
        probs, acc = ph.sb("probs", [P, 2, 4, S]), ph.sb("acc", [P, 4, S])
        av, rsum, out = ph.sb("av", [P, S]), ph.sb("rsum", [P, S]), ph.sb("out", [P, 2, S])
        max_ps, s_ps = ph.banks("max", 2), ph.banks("s", 2, 1024)
        av_ps, sum_ps = ph.banks("av", 1)[0], ph.banks("sum", 1)[0]
        loaded, stored = ph.sems2("loaded"), ph.sems2("stored")
        rounded, max_ready, maxed, negmax_ready, diag_ready = (
            ph.sem(n) for n in ("rounded", "max_ready", "maxed", "negmax_ready", "diag_ready"))
        s_ready, probs_ready, probs_used, added, av_copied, sum_ready, rsum_ready, out_ready = (
            ph.sem(n) for n in ("s_ready", "probs_ready", "probs_used", "added", "av_copied", "sum_ready", "rsum_ready", "out_ready"))
        NC = len(KCH)
        NM = 2 * NC
        quads = [range(t, min(t + 4, KT)) for t in range(0, KT, 4)]
        NQ = len(quads)

        with nc.Block() as block:
            @block.sync
            def _(sp):
                def load(u):
                    b, p, _, _ = u
                    counted(sp, probs_used, (b - 1) * NQ)
                    sp.dma_start(ct[:, p], src["ctx_t"][b]).then_inc(loaded[p], 16)
                    sp.dma_start(cn[:, p], src["ctx_n"][b]).then_inc(loaded[p], 16)
                    sp.dma_start(q[:, p], q_d[b]).then_inc(loaded[p], 16)

                def step(u, nxt):
                    b, p, _, _ = u
                    if nxt:
                        load(nxt)
                    counted(sp, out_ready, b + 1)
                    sp.dma_start(out_d[b], out[:, p]).then_inc(stored[p], 16)

                units(sp, 1, load, step)
                for s in stored:
                    sp.wait_ge(s, 16 * B // 2)

            @block.gpsimd
            def _(pool):
                prime(pool, added)

                def step(u, nxt):
                    b, p, _, _ = u
                    for i in range(1, NQ):
                        counted(pool, probs_ready, b * NQ + i + 1)
                        if i == 1:
                            counted(pool, sum_ready, b)
                        else:
                            counted(pool, added, b * (NQ - 1) + i - 1)
                        if i < NQ - 1:
                            nc.gpsimd.tensor_tensor(acc[:], probs[:, 0] if i == 1 else acc[:], probs[:, i % 2], ALU.add
                                                    ).then_inc(added, 1)
                        else:
                            nc.gpsimd.tensor_tensor(acc[0:KLAST, 0], acc[0:KLAST, 0], probs[0:KLAST, i % 2, 0], ALU.add
                                                    ).then_inc(added, 1)

                units(pool, 1, lambda u: None, step)

            @block.scalar
            def _(act):
                act.preload_act_table_set(EXP_LN)
                prime(act, rounded, probs_ready, av_copied)

                def ahead(u):
                    b, p, _, _ = u
                    act.wait_ge(loaded[p], half(b, p) * 48 + 48)
                    counted(act, max_ready, (b - 1) * NM)
                    nc.scalar.activation(q_r[:, p], q[:, p], ACT.Copy)
                    nc.scalar.activation(ct_r[:, p], ct[:, p], ACT.Copy).then_inc(rounded, 1)

                def step(u, nxt):
                    b, p, _, _ = u
                    if nxt:
                        ahead(nxt)
                    for i, tiles in enumerate(quads):
                        n = b * NQ + i
                        counted(act, s_ready, n + 1)
                        counted(act, probs_used, b * NQ + max(i - 1, 0))
                        counted(act, added, b * (NQ - 1) + (max(i - 2, 1) if i >= 2 else 0))
                        w, m = width(tiles[-1]), len(tiles)
                        nc.scalar.activation(probs[0:w, i % 2, 0:m], s_ps[i % 2][0:w, 0:m * S].rearrange("p (t s) -> p t s", t=m),
                                             ACT.Exp, scale=D ** -0.5).then_inc(probs_ready, 1)
                    counted(act, probs_used, (b + 1) * NQ)
                    counted(act, out_ready, b)
                    nc.scalar.activation(av[:], av_ps[:, 0:S], ACT.Copy).then_inc(av_copied, 1)

                units(act, 1, ahead, step)

            @block.vector
            def _(dve):
                prime(dve, maxed, negmax_ready, diag_ready, rsum_ready, out_ready)

                def ahead(u):
                    b, p, _, _ = u
                    counted(dve, negmax_ready, b)
                    for m in range(NM):
                        w = KCH[m % NC][1]
                        counted(dve, max_ready, b * NM + m + 1)
                        nc.vector.tensor_reduce(partmax[:, m // NC, m % NC:m % NC + 1], max_ps[m % 2][:, 0:w], AX.X, ALU.max
                                                ).then_inc(maxed, 1)
                    counted(dve, maxed, (b + 1) * NM)
                    counted(dve, diag_ready, b)
                    nc.vector.tensor_reduce(negmax[:], partmax[:], AX.X, ALU.max, negate=True).then_inc(negmax_ready, 1)
                    counted(dve, negmax_ready, b + 1)
                    counted(dve, s_ready, (b - 1) * NQ)
                    for m in range(2):
                        last = nc.vector.tensor_scalar(diag[:, p, m * P:(m + 1) * P], c["ident"][:], negmax[:, m:m + 1], None,
                                                       ALU.mult)
                    last.then_inc(diag_ready, 1)

                def step(u, nxt):
                    b, p, _, _ = u
                    if nxt:
                        ahead(nxt)
                    counted(dve, sum_ready, b + 1)
                    counted(dve, out_ready, b)
                    nc.vector.reciprocal(rsum[:], sum_ps[:, 0:S]).then_inc(rsum_ready, 1)
                    counted(dve, rsum_ready, b + 1)
                    counted(dve, av_copied, b + 1)
                    dve.wait_ge(stored[p], half(b, p) * 16)
                    nc.vector.tensor_tensor(out[:, p], av[:], rsum[:], ALU.mult).then_inc(out_ready, 1)

                units(dve, 1, ahead, step)

            @block.tensor
            def _(pe):
                prime(pe, max_ready, s_ready, probs_used, sum_ready)

                def maxima(u, m):
                    b, p, _, _ = u
                    counted(pe, rounded, b + 1)
                    for i, (k0, w) in enumerate(KCH):
                        counted(pe, maxed, b * NM + m * NC + i - 1)
                        nc.tensor.matmul(max_ps[i % 2][:, 0:w], q_r[:, p, m * P:(m + 1) * P], ct_r[:, p, k0:k0 + w],
                                         start=True, stop=True).then_inc(max_ready, 1)

                def scores(u, i):
                    b, p, _, _ = u
                    counted(pe, probs_ready, b * NQ + i - (i > 0))
                    for k, t in enumerate(quads[i]):
                        w = width(t)
                        o = s_ps[i % 2][0:w, k * S:(k + 1) * S]
                        nc.tensor.matmul(o, ct[:, p, t * P:t * P + w], q[:, p], start=True, stop=False)
                        last = nc.tensor.matmul(o, c["ones_r"][:, 0:w], diag[:, p], start=False, stop=True)
                    last.then_inc(s_ready, 1)

                def values(u, i):
                    b, p, _, _ = u
                    counted(pe, probs_ready, b * NQ + i + 1)
                    if i == 0:
                        counted(pe, av_copied, b)
                    for k, t in enumerate(quads[i]):
                        w = width(t)
                        last = nc.tensor.matmul(av_ps[:, 0:S], cn[0:w, p, t], probs[0:w, i % 2, k], start=(t == 0), stop=(t == KT - 1))
                    last.then_inc(probs_used, 1)

                def ahead(u):
                    for m in range(2):
                        maxima(u, m)

                def step(u, nxt):
                    b, p, _, _ = u
                    counted(pe, diag_ready, b + 1)
                    pe.wait_ge(loaded[p], half(b, p) * 48 + 48)
                    scores(u, 0)
                    for i in range(NQ):
                        if i + 1 < NQ:
                            scores(u, i + 1)
                        if nxt and i < 2:
                            maxima(nxt, i)
                        values(u, i)
                    counted(pe, added, (b + 1) * (NQ - 1))
                    counted(pe, rsum_ready, b)
                    for k in range(4):
                        last = nc.tensor.matmul(sum_ps[:, 0:S], c["ones"][:], acc[:, k], start=(k == 0), stop=(k == 3))
                    last.then_inc(sum_ready, 1)

                units(pe, 1, ahead, step)


def gated_memory(nc, src, c, name, layer, x_d, mem_d, out_d, w_proj=None, proj_d=None):
    with Phase(nc, name) as ph:
        x, mem = ph.sb("x", [P, 2, DC, S]), ph.sb("mem", [P, 2, S])
        wm, wg = ph.sb("wm", [P, D]), ph.sb("wg", [P, 2 * DC, D])
        wp = ph.sb("wp", [P, DC, C])
        neg_b = ph.sb("neg_b", [P, DC])
        mc, e = ph.sb("mc", [P, 2, DC, S]), ph.sb("e", [P, DC, S])
        e1, g, gm = ph.sb("e1", [P, DC, S]), ph.sb("g", [P, DC, S]), ph.sb("gm", [P, DC, S])
        f, sq, ln, rs = ph.sb("f", [P, DC, S]), ph.sb("sq", [P, DC, S]), ph.sb("ln", [P, S]), ph.sb("rs", [P, S])
        out, pr = ph.sb("out", [P, 2, DC, S]), ph.sb("pr", [P, 2, S])
        mc_ps, g_ps, var_ps, pr_ps = ph.banks("mc", 2), ph.banks("g", 2), ph.banks("var", 1), ph.banks("pr", 1)
        loaded, stored, pr_stored, w_ready = ph.sems2("loaded"), ph.sems2("stored"), ph.sems2("pr_stored"), ph.sem("w_ready")
        b_ready, mcp_ready, mc_ready, gp_ready, e_ready, steps, f_ready = (
            ph.sem(n) for n in ("b_ready", "mcp_ready", "mc_ready", "gp_ready", "e_ready", "steps", "f_ready"))
        sq_ready, var_ready, ln_ready, rs_ready, out_ready, pr_ready, pr_copied = (
            ph.sem(n) for n in ("sq_ready", "var_ready", "ln_ready", "rs_ready", "out_ready", "pr_ready", "pr_copied"))
        project = proj_d is not None
        with nc.Block() as block:
            @block.sync
            def _(sp):
                sp.dma_start(wm[:], src[layer + "_mem_t"]).then_inc(w_ready, 16)
                sp.dma_start(wg[:], src[layer + "_gate"]).then_inc(w_ready, 16)
                if project:
                    sp.dma_start(wp[:], w_proj).then_inc(w_ready, 16)

                def load(u):
                    b, p, _, _ = u
                    counted(sp, out_ready, b - 1)
                    sp.dma_start(x[:, p], x_d[b]).then_inc(loaded[p], 16)
                    sp.dma_start(mem[:, p], mem_d[b]).then_inc(loaded[p], 16)

                def step(u, nxt):
                    if nxt:
                        load(nxt)
                    b, p, _, _ = u
                    counted(sp, out_ready, b + 1)
                    sp.dma_start(out_d[b], out[:, p]).then_inc(stored[p], 16)
                    if project:
                        counted(sp, pr_copied, b + 1)
                        sp.dma_start(proj_d[b], pr[:, p]).then_inc(pr_stored[p], 16)

                units(sp, 1, load, step)
                for p in range(2):
                    sp.wait_ge(stored[p], B // 2 * 16)
                    if project:
                        sp.wait_ge(pr_stored[p], B // 2 * 16)

            @block.scalar
            def _(act):
                act.preload_act_table_set(EXP_LN)
                prime(act, mc_ready, e_ready, sq_ready, ln_ready, rs_ready, pr_copied)
                act.wait_ge(b_ready, 1)

                def ahead(u):
                    b, p, _, _ = u
                    counted(act, mcp_ready, b + 1)
                    counted(act, gp_ready, b - 1)
                    counted(act, f_ready, b - 1)
                    nc.scalar.activation(mc[:, p], mc_ps[p][:].rearrange("p (m s) -> p m s", m=DC), ACT.Copy).then_inc(mc_ready, 1)

                def step(u, nxt):
                    b, p, _, _ = u
                    counted(act, gp_ready, b + 1)
                    counted(act, f_ready, b)
                    for m in range(DC):
                        last = nc.scalar.activation(e[:, m], g_ps[p][:, m * S:(m + 1) * S], ACT.Exp, scale=-1.0,
                                                    bias=neg_b[:, m:m + 1])
                    last.then_inc(e_ready, 1)
                    if nxt:
                        ahead(nxt)
                    counted(act, f_ready, b + 1)
                    counted(act, var_ready, b)
                    nc.scalar.activation(sq[:], f[:], ACT.Square).then_inc(sq_ready, 1)
                    counted(act, var_ready, b + 1)
                    nc.scalar.activation(ln[:], var_ps[0][:, 0:S], ACT.Ln, bias=c["eps6"][:, 0:1]).then_inc(ln_ready, 1)
                    counted(act, ln_ready, b + 1)
                    counted(act, out_ready, b)
                    nc.scalar.activation(rs[:], ln[:], ACT.Exp, scale=-0.5).then_inc(rs_ready, 1)
                    if project:
                        counted(act, pr_ready, b + 1)
                        act.wait_ge(pr_stored[p], half(b, p) * 16)
                        nc.scalar.activation(pr[:, p], pr_ps[0][:, 0:S], ACT.Copy).then_inc(pr_copied, 1)

                units(act, 1, ahead, step)

            @block.vector
            def _(dve):
                prime(dve, f_ready, out_ready)
                nc.vector.tensor_scalar(neg_b[:], c[layer + "_bgate"][:], -1.0, None, ALU.mult).then_inc(b_ready, 1)

                def step(u, nxt):
                    b, p, _, _ = u
                    ch = Chain(dve, steps, b * 3)
                    counted(dve, e_ready, b + 1)
                    ch.link(nc.vector.tensor_scalar(e1[:], e[:], BIG, 1.0, ALU.min, ALU.add))
                    ch.link(nc.vector.reciprocal(g[:], e1[:]))
                    counted(dve, mc_ready, b + 1)
                    ch.link(nc.vector.tensor_tensor(gm[:], g[:], mc[:, p], ALU.mult))
                    dve.wait_ge(loaded[p], half(b, p) * 32 + 32)
                    counted(dve, sq_ready, b)
                    nc.vector.tensor_tensor(f[:], gm[:], x[:, p], ALU.add).then_inc(f_ready, 1)
                    counted(dve, f_ready, b + 1)
                    counted(dve, rs_ready, b + 1)
                    dve.wait_ge(stored[p], half(b, p) * 16)
                    if project:
                        counted(dve, pr_ready, b - 1)
                    for k in range(DC):
                        last = nc.vector.scalar_tensor_tensor(out[:, p, k], f[:, k], c[layer + "_norm"][:, k:k + 1], rs[:],
                                                              ALU.mult, ALU.mult)
                    last.then_inc(out_ready, 1)

                units(dve, 1, lambda u: None, step)

            @block.tensor
            def _(pe):
                prime(pe, mcp_ready, gp_ready, var_ready, pr_ready)
                pe.wait_ge(w_ready, (2 + project) * 16)

                def ahead(u):
                    b, p, _, _ = u
                    pe.wait_ge(loaded[p], half(b, p) * 32 + 32)
                    counted(pe, mc_ready, b - 1)
                    for m in range(DC):
                        last = nc.tensor.matmul(mc_ps[p][:, m * S:(m + 1) * S], wm[:, m * P:(m + 1) * P], mem[:, p],
                                                start=True, stop=True)
                    last.then_inc(mcp_ready, 1)
                    counted(pe, mc_ready, b + 1)
                    counted(pe, e_ready, b - 1)
                    for m in range(DC):
                        for k in range(2 * DC):
                            rhs = x[:, p, k] if k < DC else mc[:, p, k - DC]
                            last = nc.tensor.matmul(g_ps[p][:, m * S:(m + 1) * S], wg[:, k, m * P:(m + 1) * P], rhs,
                                                    start=(k == 0), stop=(k == 2 * DC - 1))
                    last.then_inc(gp_ready, 1)

                def step(u, nxt):
                    b, p, _, _ = u
                    if nxt:
                        ahead(nxt)
                    counted(pe, sq_ready, b + 1)
                    counted(pe, ln_ready, b)
                    for k in range(DC):
                        last = nc.tensor.matmul(var_ps[0][:, 0:S], c["mean"][:], sq[:, k], start=(k == 0), stop=(k == DC - 1))
                    last.then_inc(var_ready, 1)
                    if project:
                        counted(pe, out_ready, b + 1)
                        counted(pe, pr_copied, b)
                        for k in range(DC):
                            last = nc.tensor.matmul(pr_ps[0][:, 0:S], wp[:, k], out[:, p, k], start=(k == 0), stop=(k == DC - 1))
                        last.then_inc(pr_ready, 1)

                units(pe, 1, ahead, step)


def build(nc, src, out):
    def scratch(name, shape, dt=F32):
        return nc.dram_tensor("d_" + name, shape, dt, kind="Internal").ap()

    with ExitStack() as ctx:
        def keep(name, shape, dt=F32):
            return ctx.enter_context(nc.sbuf_tensor("c_" + name, shape, dt))

        c = {"ident": keep("ident", [P, P]), "ones": keep("ones", [P, P]), "rot": keep("rot", [P, P]),
             "headmask": keep("headmask", [P, P // SHD]), "causal_t": keep("causal_t", [P, 2, S]),
             "sum16": keep("sum16", [P, P]), "sum8": keep("sum8", [P, P]), "low": keep("low", [P, 5])}
        c["loads"] = {k: src["c_" + k] for k in c}
        vectors = {"ln_in_w": DC, "ln_post_attn_w": DC, "ln_post_cross_w": DC, "ln_q_g": DC, "ln_q_b": DC,
                   "ln_ff_g": DC, "ln_ff_b": DC, "L2_bgate": DC, "L2_norm": DC, "L3_bgate": DC, "L3_norm": DC}
        for k, n in vectors.items():
            c[k] = keep(k, [P, n])
            c["loads"][k] = src[k]
        for k in ("attn_gate", "ff_gate"):
            c[k] = keep(k, [P, 1])
            c["loads"][k] = src[k][0].partition_broadcast(P)
        for k, shape, dt in (("mean", [P, P], F32), ("cos", [P, S], F32), ("sin", [P, S], F32), ("vm", [P, B, S], F32),
                             ("ident_b", [P, P], BF16), ("ones_r", [P, P], F32R), ("sel_r", [P, 4, P], F32R),
                             ("causal", [P, 2, S], BF16), ("causal_tb", [P, 2, S], BF16), ("key_bias", [P, B, KT], F32),
                             ("eps6", [P, 1], F32), ("eps5", [P, 1], F32), ("tanh_gate", [P, 2], F32)):
            c[k] = keep(k, shape, dt)
        load_constants(nc, src, c)
        masked_d = scratch("masked_ctx", [B, P, NKP])
        mask_context(nc, src, c, masked_d)
        q_d, k_d = (scratch(n, [B, P, 2, S]) for n in ("self_q", "self_k"))
        v_d = scratch("self_v", [B, P, 2, NH, 32])
        self_projections(nc, src, c, q_d, k_d, v_d)
        self_d = scratch("self_out", [B, P, NG, S])
        self_attention(nc, c, q_d, k_d, v_d, self_d)
        x1_d = scratch("x1", [B, P, DC, S])
        cross = scratch("cross", [B, P, 2, NG, S])
        cq_d, cross_d = cross[:, :, 0], cross[:, :, 1]
        residual_norm(nc, c, "selfout", src["x_t"], "rms", c["ln_post_cross_w"], attn_d=self_d,
                      w_attn=(src["v_dense"], src["l_dense"]), experts=True, x_out_d=x1_d,
                      w_proj=src["cq_stack"], proj_d=cq_d, split=True)
        cross_attention_0(nc, src, c, cq_d, cross_d)
        x2_d, n2_d, x3_d = (scratch(n, [B, P, DC, S]) for n in ("x2", "n2", "x3"))
        residual_norm(nc, c, "crossout", x1_d, "rms", c["ln_post_attn_w"], attn_d=cross_d, w_attn=(src["cdense"],),
                      x_out_d=x2_d, normed_d=n2_d)
        feed_forward(nc, src, c, "ffn0", x2_d, n2_d, [src[k] for k in ("v_gate", "v_up", "l_gate", "l_up")],
                     [src["v_down"], src["l_down"]], x3_d, silu=True)
        cross1 = scratch("cross1", [B, P, 2, NP, S])
        q1_d, out1_d = cross1[:, :, 0], cross1[:, :, 1]
        residual_norm(nc, c, "query1", x3_d, "layer", c["ln_q_g"], c["ln_q_b"], w_proj=src["Wq"], proj_d=q1_d)
        cross_attention_1(nc, src, c, masked_d, q1_d, out1_d)
        x4_d, n4_d, x5_d, x6_d = (scratch(n, [B, P, DC, S]) for n in ("x4", "n4", "x5", "x6"))
        q2_d, q3_d, m2_d, m3_d = (scratch(n, [B, P, S]) for n in ("q2", "q3", "m2", "m3"))
        residual_norm(nc, c, "out1", x3_d, "layer", c["ln_ff_g"], c["ln_ff_b"], attn_d=out1_d, w_attn=(src["Wo"],),
                      gate=c["tanh_gate"][:, 0:1], x_out_d=x4_d, normed_d=n4_d)
        feed_forward(nc, src, c, "ffn1", x4_d, n4_d, [src["W1"]], [src["W2"]], x5_d, silu=False,
                     gate=c["tanh_gate"][:, 1:2], w_proj=src["L2_mem"], proj_d=q2_d)
        memory_attention(nc, src, c, "mem2", q2_d, m2_d)
        gated_memory(nc, src, c, "gated2", "L2", x5_d, m2_d, x6_d, w_proj=src["L3_mem"], proj_d=q3_d)
        memory_attention(nc, src, c, "mem3", q3_d, m3_d)
        gated_memory(nc, src, c, "gated3", "L3", x6_d, m3_d, out)


def _inputs(inputs):
    n = {k: np.asarray(v) for k, v in inputs.items()}
    f32 = np.float32
    x, ctx = n["x"], n["ctx_1024"]
    mask = n["mask_BxS2_bk0"].view(np.uint8)

    def rows(w):
        return np.ascontiguousarray(w.reshape(-1, P, w.shape[-1]).transpose(1, 0, 2))

    def cols(w):
        return np.ascontiguousarray(w.reshape(-1, P).T)

    a = {
        "x_t": x.reshape(B, S, DC, P).transpose(0, 3, 2, 1),
        "ctx_t": np.concatenate([ctx, ctx[:, NK - 1:NK]], axis=1)[:, :NKP].transpose(0, 2, 1),
        "ctx_n": np.concatenate([ctx, np.zeros((B, KT * P - NK, C), f32)], axis=1).reshape(B, KT, P, C).transpose(0, 2, 1, 3),
        "tok_mask": n["mask_BxS_ik0"], "pos": n["pos_1xS"],
        "key_mask": np.concatenate([mask, mask[:, NK - 1:NK], np.zeros((B, 4 * MW - NK - 1), np.uint8)], axis=1).view(np.int32),
        "key_mask_t": np.ascontiguousarray(np.concatenate([mask, np.zeros((B, KT * P - NK), np.uint8)], axis=1).reshape(
            B, KT, P).transpose(2, 0, 1)).reshape(P, B * KT).view(np.int32),
        "ln_in_w": cols(n["L0_xattn_ln_in_w"]), "ln_post_attn_w": cols(n["L0_xattn_ln_post_attn_w"]),
        "ln_post_cross_w": cols(n["L0_xattn_ln_post_cross_w"]),
        "v_qkv": rows(n["L0_xattn_v_qkv"]), "l_qkv": rows(n["L0_xattn_l_qkv"]),
    }
    def spread(w, width):
        out = np.zeros((NG, 4, 32, w.shape[1]), f32)
        out[:, :, :width] = w.reshape(NG, 4, width, w.shape[1])
        return rows(out.reshape(NG * P, -1))

    a["v_dense"], a["l_dense"] = spread(n["L0_xattn_v_dense"], SHD), spread(n["L0_xattn_l_dense"], SHD)
    a["cdense"] = spread(n["L0_xattn_cdense_w"], CHD)

    def stacked(w):
        out = np.zeros((w.shape[0], NH, 4, CHD), f32)
        out[:, :, 1:] = w.reshape(w.shape[0], NH, 1, CHD)
        return out.reshape(w.shape[0], NH * 32)

    a["cq_stack"] = rows(stacked(n["L0_xattn_cq_w"]))
    a["ck_stack"] = stacked(n["L0_xattn_ckv_w"][:, :C])
    a["cv"] = n["L0_xattn_ckv_w"][:, C:]
    for k in ("v_gate", "v_up", "l_gate", "l_up"):
        w = n["L0_xattn_" + k]
        a[k] = rows(np.concatenate([w, np.zeros((D, -FF0 % P), f32)], axis=1))
    for k in ("v_down", "l_down"):
        w = n["L0_xattn_" + k]
        a[k] = rows(np.concatenate([w, np.zeros((-FF0 % P, D), f32)]))
    for k in ("ln_q_g", "ln_q_b", "ln_ff_g", "ln_ff_b"):
        a[k] = cols(n["L1_xattn_" + k])
    a["attn_gate"], a["ff_gate"] = n["L1_xattn_attn_gate"].reshape(1, 1), n["L1_xattn_ff_gate"].reshape(1, 1)
    a["Wq"], a["W1"], a["W2"], a["Wo"] = (rows(n["L1_xattn_" + k]) for k in ("Wq", "W1", "W2", "Wo"))
    a["Wkv"] = n["L1_xattn_Wkv"]
    for layer in ("L2", "L3"):
        a[layer + "_mem"] = rows(n[layer + "_xattn_W_mem"])
        a[layer + "_mem_t"] = n[layer + "_xattn_W_mem"].T
        a[layer + "_gate"] = rows(n[layer + "_xattn_W_gate"].T)
        a[layer + "_bgate"], a[layer + "_norm"] = cols(n[layer + "_xattn_b_gate"]), cols(n[layer + "_xattn_norm_w"])

    eye = np.eye(P, dtype=f32)
    a["c_ident"], a["c_ones"] = eye, np.ones((P, P), f32)
    a["c_iota"] = (np.arange(P)[:, None] + P * np.arange(2)[None, :]).astype(f32)
    inv = (f32(1) / f32(10000) ** (np.arange(0, SHD, 2, dtype=f32) / f32(SHD))).astype(f32)
    angle = np.outer(np.arange(S, dtype=f32), inv).astype(f32)
    table = np.stack([np.tile(np.concatenate([f(angle), f(angle)], axis=1), (1, P // SHD)) for f in (np.cos, np.sin)])
    a["c_rope"] = table.astype(f32).reshape(2, 2, P, P).transpose(2, 0, 1, 3)
    rot = np.zeros((P, P), f32)
    for m in range(P):
        if m % SHD < SHD // 2:
            rot[m + SHD // 2, m] = -1
        else:
            rot[m - SHD // 2, m] = 1
    a["c_rot"] = rot
    key, query = np.arange(S)[None, :], np.arange(S)[:, None]
    bias = np.where(key > query, -BIG, 0.0).astype(f32)
    a["c_causal"] = bias.reshape(2, P, S).transpose(1, 0, 2)
    a["c_causal_t"] = bias.T.reshape(2, P, S).transpose(1, 0, 2)
    a["c_headmask"] = (np.arange(P)[:, None] // SHD == np.arange(P // SHD)[None, :]).astype(f32)
    sel = np.zeros((P, 4, P), f32)
    for j in range(4):
        sel[:, j, 32 * j] = 1
    a["c_sel"] = sel
    for width in (SHD, CHD):
        m = np.zeros((P, P), f32)
        for j in range(P):
            m[j // 32 * 32 + width, j] = 1
        a[f"c_sum{width}"] = m
    low = np.zeros((P, 5), f32)
    block = np.arange(P) % 32 // CHD
    low[:, 0] = np.where(block == 2, 1, 0)
    low[:, 1] = np.where(block == 3, 1, 0)
    low[:, 2] = np.arange(P) % 32 == 0
    low[:, 3:5] = 1 - 2 * low[:, 0:2]
    a["c_low"] = low
    return {k: np.ascontiguousarray(v) for k, v in a.items()}


def kernel(**inputs):
    from concourse import bacc
    from concourse.bass_utils import run_bass_kernel_spmd

    nc = bacc.Bacc("TRN2", target_bir_lowering=False, num_devices=1)
    arrays = _inputs(inputs)
    src = {k: nc.dram_tensor("in_" + k, v.shape, mybir.dt.from_np(v.dtype), kind="ExternalInput").ap()
           for k, v in arrays.items()}
    out = nc.dram_tensor("out_t", (B, P, DC, S), F32, kind="ExternalOutput").ap()
    build(nc, src, out)
    r = run_bass_kernel_spmd(nc, [{"in_" + k: v for k, v in arrays.items()}], core_ids=[0])
    return np.ascontiguousarray(r.results[0]["out_t"].transpose(0, 3, 2, 1).reshape(B, S, D))
```

```python
import numpy as np

import concourse.bass as bass
from concourse import mybir
from contextlib import ExitStack

F32, F32R, BF16 = mybir.dt.float32, mybir.dt.float32r, mybir.dt.bfloat16
I32, U8 = mybir.dt.int32, mybir.dt.uint8
ACT, ALU, AX = mybir.ActivationFunctionType, mybir.AluOpType, mybir.AxisListType

P = 128
B, S, D = 8, 256, 256
DC = D // P
C = 128
NK = 1601
KT = -(-NK // P)
KLAST = NK - (KT - 1) * P
NKP = NK + NK % 2
MW = -(-NKP // 4)
NC = 4
KCH = [(i * (NKP // 8 * 2), NKP // 8 * 2 if i < NC - 1 else NKP - i * (NKP // 8 * 2)) for i in range(NC)]
NH = 16
SHD, CHD, XHD = D // NH, C // NH, 64
FF0, FF1 = 688, 1024
NG = NH // 4
NP = NH // 2
BIG = 1e30
EXP_LN = "natural_log_exp_and_others"


class Phase:

    def __init__(self, nc, name):
        self.nc, self.name, self.stack, self.sems = nc, name, ExitStack(), []

    def __enter__(self):
        return self

    def __exit__(self, *error):
        self.stack.close()
        if error[0] is None:
            self.nc.clear_and_free_semaphores(self.sems)
            self.nc.all_engine_barrier()

    def sem(self, name):
        self.sems.append(self.nc.alloc_semaphore(f"{self.name}_{name}"))
        return self.sems[-1]

    def sems2(self, name):
        return [self.sem(f"{name}{k}") for k in range(2)]

    def sb(self, name, shape, dt=F32):
        return self.stack.enter_context(self.nc.sbuf_tensor(f"{self.name}_{name}", shape, dt))

    def banks(self, name, n, width=512):
        return [self.stack.enter_context(self.nc.psum_tensor(f"{self.name}_{name}{k}", [P, width], F32))
                for k in range(n)]


def batches(eng, ahead, main):
    ahead(0, 0)
    with eng.Fori(0, B // 2 - 1) as i:
        ahead(i * 2 + 1, 1)
        main(i * 2, 0)
        ahead(i * 2 + 2, 0)
        main(i * 2 + 1, 1)
    ahead(B - 1, 1)
    main(B - 2, 0)
    main(B - 1, 1)


def half(b, p):
    return b // 2 if isinstance(b, int) else (b - p) // 2


class Chain:

    def __init__(self, eng, sem, before):
        self.eng, self.sem, self.n = eng, sem, before

    def link(self, instruction):
        self.n = self.n + 1
        instruction.then_inc(self.sem, 1)
        self.eng.wait_ge(self.sem, self.n)


def load_constants(nc, src, c):
    with Phase(nc, "setup") as ph:
        names = list(c["loads"])
        loaded, built, pe_done = ph.sem("loaded"), ph.sem("built"), ph.sem("pe_done")
        tok = ph.sb("tok", [P, B, S], I32)
        is_one = ph.sb("is_one", [P, B, S])
        pos_i = ph.sb("pos_i", [P, S], I32)
        pos = ph.sb("pos", [P, 3, S])
        onehot = ph.sb("onehot", [P, 2, S])
        iota = ph.sb("iota", [P, 2])
        tables = ph.sb("tables", [P, 2, 2, P])
        stage = ph.sb("stage", [P, 2, S])
        causal = ph.sb("causal", [P, 2, S])
        sel = ph.sb("sel", [P, 4, P])
        rope_ps = ph.banks("rope", 2)
        with nc.Block() as block:
            n_loads = len(names) + 6

            @block.sync
            def _(sp):
                for name in names:
                    sp.dma_start(c[name][:], c["loads"][name]).then_inc(loaded, 16)
                sp.dma_start(tok[:], src["tok_mask"].partition_broadcast(P)).then_inc(loaded, 16)
                sp.dma_start(pos_i[:], src["pos"][0].partition_broadcast(P)).then_inc(loaded, 16)
                sp.dma_start(iota[:], src["c_iota"]).then_inc(loaded, 16)
                sp.dma_start(tables[:], src["c_rope"]).then_inc(loaded, 16)
                sp.dma_start(causal[:], src["c_causal"]).then_inc(loaded, 16)
                sp.dma_start(sel[:], src["c_sel"]).then_inc(loaded, 16)

            @block.vector
            def _(dve):
                dve.wait_ge(loaded, 16 * n_loads)
                ch = Chain(dve, built, 0)
                ch.link(nc.vector.tensor_scalar(is_one[:], tok[:], 1.0, None, ALU.is_equal))
                ch.link(nc.vector.tensor_tensor(c["vm"][:, :, 0:S - 1], is_one[:, :, 0:S - 1],
                                                is_one[:, :, 1:S], ALU.mult))
                ch.link(nc.vector.memset(c["vm"][:, :, S - 1:S], 0.0))
                ch.link(nc.vector.tensor_copy(pos[:, 0, :], pos_i[:]))
                ch.link(nc.vector.tensor_scalar(pos[:, 1, :], pos[:, 0, :], 0.0, float(S), ALU.is_lt, ALU.mult))
                ch.link(nc.vector.tensor_tensor(pos[:, 2, :], pos[:, 0, :], pos[:, 1, :], ALU.add))
                ch.link(nc.vector.tensor_scalar(pos[:, 0, :], pos[:, 2, :], 0.0, float(S - 1), ALU.max, ALU.min))
                for k in range(2):
                    ch.link(nc.vector.tensor_scalar(onehot[:, k, :], pos[:, 0, :], iota[:, k:k + 1], None,
                                                    ALU.is_equal))
                dve.wait_ge(pe_done, 1)
                ch.link(nc.vector.tensor_copy(c["cos"][:], rope_ps[0][:, 0:S]))
                ch.link(nc.vector.tensor_copy(c["sin"][:], rope_ps[1][:, 0:S]))
                ch.link(nc.vector.tensor_copy(c["causal"][:], causal[:]))
                ch.link(nc.vector.tensor_copy(c["causal_tb"][:], c["causal_t"][:]))
                ch.link(nc.vector.tensor_copy(c["ident_b"][:], c["ident"][:]))
                ch.link(nc.vector.memset(c["eps6"][:], 1e-6))
                ch.link(nc.vector.memset(c["eps5"][:], 1e-5))
                ch.link(nc.vector.tensor_copy(c["ones_r"][:], c["ones"][:]))
                ch.link(nc.vector.tensor_copy(c["sel_r"][:], sel[:]))
                ch.link(nc.vector.tensor_scalar(c["mean"][:], c["ones"][:], 1.0 / D, None, ALU.mult))

            @block.scalar
            def _(act):
                act.wait_ge(loaded, 16 * n_loads)
                for k, name in enumerate(("attn_gate", "ff_gate")):
                    nc.scalar.activation(c["tanh_gate"][:, k:k + 1], c[name][:], ACT.Tanh)

            @block.tensor
            def _(pe):
                pe.wait_ge(built, 9)
                for k in range(2):
                    for t in range(2):
                        last = nc.tensor.matmul(rope_ps[k][:, 0:S], tables[:, k, t, :], onehot[:, t, :],
                                                start=(t == 0), stop=(t == 1))
                last.then_inc(pe_done, 1)
def self_projections(nc, src, c, q_d, k_d, v_d):
    with Phase(nc, "selfproj") as ph:
        x = ph.sb("x", [P, 2, DC, S])
        sq = ph.sb("sq", [P, DC, S])
        ln = ph.sb("ln", [P, S])
        rs = ph.sb("rs", [P, 2, S])
        xn = ph.sb("xn", [P, DC, S])
        xe = ph.sb("xe", [P, 2, 2, DC, S])
        w = ph.sb("w", [P, 2, DC, 3 * D])
        raw = ph.sb("raw", [P, 2, S])
        by_cos = ph.sb("by_cos", [P, 2, S])
        by_sin = ph.sb("by_sin", [P, 2, S])
        qk = ph.sb("qk", [P, 2, 4, S])
        v = ph.sb("v", [P, 2, 2, NH, 32])
        var_ps, qk_ps, rot_ps, v_ps = (ph.banks(n, k) for n, k in (("var", 1), ("qk", 2), ("rot", 2), ("v", 2)))
        x_ready, q_stored, v_stored = ph.sems2("x_ready"), ph.sems2("q_stored"), ph.sems2("v_stored")
        w_ready, x_free, sq_ready, sq_free = (ph.sem(n) for n in ("w_ready", "x_free", "sq_ready", "sq_free"))
        var_ready, ln_ready, rs_ready = ph.sem("var_ready"), ph.sem("ln_ready"), ph.sem("rs_ready")
        xe_ready, steps = ph.sem("xe_ready"), ph.sem("steps")
        qk_ready, raw_ready, rot_ready, turned = (ph.sem(n) for n in ("qk_ready", "raw_ready", "rot_ready", "turned"))
        rot_used = ph.sem("rot_used")
        v_ready, v_copied, v_set, out_free = (ph.sem(n) for n in ("v_ready", "v_copied", "v_set", "out_free"))
        with nc.Block() as block:
            @block.sync
            def _(sp):
                for e, name in enumerate(("v_qkv", "l_qkv")):
                    sp.dma_start(w[:, e], src[name]).then_inc(w_ready, 16)
                with sp.Fori(0, B // 2) as i:
                    for p in range(2):
                        sp.wait_ge(x_free, i * 2 + p + 1)
                        sp.dma_start(x[:, p], src["x_t"][i * 2 + p]).then_inc(x_ready[p], 16)

            @block.gpsimd
            def _(pool):
                nc.gpsimd.memset(v[:], 0.0).then_inc(v_set, 1)
                pool.wait_ge(v_set, 1)
                nc.gpsimd.memset(v[:, :, :, :, SHD:SHD + 1], 1.0).then_inc(v_set, 1)
                pool.sem_inc(out_free, 2)
                with pool.Fori(0, B // 2) as i:
                    for p in range(2):
                        b = i * 2 + p
                        pool.wait_ge(turned, b * 4 + 4 + PRIME)
                        pool.dma_start(q_d[b], qk[:, p, 0:2]).then_inc(q_stored[p], 16)
                        pool.dma_start(k_d[b], qk[:, p, 2:4]).then_inc(q_stored[p], 16)
                        pool.wait_ge(v_copied, b * 2 + 2 + PRIME)
                        pool.dma_start(v_d[b], v[:, p]).then_inc(v_stored[p], 16)
                        pool.wait_ge(q_stored[p], i * 32 + 32)
                        pool.wait_ge(v_stored[p], i * 16 + 16)
                        pool.sem_inc(out_free, 1)

            @block.scalar
            def _(act):
                act.preload_act_table_set(EXP_LN)
                prime(act, raw_ready, v_copied, ln_ready)

                def ahead(b, p):
                    act.wait_ge(x_ready[p], half(b, p) * 16 + 16)
                    act.wait_ge(var_ready, b + PRIME)
                    nc.scalar.activation(sq[:], x[:, p], ACT.Square).then_inc(sq_ready, 1)
                    act.wait_ge(var_ready, b + 1 + PRIME)
                    nc.scalar.activation(ln[:], var_ps[0][:, 0:S], ACT.Ln, bias=c["eps6"][:, 0:1]).then_inc(ln_ready, 1)
                    act.wait_ge(ln_ready, b + 1 + PRIME)
                    nc.scalar.activation(rs[:, p], ln[:], ACT.Exp, scale=-0.5).then_inc(rs_ready, 1)

                def main(b, p):
                    for m in range(4):
                        act.wait_ge(qk_ready, b * 4 + m + 1)
                        act.wait_ge(turned, b * 4 + m - 1 + PRIME)
                        nc.scalar.activation(raw[:, m % 2], qk_ps[m % 2][:, 0:S], ACT.Copy).then_inc(raw_ready, 1)
                    act.wait_ge(out_free, b + 1)
                    act.wait_ge(v_set, 2)
                    for t in range(2):
                        act.wait_ge(v_ready, b * 2 + t + 1 + PRIME)
                        nc.scalar.activation(v[:, p, t, :, 0:SHD],
                                             v_ps[t][:, 0:D].rearrange("p (h d) -> p h d", h=NH),
                                             ACT.Copy).then_inc(v_copied, 1)
                batches(act, ahead, main)

            @block.vector
            def _(dve):
                dve.sem_inc(x_free, 2)
                prime(dve, turned, rot_used)

                def ahead(b, p):
                    ch = Chain(dve, steps, b * 4)
                    dve.wait_ge(rs_ready, b + 1)
                    for k in range(DC):
                        ins = nc.vector.scalar_tensor_tensor(xn[:, k], x[:, p, k], c["ln_in_w"][:, k:k + 1], rs[:, p],
                                                             ALU.mult, ALU.mult)
                        ch.link(ins)
                    dve.sem_inc(x_free, 1)
                    dve.wait_ge(v_ready, b * 2 - 2 + PRIME)
                    for k in range(DC):
                        ch.link(nc.vector.tensor_tensor(xe[:, p, 0, k], xn[:, k], c["vm"][:, b, :], ALU.mult))
                    nc.vector.tensor_tensor(xe[:, p, 1], xn[:], xe[:, p, 0], ALU.subtract).then_inc(xe_ready, 1)
                    dve.wait_ge(xe_ready, b + 1)

                def main(b, p):
                    dve.wait_ge(out_free, b + 1)
                    for m in range(4):
                        ch = m % 2
                        dve.wait_ge(raw_ready, b * 4 + m + 1 + PRIME)
                        nc.vector.tensor_tensor(by_cos[:, ch], raw[:, ch], c["cos"][:], ALU.mult)
                        dve.wait_ge(rot_ready, b * 4 + m + 1)
                        nc.vector.tensor_tensor(by_sin[:, ch], rot_ps[ch][:, 0:S], c["sin"][:], ALU.mult).then_inc(
                            rot_used, 1)
                        dve.wait_ge(rot_used, b * 4 + m + 1 + PRIME)
                        nc.vector.tensor_tensor(qk[:, p, m], by_cos[:, ch], by_sin[:, ch], ALU.add).then_inc(turned, 1)
                batches(dve, ahead, main)

            @block.tensor
            def _(pe):
                prime(pe, v_ready, var_ready)
                def ahead(b, p):
                    pe.wait_ge(sq_ready, b + 1)
                    pe.wait_ge(ln_ready, b + PRIME)
                    for k in range(DC):
                        last = nc.tensor.matmul(var_ps[0][:, 0:S], c["mean"][:], sq[:, k], start=(k == 0), stop=(k == DC - 1))
                    last.then_inc(var_ready, 1)

                def turn(b, m):
                    pe.wait_ge(raw_ready, b * 4 + m + 1 + PRIME)
                    pe.wait_ge(rot_used, b * 4 + m - 1 + PRIME)
                    nc.tensor.matmul(rot_ps[m % 2][:, 0:S], c["rot"][:], raw[:, m % 2], start=True, stop=True
                                     ).then_inc(rot_ready, 1)

                def main(b, p):
                    pe.wait_ge(w_ready, 32)
                    pe.wait_ge(xe_ready, b + 1)
                    for m in range(4):
                        pe.wait_ge(raw_ready, b * 4 + m - 1 + PRIME)
                        for n in range(4):
                            e, k = divmod(n, 2)
                            last = nc.tensor.matmul(qk_ps[m % 2][:, 0:S], w[:, e, k, m * P:(m + 1) * P], xe[:, p, e, k],
                                                    start=(n == 0), stop=(n == 3))
                        last.then_inc(qk_ready, 1)
                        if m:
                            turn(b, m - 1)
                    for t in range(2):
                        pe.wait_ge(v_copied, b * 2 + t - 1 + PRIME)
                        for n in range(4):
                            e, k = divmod(n, 2)
                            last = nc.tensor.matmul(v_ps[t][:, 0:D], xe[:, p, e, k, t * P:(t + 1) * P],
                                                    w[:, e, k, 2 * D:3 * D], start=(n == 0), stop=(n == 3))
                        last.then_inc(v_ready, 1)
                        if t == 0:
                            turn(b, 3)
                batches(pe, ahead, main)


PRIME = 4


def prime(eng, *sems):
    for s in sems:
        eng.sem_inc(s, PRIME)


def counted(eng, sem, n):
    if isinstance(n, int) and n <= 0:
        return
    eng.wait_ge(sem, n + PRIME)


def units(eng, per, ahead, step):
    ahead((0, 0, 0, 0))

    def batch(b, p, last=False):
        for g in range(per):
            if g + 1 < per:
                step((b, p, g, b * per + g), (b, p, g + 1, b * per + g + 1))
            elif not last:
                step((b, p, g, b * per + g), (b + 1, 1 - p, 0, b * per + per))
            else:
                step((b, p, g, b * per + g), None)

    with eng.Fori(0, B // 2 - 1) as i:
        batch(i * 2, 0)
        batch(i * 2 + 1, 1)
    batch(B - 2, 0)
    batch(B - 1, 1, last=True)


def following(u, per):
    b, p, g, n = u
    if g + 1 < per:
        return b, p, g + 1, n + 1
    return None if isinstance(b, int) and b == B - 1 else (b + 1, 1 - p, 0, n + 1)


def self_attention(nc, c, q_d, k_d, v_d, out_d):
    with Phase(nc, "self") as ph:
        q, k = ph.sb("q", [P, 2, 2, S]), ph.sb("k", [P, 2, 2, S])
        k_r = ph.sb("k_r", [P, 2, 2, S], F32R)
        v = ph.sb("v", [P, 2, 2, NH, 32])
        qd = ph.sb("qd", [P, 2, 4, S])
        qd_r = ph.sb("qd_r", [P, 4, S], F32R)
        negmax = ph.sb("negmax", [P, 2, 4, 2])
        diag = ph.sb("diag", [P, 2, 4, S], F32R)
        p0, p1 = ph.sb("p0", [P, 2, 4, S]), ph.sb("p1", [P, 2, 4, P])
        av, rsum, out = ph.sb("av", [P, S]), ph.sb("rsum", [P, S]), ph.sb("out", [P, 2, S])
        max_ps, s0_ps, s1_ps, av_ps, sum_ps = (ph.banks(n, m) for n, m in (("max", 2), ("s0", 2), ("s1", 1), ("av", 1), ("sum", 1)))
        loaded, stored = ph.sems2("loaded"), ph.sems2("stored")
        kr_ready, qd_ready, qdr_ready, max_ready, maxed, diag_ready = (
            ph.sem(n) for n in ("kr_ready", "qd_ready", "qdr_ready", "max_ready", "maxed", "diag_ready"))
        s0_ready, s1_ready, p0_ready, p1_ready = (ph.sem(n) for n in ("s0_ready", "s1_ready", "p0_ready", "p1_ready"))
        av_ready, av_copied, sum_ready, rsum_ready, out_ready = (
            ph.sem(n) for n in ("av_ready", "av_copied", "sum_ready", "rsum_ready", "out_ready"))
        with nc.Block() as block:
            @block.sync
            def _(sp):
                prime(sp, *stored)
                def load(b, p):
                    counted(sp, av_ready, b * NG - NG)
                    for dst, s in ((q, q_d), (k, k_d), (v, v_d)):
                        sp.dma_start(dst[:, p], s[b]).then_inc(loaded[p], 16)

                def step(u, nxt):
                    b, p, g, n = u
                    if g == 0 and (nxt and not (isinstance(b, int) and b == B - 1)):
                        load(b + 1, 1 - p)
                    sp.wait_ge(out_ready, n + 1 + PRIME)
                    sp.dma_start(out_d[b, :, g, :], out[:, g % 2]).then_inc(stored[g % 2], 16)

                units(sp, NG, lambda u: load(0, 0), step)
                for s in stored:
                    sp.wait_ge(s, 16 * B * NG // 2 + PRIME)

            @block.gpsimd
            def _(pool):
                prime(pool, qd_ready)

                def ahead(u):
                    b, p, g, n = u
                    pool.wait_ge(loaded[p], half(b, p) * 48 + 48)
                    pool.wait_ge(s1_ready, n - 1 + PRIME)
                    for j in range(4):
                        h = g % 2 * 4 + j
                        last = nc.gpsimd.tensor_tensor(qd[:, g % 2, j], q[:, p, g // 2],
                                                       c["headmask"][:, h:h + 1].to_broadcast([P, S]), ALU.mult)
                    last.then_inc(qd_ready, 1)

                units(pool, NG, ahead, lambda u, nxt: nxt and ahead(nxt))

            @block.scalar
            def _(act):
                act.preload_act_table_set(EXP_LN)
                prime(act, kr_ready, qdr_ready, p0_ready, p1_ready, av_copied)

                def ahead(u):
                    b, p, g, n = u
                    if g == 0:
                        act.wait_ge(loaded[p], half(b, p) * 48 + 48)
                        nc.scalar.activation(k_r[:, p], k[:, p], ACT.Copy).then_inc(kr_ready, 1)
                    act.wait_ge(qd_ready, n + 1 + PRIME)
                    act.wait_ge(max_ready, n * 4 + PRIME)
                    nc.scalar.activation(qd_r[:], qd[:, g % 2], ACT.Copy).then_inc(qdr_ready, 1)

                def step(u, nxt):
                    b, p, g, n = u
                    act.wait_ge(av_ready, n - 1 + PRIME)
                    act.wait_ge(s0_ready, n + 1 + PRIME)
                    for h in range(2):
                        last = nc.scalar.activation(p0[:, g % 2, 2 * h:2 * h + 2], s0_ps[h][:].rearrange("p (h s) -> p h s", h=2),
                                                    ACT.Exp, scale=SHD ** -0.5)
                    last.then_inc(p0_ready, 1)
                    act.wait_ge(s1_ready, n + 1 + PRIME)
                    nc.scalar.activation(p1[:, g % 2], s1_ps[0][:].rearrange("p (h s) -> p h s", h=4), ACT.Exp,
                                         scale=SHD ** -0.5).then_inc(p1_ready, 1)
                    if nxt:
                        ahead(nxt)
                    act.wait_ge(av_ready, n + 1 + PRIME)
                    act.wait_ge(out_ready, n + PRIME)
                    nc.scalar.activation(av[:], av_ps[0][:, 0:S], ACT.Copy).then_inc(av_copied, 1)

                units(act, NG, ahead, step)

            @block.vector
            def _(dve):
                prime(dve, maxed, diag_ready, rsum_ready, out_ready)

                def ahead(u):
                    b, p, g, n = u
                    for j in range(4):
                        dve.wait_ge(max_ready, n * 4 + j + 1 + PRIME)
                        nc.vector.tensor_reduce(negmax[:, g % 2, j], max_ps[j % 2][:].rearrange("p (t s) -> p t s", t=2),
                                                AX.X, ALU.max, negate=True).then_inc(maxed, 1)
                    dve.wait_ge(maxed, n * 4 + 4 + PRIME)
                    dve.wait_ge(s1_ready, n - 1 + PRIME)
                    nc.vector.tensor_tensor(diag[:, g % 2].rearrange("p j (t s) -> p (j t) s", t=2),
                                            c["ident"][:].unsqueeze(1).to_broadcast([P, 8, P]),
                                            negmax[:, g % 2].rearrange("p j t -> p (j t)").unsqueeze(2).to_broadcast([P, 8, P]),
                                            ALU.mult).then_inc(diag_ready, 1)

                def step(u, nxt):
                    b, p, g, n = u
                    if nxt:
                        ahead(nxt)
                    dve.wait_ge(sum_ready, n + 1 + PRIME)
                    nc.vector.reciprocal(rsum[:], sum_ps[0][:, 0:S]).then_inc(rsum_ready, 1)
                    dve.wait_ge(rsum_ready, n + 1 + PRIME)
                    dve.wait_ge(stored[g % 2], (b * 2 + g // 2) * 16 + PRIME)
                    nc.vector.tensor_tensor(out[:, g % 2], av[:], rsum[:], ALU.mult).then_inc(out_ready, 1)

                units(dve, NG, ahead, step)

            @block.tensor
            def _(pe):
                prime(pe, max_ready, s0_ready, s1_ready, av_ready, sum_ready)

                def maxima(u, heads):
                    b, p, g, n = u
                    if 0 in heads:
                        pe.wait_ge(kr_ready, b + 1 + PRIME)
                        pe.wait_ge(qdr_ready, n + 1 + PRIME)
                    for j in heads:
                        pe.wait_ge(maxed, n * 4 + j - 1 + PRIME)
                        for t in range(2):
                            o = max_ps[j % 2][:, t * S:(t + 1) * S]
                            nc.tensor.matmul(o, qd_r[:, j, t * P:(t + 1) * P], k_r[:, p, g // 2], start=True, stop=False)
                            last = nc.tensor.matmul(o, c["ident_b"][:], c["causal"][:, t], start=False, stop=True)
                        last.then_inc(max_ready, 1)

                def scores(u, t):
                    b, p, g, n = u
                    lo = t * P
                    for h in range(2):
                        if t == 0:
                            o = s0_ps[h][:].rearrange("p (h s) -> p h s", h=2)
                        else:
                            o = s1_ps[0][:, h * 2 * P:(h + 1) * 2 * P].rearrange("p (h s) -> p h s", h=2)
                        two = slice(2 * h, 2 * h + 2)
                        nc.tensor.matmul(o, k[:, p, g // 2, t * P:(t + 1) * P], qd[:, g % 2, two, lo:S], start=True, stop=False)
                        nc.tensor.matmul(o[:, :, 0:P], c["ident_b"][:],
                                         c["causal_tb"][:, t, lo:lo + P].unsqueeze(1).to_broadcast([P, 2, P]),
                                         start=False, stop=False)
                        last = nc.tensor.matmul(o, c["ones_r"][:], diag[:, g % 2, two, lo:S], start=False, stop=True)
                    last.then_inc(s1_ready if t else s0_ready, 1)

                def step(u, nxt):
                    b, p, g, n = u
                    pe.wait_ge(diag_ready, n + 1 + PRIME)
                    pe.wait_ge(qd_ready, n + 1 + PRIME)
                    pe.wait_ge(p0_ready, n + PRIME)
                    scores(u, 0)
                    pe.wait_ge(p1_ready, n + PRIME)
                    scores(u, 1)
                    if nxt:
                        maxima(nxt, (0, 1))
                    pe.wait_ge(p0_ready, n + 1 + PRIME)
                    pe.wait_ge(av_copied, n + PRIME)
                    for j in range(4):
                        nc.tensor.matmul(av_ps[0][32 * j:32 * j + 32, 0:S], v[:, p, 0, 4 * g + j], p0[:, g % 2, j],
                                         start=True, stop=False)
                    if nxt:
                        maxima(nxt, (2, 3))
                    pe.wait_ge(p1_ready, n + 1 + PRIME)
                    for j in range(4):
                        last = nc.tensor.matmul(av_ps[0][32 * j:32 * j + 32, P:S], v[:, p, 1, 4 * g + j], p1[:, g % 2, j],
                                                start=False, stop=True)
                    last.then_inc(av_ready, 1)
                    pe.wait_ge(av_copied, n + 1 + PRIME)
                    pe.wait_ge(rsum_ready, n + PRIME)
                    nc.tensor.matmul(sum_ps[0][:, 0:S], c["sum16"][:], av[:], start=True, stop=True).then_inc(sum_ready, 1)

                units(pe, NG, lambda u: maxima(u, (0, 1, 2, 3)), step)


class MaskedContext:

    def __init__(self, nc, ph, src, c, masked_d):
        self.nc, self.src, self.c, self.masked_d = nc, src, c, masked_d
        self.loaded, self.stored = ph.sems2("ctx_loaded"), ph.sems2("ctx_stored")
        self.mt_ready, self.read, self.steps, self.ready = (ph.sem(n) for n in ("mt_ready", "ctx_read", "ctx_steps", "ctx_ready"))
        self.ct = ph.sb("ct", [P, 2, NKP])
        self.mk_words = ph.sb("mk", [P, 2, MW], I32)
        self.mt_words = ph.sb("mt", [P, B * KT // 4], I32)
        self.mk = self.mk_words.bitcast(U8)
        self.mt = self.mt_words.bitcast(U8).rearrange("p (b t) -> p b t", b=B)
        self.valid, self.invalid, self.kept = (ph.sb(n, [P, NKP]) for n in ("valid", "invalid", "kept"))
        self.out = ph.sb("ctx_out", [P, 2, NKP])
        self.stat = ph.sb("stat", [P, 6])

    def prime_sync(self, sp):
        prime(sp, *self.stored)
        sp.dma_start(self.mt_words[:], self.src["key_mask_t"]).then_inc(self.mt_ready, 16)

    def prime_vector(self, dve):
        prime(dve, self.steps, self.read, self.ready)
        dve.wait_ge(self.mt_ready, 16)

    def load(self, sp, u):
        b, p, _, _ = u
        sp.wait_ge(self.read, b - 1 + PRIME)
        sp.dma_start(self.ct[:, p, :], self.src["ctx_t"][b]).then_inc(self.loaded[p], 16)
        sp.dma_start(self.mk_words[:, p, :], self.src["key_mask"][b].partition_broadcast(P)).then_inc(self.loaded[p], 16)

    def store(self, sp, u):
        b, p, _, _ = u
        sp.wait_ge(self.ready, b + 1 + PRIME)
        sp.dma_start(self.masked_d[b], self.out[:, p, :]).then_inc(self.stored[p], 16)

    def finish(self, sp):
        for s in self.stored:
            sp.wait_ge(s, 16 * B // 2 + PRIME)

    LINKS = 8

    def vector_step(self, dve, u, i):
        b, p, _, _ = u
        nc, stat, valid, invalid, kept = self.nc, self.stat, self.valid, self.invalid, self.kept
        done = (0, 1, 2, 3, 4, 7)[i]
        ch = Chain(dve, self.steps, b * self.LINKS + done + PRIME)
        if i == 0:
            dve.wait_ge(self.loaded[p], half(b, p) * 32 + 32)
            ch.link(nc.vector.tensor_scalar(invalid[:], self.mk[:, p, 0:NKP], 0.0, None, ALU.is_equal))
        elif i == 1:
            ch.link(nc.vector.tensor_scalar(valid[:], invalid[:], -1.0, 1.0, ALU.mult, ALU.add))
        elif i == 2:
            ch.link(nc.vector.tensor_reduce(stat[:, 0:1], valid[:, 0:NK], AX.X, ALU.add))
        elif i == 3:
            ch.link(nc.vector.tensor_tensor(kept[:], self.ct[:, p, :], valid[:], ALU.mult))
            dve.sem_inc(self.read, 1)
        elif i == 4:
            nc.vector.tensor_reduce(stat[:, 1:2], kept[:, 0:NK], AX.X, ALU.add)
            ch.link(nc.vector.tensor_scalar(stat[:, 2:3], stat[:, 0:1], 1.0, None, ALU.max))
            ch.link(nc.vector.reciprocal(stat[:, 3:4], stat[:, 2:3]))
            nc.vector.tensor_scalar(stat[:, 4:5], stat[:, 0:1], 1.0, -BIG, ALU.min, ALU.mult)
            ch.link(nc.vector.tensor_tensor(stat[:, 5:6], stat[:, 1:2], stat[:, 3:4], ALU.mult))
        else:
            dve.wait_ge(self.stored[p], half(b, p) * 16 + PRIME)
            nc.vector.scalar_tensor_tensor(self.out[:, p, :], invalid[:], stat[:, 5:6], kept[:],
                                           ALU.mult, ALU.add).then_inc(self.ready, 1)
            ch.link(nc.vector.tensor_scalar(self.c["key_bias"][:, b, :], self.mt[:, b, :], 0.0, stat[:, 4:5],
                                            ALU.is_equal, ALU.mult))

    STEPS = 6


def residual_norm(nc, c, name, x_d, norm, w_norm, b_norm=None, attn_d=None, w_attn=None, experts=False, gate=None,
                  x_out_d=None, normed_d=None, w_proj=None, proj_d=None, split=False):
    NE = 2 if experts else 1
    with Phase(nc, name) as ph:
        ka = attn_d.shape[2] if attn_d is not None else 0
        kp = proj_d.shape[2] if proj_d is not None else 0
        x, x1 = ph.sb("x", [P, 2, DC, S]), ph.sb("x1", [P, 2, DC, S])
        xc, sq, ln = ph.sb("xc", [P, DC, S]), ph.sb("sq", [P, DC, S]), ph.sb("ln", [P, S])
        rs, xs = ph.sb("rs", [P, S]), ph.sb("xs", [P, DC, S])
        xn = ph.sb("xn", [P, 2, DC, S])
        if ka:
            at = ph.sb("at", [P, 2, ka, S])
            ae = ph.sb("ae", [P, 2, 2, ka, S]) if experts else None
            wa = ph.sb("wa", [P, NE * ka, D])
        if kp:
            wp = ph.sb("wp", [P, DC, kp * P])
            high = ph.sb("high", [P, kp, S], F32R) if split else None
            pr = ph.sb("pr", [P, 2, kp, S], F32R if split else F32)
        at_ps, mean_ps, var_ps, pr_ps = (ph.banks(n, m) for n, m in (("at", 2), ("mean", 1), ("var", 1), ("pr", 4)))
        loaded, at_loaded, w_ready = ph.sems2("loaded"), ph.sems2("at_loaded"), ph.sem("w_ready")
        stored, pr_stored = ph.sems2("stored"), ph.sems2("pr_stored")
        ae_ready, at_ready, x1_ready, mean_ready, xc_ready = (
            ph.sem(n) for n in ("ae_ready", "at_ready", "x1_ready", "mean_ready", "xc_ready"))
        sq_ready, var_ready, ln_ready, rs_ready, xs_ready, xn_ready = (
            ph.sem(n) for n in ("sq_ready", "var_ready", "ln_ready", "rs_ready", "xs_ready", "xn_ready"))
        pr_ready, high_ready, pr_copied = ph.sem("pr_ready"), ph.sem("high_ready"), ph.sem("pr_copied")
        n_stored = (x_out_d is not None) + (normed_d is not None)
        n_weights = (NE if ka else 0) + (kp > 0)
        kpp = max(1, kp // 2)
        pair = min(kp, 2)
        with nc.Block() as block:
            @block.sync
            def _(sp):
                prime(sp, *stored, *pr_stored)
                if ka:
                    for e, w in enumerate(w_attn):
                        sp.dma_start(wa[:, e * ka:(e + 1) * ka], w).then_inc(w_ready, 16)
                if kp:
                    sp.dma_start(wp[:], w_proj).then_inc(w_ready, 16)

                def load_x(u):
                    b, p, _, _ = u
                    sp.wait_ge(xn_ready, b - 1 + PRIME)
                    sp.dma_start(x[:, p], x_d[b]).then_inc(loaded[p], 16)

                def load_attn(u):
                    b, p, _, _ = u
                    if not ka:
                        return
                    if experts:
                        sp.wait_ge(ae_ready, b * 2 - 2 + PRIME)
                    else:
                        sp.wait_ge(at_ready, b - 1 + PRIME)
                    sp.dma_start(at[:, p], attn_d[b]).then_inc(at_loaded[p], 16)

                def load(u):
                    load_attn(u)
                    load_x(u)
                    load_attn(following(u, 1))

                def step(u, nxt):
                    if nxt and following(nxt, 1):
                        load_attn(following(nxt, 1))
                    if nxt:
                        load_x(nxt)
                    b, p, _, _ = u
                    if x_out_d is not None:
                        sp.wait_ge(x1_ready, b + 1 + PRIME)
                        sp.dma_start(x_out_d[b], x1[:, p]).then_inc(stored[p], 16)
                    if normed_d is not None:
                        sp.wait_ge(xn_ready, b + 1 + PRIME)
                        sp.dma_start(normed_d[b], xn[:, p]).then_inc(stored[p], 16)
                    if kp:
                        sp.wait_ge(pr_copied, (b + 1) * kpp + PRIME)
                        sp.dma_start(proj_d[b], pr[:, p].bitcast(F32) if split else pr[:, p]).then_inc(pr_stored[p], 16)

                units(sp, 1, load, step)
                for p in range(2):
                    if n_stored:
                        sp.wait_ge(stored[p], B // 2 * n_stored * 16 + PRIME)
                    if kp:
                        sp.wait_ge(pr_stored[p], B // 2 * 16 + PRIME)

            @block.scalar
            def _(act):
                act.preload_act_table_set(EXP_LN)
                prime(act, sq_ready, ln_ready, rs_ready, high_ready)
                if kp and not split:
                    prime(act, pr_copied)

                def ahead(u):
                    b, p, _, _ = u
                    act.wait_ge(xc_ready, b + 1 + PRIME)
                    act.wait_ge(var_ready, b + PRIME)
                    nc.scalar.activation(sq[:], xc[:], ACT.Square).then_inc(sq_ready, 1)

                def statistics(u):
                    b, p, _, _ = u
                    act.wait_ge(var_ready, b + 1 + PRIME)
                    eps = c["eps5"] if norm == "layer" else c["eps6"]
                    nc.scalar.activation(ln[:], var_ps[0][:, 0:S], ACT.Ln, bias=eps[:, 0:1]).then_inc(ln_ready, 1)
                    act.wait_ge(ln_ready, b + 1 + PRIME)
                    act.wait_ge(xs_ready, b + PRIME)
                    nc.scalar.activation(rs[:], ln[:], ACT.Exp, scale=-0.5).then_inc(rs_ready, 1)

                def project(u):
                    b, p, _, _ = u
                    if not kp:
                        return
                    act.wait_ge(pr_stored[p], half(b, p) * 16 + PRIME)
                    for m in range(kpp):
                        act.wait_ge(pr_ready, b * kpp + m + 1 + PRIME)
                        src = pr_ps[m % 4][:, 0:pair * S].rearrange("p (m s) -> p m s", m=pair)
                        if split:
                            if m == 0:
                                act.wait_ge(pr_copied, b * kpp + PRIME)
                            nc.scalar.activation(high[:, 2 * m:2 * m + 2], src, ACT.Copy, scale=c["low"][:, 3:4]
                                                 ).then_inc(high_ready, 1)
                        else:
                            nc.scalar.activation(pr[:, p, pair * m:pair * m + pair], src, ACT.Copy).then_inc(pr_copied, 1)

                def first_unit(u):
                    ahead(u)
                    statistics(u)

                def step(u, nxt):
                    if nxt:
                        ahead(nxt)
                    project(u)
                    if nxt:
                        statistics(nxt)

                units(act, 1, first_unit, step)

            @block.vector
            def _(dve):
                prime(dve, ae_ready, x1_ready, xc_ready, xs_ready, xn_ready)
                if kp and split:
                    prime(dve, pr_copied)

                def split_experts(u):
                    b, p, _, _ = u
                    dve.wait_ge(at_loaded[p], half(b, p) * 16 + 16)
                    dve.wait_ge(at_ready, b - 1 + PRIME)
                    for g in range(ka):
                        last = nc.vector.tensor_tensor(ae[:, p, 0, g], at[:, p, g], c["vm"][:, b, :], ALU.mult)
                    last.then_inc(ae_ready, 1)
                    dve.wait_ge(ae_ready, b * 2 + 1 + PRIME)
                    nc.vector.tensor_tensor(ae[:, p, 1], at[:, p], ae[:, p, 0], ALU.subtract).then_inc(ae_ready, 1)

                def residual(u):
                    b, p, _, _ = u
                    dve.wait_ge(loaded[p], half(b, p) * 16 + 16)
                    if n_stored:
                        dve.wait_ge(stored[p], half(b, p) * 16 * n_stored + PRIME)
                    if ka:
                        dve.wait_ge(at_ready, b + 1 + PRIME)
                        src = at_ps[p][:].rearrange("p (m s) -> p m s", m=DC)
                        if gate is not None:
                            nc.vector.scalar_tensor_tensor(x1[:, p], src, gate, x[:, p], ALU.mult, ALU.add
                                                           ).then_inc(x1_ready, 1)
                        else:
                            nc.vector.tensor_tensor(x1[:, p], src, x[:, p], ALU.add).then_inc(x1_ready, 1)
                    else:
                        nc.vector.tensor_copy(x1[:, p], x[:, p]).then_inc(x1_ready, 1)
                    dve.wait_ge(x1_ready, b + 1 + PRIME)
                    dve.wait_ge(sq_ready, b + PRIME)
                    if norm == "layer":
                        dve.wait_ge(mean_ready, b + 1 + PRIME)
                        for k in range(DC):
                            last = nc.vector.tensor_tensor(xc[:, k], x1[:, p, k], mean_ps[0][:, 0:S], ALU.subtract)
                    else:
                        last = nc.vector.tensor_copy(xc[:], x1[:, p])
                    last.then_inc(xc_ready, 1)

                def normalise(u):
                    b, p, _, _ = u
                    dve.wait_ge(rs_ready, b + 1 + PRIME)
                    if kp:
                        counted(dve, pr_ready, (b - 1) * kpp)
                    dst = xs if norm == "layer" else xn[:, p]
                    for k in range(DC):
                        last = nc.vector.scalar_tensor_tensor(dst[:, k], xc[:, k], w_norm[:, k:k + 1], rs[:],
                                                              ALU.mult, ALU.mult)
                    last.then_inc(xs_ready, 1)
                    dve.wait_ge(xs_ready, b + 1 + PRIME)
                    if norm == "layer":
                        for k in range(DC):
                            last = nc.vector.tensor_scalar(xn[:, p, k], xs[:, k], b_norm[:, k:k + 1], None, ALU.add)
                        last.then_inc(xn_ready, 1)
                    else:
                        dve.sem_inc(xn_ready, 1)

                def low_parts(u):
                    b, p, _, _ = u
                    dve.wait_ge(pr_stored[p], half(b, p) * 16 + PRIME)
                    for m in range(kpp):
                        dve.wait_ge(high_ready, b * kpp + m + 1 + PRIME)
                        src = pr_ps[m % 4][:].rearrange("p (m s) -> p m s", m=2)
                        nc.vector.scalar_tensor_tensor(pr[:, p, 2 * m:2 * m + 2], src, c["low"][:, 0:1],
                                                       high[:, 2 * m:2 * m + 2], ALU.mult, ALU.add).then_inc(pr_copied, 1)

                def first_unit(u):
                    if experts:
                        split_experts(u)
                    residual(u)
                    normalise(u)
                    if experts:
                        split_experts(following(u, 1))

                def step(u, nxt):
                    if nxt:
                        residual(nxt)
                    if kp and split:
                        low_parts(u)
                    if nxt:
                        normalise(nxt)
                    if experts and nxt and following(nxt, 1):
                        split_experts(following(nxt, 1))

                units(dve, 1, first_unit, step)

            @block.tensor
            def _(pe):
                prime(pe, at_ready, mean_ready, var_ready, pr_ready)
                if n_weights:
                    pe.wait_ge(w_ready, n_weights * 16)

                def attend(u):
                    b, p, _, _ = u
                    if not ka:
                        return
                    if experts:
                        pe.wait_ge(ae_ready, b * 2 + 2 + PRIME)
                    else:
                        pe.wait_ge(at_loaded[p], half(b, p) * 16 + 16)
                    pe.wait_ge(x1_ready, b - 1 + PRIME)
                    for m in range(DC):
                        for n in range(NE * ka):
                            rhs = ae[:, p, n // ka, n % ka] if experts else at[:, p, n]
                            last = nc.tensor.matmul(at_ps[p][:, m * S:(m + 1) * S], wa[:, n, m * P:(m + 1) * P], rhs,
                                                    start=(n == 0), stop=(n == NE * ka - 1))
                    last.then_inc(at_ready, 1)

                def statistics(u):
                    b, p, _, _ = u
                    if norm == "layer":
                        pe.wait_ge(x1_ready, b + 1 + PRIME)
                        pe.wait_ge(xc_ready, b + PRIME)
                        for k in range(DC):
                            last = nc.tensor.matmul(mean_ps[0][:, 0:S], c["mean"][:], x1[:, p, k], start=(k == 0), stop=(k == DC - 1))
                        last.then_inc(mean_ready, 1)
                    pe.wait_ge(sq_ready, b + 1 + PRIME)
                    pe.wait_ge(ln_ready, b + PRIME)
                    for k in range(DC):
                        last = nc.tensor.matmul(var_ps[0][:, 0:S], c["mean"][:], sq[:, k], start=(k == 0), stop=(k == DC - 1))
                    last.then_inc(var_ready, 1)

                def project(u):
                    b, p, _, _ = u
                    if not kp:
                        return
                    pe.wait_ge(xn_ready, b + 1 + PRIME)
                    for m in range(kpp):
                        counted(pe, pr_copied, b * kpp + m - 3 if kpp >= 4 else (b - 1) * kpp + m + 1)
                        for h in range(pair):
                            t = pair * m + h
                            for k in range(DC):
                                last = nc.tensor.matmul(pr_ps[m % 4][:, h * S:(h + 1) * S], wp[:, k, t * P:(t + 1) * P],
                                                        xn[:, p, k], start=(k == 0), stop=(k == DC - 1))
                        last.then_inc(pr_ready, 1)

                def first_unit(u):
                    attend(u)
                    statistics(u)

                def step(u, nxt):
                    if nxt:
                        attend(nxt)
                    project(u)
                    if nxt:
                        statistics(nxt)

                units(pe, 1, first_unit, step)


def width(t):
    return P if t < KT - 1 else KLAST


def cross_attention_0(nc, src, c, q_d, out_d):
    with Phase(nc, "cross0") as ph:
        ct = ph.sb("ct", [P, 2, NKP])
        wk, wv = ph.sb("wk", [P, NG * P]), ph.sb("wv", [P, C])
        k_high = ph.sb("k_high", [P, 2, 512], F32R)
        ks = ph.sb("ks", [P, NG, NKP], F32R)
        qd = ph.sb("qd", [P, NG, 4, S], F32R)
        cv = ph.sb("cv", [P, 2, KT, C])
        v = ph.sb("v", [P, 2, KT, 4, 32])
        partmax, negmax = ph.sb("partmax", [P, 8, len(KCH)]), ph.sb("negmax", [P, 8])
        diag = ph.sb("diag", [P, 4, S], F32R)
        probs = ph.sb("probs", [P, 4, 4, S])
        av, ln_sum = ph.sb("av", [P, S]), ph.sb("ln_sum", [P, S])
        rsum, out = ph.sb("rsum", [P, S]), ph.sb("out", [P, 2, S])
        max_ps, s_ps = ph.banks("max", 2), ph.banks("s", 2, 1024)
        av_ps, misc_ps = ph.banks("av", 1)[0], ph.banks("misc", 1)[0]
        loaded, stored, w_ready = ph.sems2("loaded"), ph.sems2("stored"), ph.sem("w_ready")
        ln_ready, q_loaded, v_set, qd_set = ph.sem("ln_ready"), ph.sems2("q_loaded"), ph.sem("v_set"), ph.sem("qd_set")
        kp_ready, k_high_ready, k_ready, vp_ready, cv_ready, v_ready = (
            ph.sem(n) for n in ("kp_ready", "k_high_ready", "k_ready", "vp_ready", "cv_ready", "v_ready"))
        max_ready, maxed, negmax_ready, diag_ready, shift_ready, shifted = (
            ph.sem(n) for n in ("max_ready", "maxed", "negmax_ready", "diag_ready", "shift_ready", "shifted"))
        s_ready, probs_ready, probs_used, av_copied, sum_ready, rsum_ready, out_ready = (
            ph.sem(n) for n in ("s_ready", "probs_ready", "probs_used", "av_copied", "sum_ready", "rsum_ready", "out_ready"))
        NM = 8 * NC

        k_step = {4 + 2 * i: i for i in range(NC)}
        v_step = {5 + 2 * i: i for i in range(NC - 1)} | {10: NC - 1}
        shift_step = 11
        share = (2, 2, 3, 3, 3, 3, 2, 2, 3, 3, 3, 3)
        parts = [range(sum(share[:i]), sum(share[:i + 1])) for i in range(len(share))]
        early = {11 + i: parts[i] for i in range(3)}
        late = {1 + i: parts[3 + i] for i in range(9)}

        def max_items(nxt, after, step):
            items = [(nxt, q) for q in late.get(step, ())] if nxt else []
            return items + ([(after, q) for q in early.get(step, ())] if after else [])

        def tile(u, nxt, step):
            if step == KT:
                u, step = nxt, 0
            return u and (u, step, u[3] * KT + step, u[2] * KT + step)

        with nc.Block() as block:
            @block.sync
            def _(sp):
                prime(sp, *stored)
                sp.wait_ge(qd_set, 1)
                sp.dma_start(wk[:], src["ck_stack"]).then_inc(w_ready, 16)
                sp.dma_start(wv[:], src["cv"]).then_inc(w_ready, 16)

                def load(b, p):
                    counted(sp, probs_used, (b - 1) * NG * KT)
                    sp.dma_start(ct[:, p], src["ctx_t"][b]).then_inc(loaded[p], 16)

                def load_q(u):
                    b, p, g, n = u
                    if not isinstance(n, int) or n > 1:
                        counted(sp, max_ready, (n - 2) * NM + 1)
                    for j in range(4):
                        r = slice(32 * j, 32 * j + 32)
                        sp.dma_start(qd[r, g, j].bitcast(F32), q_d[b, r, g, :]).then_inc(q_loaded[g % 2], 16)

                def ahead(u):
                    load(0, 0)
                    load_q(u)
                    load_q(following(u, NG))

                def step(u, nxt):
                    b, p, g, n = u
                    if g == 0 and not (isinstance(b, int) and b == B - 1):
                        load(b + 1, 1 - p)
                    after = nxt and following(nxt, NG)
                    if after:
                        load_q(after)
                    sp.wait_ge(out_ready, n + 1 + PRIME)
                    sp.dma_start(out_d[b, :, g, :], out[:, g % 2]).then_inc(stored[g % 2], 16)

                units(sp, NG, ahead, step)
                for s in stored:
                    sp.wait_ge(s, 16 * B * NG // 2 + PRIME)

            @block.gpsimd
            def _(pool):
                nc.gpsimd.memset(qd[:].bitcast(F32), 0.0).then_inc(qd_set, 1)
                nc.gpsimd.memset(v[:], 0.0).then_inc(v_set, 1)
                pool.wait_ge(v_set, 1)
                nc.gpsimd.memset(v[:, :, :, :, CHD:CHD + 1], 1.0).then_inc(v_set, 1)

            def copy_shift(eng, u, heads):
                b, p, g, n = u
                eng.wait_ge(shift_ready, n + 1 + PRIME)
                for j in heads:
                    r = slice(32 * j, 32 * j + 1)
                    if eng is nc.scalar:
                        nc.scalar.activation(qd[r, g, j], misc_ps[r, 0:S], ACT.Copy).then_inc(shifted, 1)
                    else:
                        nc.vector.tensor_copy(qd[r, g, j], misc_ps[r, 0:S]).then_inc(shifted, 1)

            @block.scalar
            def _(act):
                act.preload_act_table_set(EXP_LN)
                prime(act, k_high_ready, cv_ready, probs_ready, av_copied, ln_ready, rsum_ready)

                def k_chunk(u, i):
                    b, p, g, n = u
                    w = KCH[i][1]
                    act.wait_ge(kp_ready, n * NC + i + 1 + PRIME)
                    act.wait_ge(k_ready, n * NC + i - 1 + PRIME)
                    nc.scalar.activation(k_high[:, i % 2, 0:w], misc_ps[:, 0:w], ACT.Identity, scale=c["low"][:, 4:5],
                                         bias=c["low"][:, 2:3]).then_inc(k_high_ready, 1)

                def v_chunk(u, i):
                    b, p, g, n = u
                    act.wait_ge(vp_ready, b * NC + i + 1 + PRIME)
                    if i == 0:
                        counted(act, v_ready, (b - 1) * NG)
                    rows, tiles = (P, 4) if i < NC - 1 else (KLAST, 1)
                    nc.scalar.activation(cv[0:rows, p, 4 * i:4 * i + tiles], misc_ps[0:rows, 0:tiles * C]
                                         .rearrange("p (t d) -> p t d", t=tiles), ACT.Copy).then_inc(cv_ready, 1)

                def exponentials(of_tile):
                    _, t, number, buf = of_tile
                    w = width(t)
                    act.wait_ge(s_ready, number + 1 + PRIME)
                    act.wait_ge(probs_used, number - 3 + PRIME)
                    nc.scalar.activation(probs[0:w, buf % 4], s_ps[buf % 2][0:w].rearrange("p (h s) -> p h s", h=4),
                                         ACT.Exp, scale=CHD ** -0.5).then_inc(probs_ready, 1)

                def beside(u, nxt, t):
                    after = nxt and following(nxt, NG)
                    if tile(u, nxt, t):
                        exponentials(tile(u, nxt, t))
                    if after and t in k_step:
                        k_chunk(after, k_step[t])
                    if nxt and nxt[2] == 0 and t in v_step:
                        v_chunk(nxt, v_step[t])
                    if nxt and t == shift_step:
                        copy_shift(nc.scalar, nxt, (0, 2))

                def ahead(u):
                    for i in range(NC):
                        k_chunk(u, i)
                    for i in range(NC):
                        k_chunk(following(u, NG), i)
                        v_chunk(u, i)
                    copy_shift(nc.scalar, u, (0, 2))
                    exponentials(tile(u, None, 0))
                    for t in range(1, 3):
                        beside(u, following(u, NG), t)

                def step(u, nxt):
                    b, p, g, n = u
                    for t in range(3, KT + 1):
                        beside(u, nxt, t)
                    act.wait_ge(probs_used, (n + 1) * KT + PRIME)
                    act.wait_ge(out_ready, n + PRIME)
                    nc.scalar.activation(av[:], av_ps[:, 0:S], ACT.Copy).then_inc(av_copied, 1)
                    if nxt:
                        for t in range(1, 3):
                            beside(nxt, following(nxt, NG), t)
                    act.wait_ge(sum_ready, n + 1 + PRIME)
                    nc.scalar.activation(ln_sum[:], misc_ps[:, 0:S], ACT.Ln).then_inc(ln_ready, 1)
                    act.wait_ge(ln_ready, n + 1 + PRIME)
                    nc.scalar.activation(rsum[:], ln_sum[:], ACT.Exp, scale=-1.0).then_inc(rsum_ready, 1)

                units(act, NG, ahead, step)

            @block.vector
            def _(dve):
                prime(dve, k_ready, v_ready, maxed, negmax_ready, diag_ready, out_ready)
                prime(dve, shifted)

                def k_chunk(u, i):
                    b, p, g, n = u
                    k0, w = KCH[i]
                    dve.wait_ge(k_high_ready, n * NC + i + 1 + PRIME)
                    nc.vector.scalar_tensor_tensor(ks[:, g, k0:k0 + w], misc_ps[:, 0:w], c["low"][:, 1:2],
                                                   k_high[:, i % 2, 0:w], ALU.mult, ALU.add).then_inc(k_ready, 1)

                def maxima(u, q):
                    b, p, g, n = u
                    w = KCH[q % NC][1]
                    if q == 0:
                        dve.wait_ge(negmax_ready, n + PRIME)
                    dve.wait_ge(max_ready, n * NM + q + 1 + PRIME)
                    nc.vector.tensor_reduce(partmax[:, q // NC, q % NC:q % NC + 1], max_ps[q % 2][:, 0:w], AX.X, ALU.max
                                            ).then_inc(maxed, 1)

                def diagonals(u):
                    b, p, g, n = u
                    dve.wait_ge(maxed, (n + 1) * NM + PRIME)
                    dve.wait_ge(diag_ready, n + PRIME)
                    nc.vector.tensor_reduce(negmax[:], partmax[:], AX.X, ALU.max, negate=True).then_inc(negmax_ready, 1)
                    dve.wait_ge(negmax_ready, n + 1 + PRIME)
                    dve.wait_ge(shift_ready, n + PRIME)
                    nc.vector.tensor_tensor(diag[:].rearrange("p j (t s) -> p (j t) s", t=2),
                                            c["ident"][:].unsqueeze(1).to_broadcast([P, 8, P]),
                                            negmax[:].unsqueeze(2).to_broadcast([P, 8, P]), ALU.mult).then_inc(diag_ready, 1)

                def group_values(u):
                    b, p, g, n = u
                    if isinstance(n, int) and n == 0:
                        dve.wait_ge(v_set, 2)
                    dve.wait_ge(cv_ready, (b + 1) * NC + PRIME)
                    counted(dve, probs_used, (n - 1) * KT)
                    nc.vector.tensor_copy(v[:, g % 2, 0:KT - 1, :, 0:CHD],
                                          cv[:, p, 0:KT - 1, g * 32:g * 32 + 32].rearrange("p t (j d) -> p t j d", j=4))
                    nc.vector.tensor_copy(v[0:KLAST, g % 2, KT - 1, :, 0:CHD],
                                          cv[0:KLAST, p, KT - 1, g * 32:g * 32 + 32].rearrange("p (j d) -> p j d", j=4)
                                          ).then_inc(v_ready, 1)

                def beside(u, nxt, t):
                    after = nxt and following(nxt, NG)
                    if after and t - 1 in k_step:
                        k_chunk(after, k_step[t - 1])
                    for v_, q in max_items(nxt, after, t):
                        maxima(v_, q)
                    if nxt and t == shift_step - 2:
                        diagonals(nxt)
                    if nxt and t == shift_step:
                        copy_shift(nc.vector, nxt, (1, 3))
                        group_values(nxt)

                def ahead(u):
                    for v_ in (u, following(u, NG)):
                        for i in range(NC):
                            k_chunk(v_, i)
                    for q in range(NM):
                        maxima(u, q)
                    diagonals(u)
                    copy_shift(nc.vector, u, (1, 3))
                    group_values(u)
                    for part in early.values():
                        for q in part:
                            maxima(following(u, NG), q)
                    beside(u, following(u, NG), 1)
                    beside(u, following(u, NG), 2)

                def step(u, nxt):
                    b, p, g, n = u
                    for t in range(3, KT + 1):
                        beside(u, nxt, t)
                    if nxt:
                        beside(nxt, following(nxt, NG), 1)
                        beside(nxt, following(nxt, NG), 2)
                    dve.wait_ge(rsum_ready, n + 1 + PRIME)
                    dve.wait_ge(stored[g % 2], (b * 2 + g // 2) * 16 + PRIME)
                    nc.vector.tensor_tensor(out[:, g % 2], av[:], rsum[:], ALU.mult).then_inc(out_ready, 1)

                units(dve, NG, ahead, step)

            @block.tensor
            def _(pe):
                prime(pe, kp_ready, vp_ready, max_ready, shift_ready, s_ready, probs_used, sum_ready)
                pe.wait_ge(w_ready, 32)

                def k_chunk(u, i):
                    b, p, g, n = u
                    k0, w = KCH[i]
                    if i == 0:
                        pe.wait_ge(loaded[p], half(b, p) * 16 + 16)
                        pe.wait_ge(rsum_ready, n - 2 + PRIME)
                    pe.wait_ge(k_ready, n * NC + i + PRIME)
                    if g == 1 and i:
                        pe.wait_ge(cv_ready, b * NC + i + PRIME)
                    nc.tensor.matmul(misc_ps[:, 0:w], wk[:, g * P:(g + 1) * P], ct[:, p, k0:k0 + w], start=True, stop=True
                                     ).then_inc(kp_ready, 1)

                def v_chunk(u, i):
                    b, p, g, n = u
                    pe.wait_ge(k_ready, (n + 1) * NC + i + 1 + PRIME)
                    for t in range(4 * i, min(4 * i + 4, KT)):
                        w = width(t)
                        last = nc.tensor.matmul(misc_ps[0:w, t % 4 * C:(t % 4 + 1) * C], ct[:, p, t * P:t * P + w], wv[:],
                                                start=True, stop=True)
                    last.then_inc(vp_ready, 1)

                def maxima(u, q):
                    b, p, g, n = u
                    m, (k0, w) = q // NC, KCH[q % NC]
                    if q == 0:
                        pe.wait_ge(k_ready, (n + 1) * NC + PRIME)
                        pe.wait_ge(q_loaded[g % 2], (b * 2 + g // 2 + 1) * 64)
                    pe.wait_ge(maxed, n * NM + q - 1 + PRIME)
                    nc.tensor.matmul(max_ps[q % 2][:, 0:w], qd[:, g, m // 2, m % 2 * P:m % 2 * P + P],
                                     ks[:, g, k0:k0 + w], start=True, stop=True).then_inc(max_ready, 1)

                def shift(u):
                    b, p, g, n = u
                    pe.wait_ge(diag_ready, n + 1 + PRIME)
                    pe.wait_ge(cv_ready, (b + 1) * NC + PRIME)
                    pe.wait_ge(rsum_ready, n - 1 + PRIME)
                    if following(u, NG):
                        pe.wait_ge(k_ready, (n + 2) * NC + PRIME)
                    for j in range(4):
                        last = nc.tensor.matmul(misc_ps[:, 0:S], c["sel_r"][:, j], diag[:, j], start=(j == 0), stop=(j == 3))
                    last.then_inc(shift_ready, 1)

                def scores(of_tile, halves=(0, 1)):
                    (b, p, g, n), t, number, buf = of_tile
                    w = width(t)
                    if 0 in halves:
                        pe.wait_ge(probs_ready, number - 1 + PRIME)
                        if t == 0:
                            pe.wait_ge(shifted, (n + 1) * 4 + PRIME)
                    for h in halves:
                        last = nc.tensor.matmul(s_ps[buf % 2][0:w, h * 512:(h + 1) * 512], ks[:, g, t * P:t * P + w],
                                                qd[:, g, 2 * h:2 * h + 2, :], start=True, stop=True)
                    if 1 in halves:
                        last.then_inc(s_ready, 1)

                def values(of_tile, heads):
                    (b, p, g, n), t, number, buf = of_tile
                    w = width(t)
                    if 0 in heads:
                        pe.wait_ge(probs_ready, number + 1 + PRIME)
                        if t == 0:
                            pe.wait_ge(v_ready, n + 1 + PRIME)
                            pe.wait_ge(av_copied, n + PRIME)
                    for j in heads:
                        last = nc.tensor.matmul(av_ps[32 * j:32 * j + 32, 0:S], v[0:w, g % 2, t, j], probs[0:w, buf % 4, j],
                                                start=(t == 0), stop=(t == KT - 1))
                    if 3 in heads:
                        last.then_inc(probs_used, 1)

                def ahead(u):
                    for i in range(NC):
                        k_chunk(u, i)
                    for i in range(NC):
                        k_chunk(following(u, NG), i)
                        v_chunk(u, i)
                    for q in range(NM):
                        maxima(u, q)
                    shift(u)
                    for part in early.values():
                        for q in part:
                            maxima(following(u, NG), q)
                    for t in range(2):
                        scores(tile(u, None, t))
                    values(tile(u, None, 0), range(4))

                def step(u, nxt):
                    b, p, g, n = u
                    after = nxt and following(nxt, NG)
                    for t in range(1, KT + 1):
                        now = tile(u, nxt, t)
                        soon = tile(u, nxt, t + 1) if t < KT else nxt and tile(nxt, None, 1)
                        items = max_items(nxt, after, t)
                        if soon:
                            scores(soon, (0,))
                        for v_, q in items[:1]:
                            maxima(v_, q)
                        if soon:
                            scores(soon, (1,))
                        if after and t in k_step:
                            k_chunk(after, k_step[t])
                        if nxt and nxt[2] == 0 and t in v_step:
                            v_chunk(nxt, v_step[t])
                        if now:
                            values(now, (0,))
                        for v_, q in items[1:2]:
                            maxima(v_, q)
                        if now:
                            values(now, (1, 2, 3))
                        for v_, q in items[2:]:
                            maxima(v_, q)
                        if nxt and t == shift_step:
                            shift(nxt)
                    pe.wait_ge(av_copied, n + 1 + PRIME)
                    if not nxt:
                        pe.wait_ge(rsum_ready, n + PRIME)
                    nc.tensor.matmul(misc_ps[:, 0:S], c["sum8"][:], av[:], start=True, stop=True).then_inc(sum_ready, 1)

                units(pe, NG, ahead, step)


def v_share(g):
    lo = (0, 4, 7, 10, 13)
    return range(lo[g % 4], lo[g % 4 + 1])


def cross_attention_1(nc, src, c, masked_d, q_d, out_d):
    with Phase(nc, "cross1") as ph:
        ct, cm = ph.sb("ct", [P, 2, NKP]), ph.sb("cm", [P, 2, NKP])
        wk, wv = ph.sb("wk", [P, NP, P]), ph.sb("wv", [P, 2, 512])
        qp = ph.sb("qp", [P, 2, S])
        ka, kb = ph.sb("ka", [P, 2, 2, NKP], F32R), ph.sb("kb", [P, 2, 2, NKP], F32R)
        qa, qb = ph.sb("qa", [P, 2, 2, S], F32R), ph.sb("qb", [P, 2, 2, S], F32R)
        v = ph.sb("v", [P, 2, KT, 512])
        partmax, negmax = ph.sb("partmax", [P, 4, len(KCH)]), ph.sb("negmax", [P, 4])
        diag = ph.sb("diag", [P, 2, S], F32R)
        bias = ph.sb("bias", [P, 2, KT])
        NPB = 4
        probs, acc = ph.sb("probs", [P, NPB, 2, S]), ph.sb("acc", [P, 2, 2, S])
        ln_sum = ph.sb("ln_sum", [P, S])
        av, rsum, out = ph.sb("av", [P, S]), ph.sb("rsum", [P, S]), ph.sb("out", [P, 2, S])
        k_ps, max_ps, s_ps = ph.banks("k", 2), ph.banks("max", 2), ph.banks("s", 2)
        av_ps, misc_ps = ph.banks("av", 1)[0], ph.banks("misc", 1)[0]
        loaded, q_loaded, stored = ph.sems2("loaded"), ph.sems2("q_loaded"), ph.sems2("stored")
        ln_ready, bias_ready, w_ready, kb_set, qb_set = ph.sem("ln_ready"), ph.sem("bias_ready"), ph.sem("w_ready"), ph.sem("kb_set"), ph.sem("qb_set")
        kp_ready, ka_ready, kb_ready, vp_ready, v_ready, qb_ready, q_ready = (
            ph.sem(n) for n in ("kp_ready", "ka_ready", "kb_ready", "vp_ready", "v_ready", "qb_ready", "q_ready"))
        max_ready, maxed, negmax_ready, diag_ready, shift_ready, shifted = (
            ph.sem(n) for n in ("max_ready", "maxed", "negmax_ready", "diag_ready", "shift_ready", "shifted"))
        s_ready, probs_ready, probs_used, added, av_copied, sum_ready, rsum_ready, out_ready = (
            ph.sem(n) for n in ("s_ready", "probs_ready", "probs_used", "added", "av_copied", "sum_ready", "rsum_ready", "out_ready"))
        NM = 4 * NC
        once = (slice(0, 64), slice(64, P))
        other = (slice(64, P), slice(0, 64))
        row = (slice(64, 65), slice(0, 1))

        def next_half(u):
            b, p, g, n = u
            if g < NP // 2:
                return b, p, 1
            return None if isinstance(b, int) and b == B - 1 else (b + 1, 1 - p, 0)

        k_step = {1 + 2 * i: i for i in range(NC)}
        v_steps = {3: (4, 7, 10), 4: (4, 6, 8, 10)}
        max_step = {2 + 2 * i + h: range(4 * i + 2 * h, 4 * i + 2 * h + 2) for i in range(NC) for h in range(2)}
        shift_step = 11

        def tile(u, nxt, step):
            if step == KT:
                u, step = nxt, 0
            return u and (u, step, u[3] * KT + step, u[2] * KT + step)

        def value_tile(u, step):
            half_batch = next_half(u)
            steps, tiles = v_steps[len(v_share(u[2]))], v_share(u[2])
            return (half_batch, tiles[steps.index(step)]) if half_batch and step in steps else None

        with nc.Block() as block:
            @block.sync
            def _(sp):
                prime(sp, *stored)
                sp.dma_start(wk[:], src["Wkv"][:, 0:NP * P].rearrange("p (h d) -> p h d", h=NP)).then_inc(w_ready, 16)
                sp.dma_start(wv[:], src["Wkv"][:, NP * P:].rearrange("p (h d) -> p h d", h=2)).then_inc(w_ready, 16)

                def load(b, p):
                    counted(sp, probs_used, (b - 1) * NP * KT)
                    sp.dma_start(ct[:, p], src["ctx_t"][b]).then_inc(loaded[p], 16)
                    sp.dma_start(cm[:, p], masked_d[b]).then_inc(loaded[p], 16)

                def load_q(u):
                    b, p, g, n = u
                    sp.wait_ge(q_ready, n - 1 + PRIME)
                    sp.dma_start(qp[:, g % 2], q_d[b, :, g, :]).then_inc(q_loaded[g % 2], 16)

                def ahead(u):
                    load(0, 0)
                    load_q(u)
                    load_q(following(u, NP))

                def step(u, nxt):
                    b, p, g, n = u
                    after = nxt and following(nxt, NP)
                    if after:
                        load_q(after)
                    if g == 0 and not (isinstance(b, int) and b == B - 1):
                        load(b + 1, 1 - p)
                    sp.wait_ge(out_ready, n + 1 + PRIME)
                    sp.dma_start(out_d[b, :, g, :], out[:, g % 2]).then_inc(stored[g % 2], 16)

                units(sp, NP, ahead, step)
                for s in stored:
                    sp.wait_ge(s, 16 * B * NP // 2 + PRIME)

            @block.gpsimd
            def _(pool):
                prime(pool, added)
                nc.gpsimd.memset(kb[:].bitcast(F32), 0.0).then_inc(kb_set, 1)
                pool.wait_ge(kb_set, 1)
                nc.gpsimd.memset(qb[:].bitcast(F32), 0.0).then_inc(qb_set, 1)
                pool.wait_ge(qb_set, 1)
                for h in range(2):
                    nc.gpsimd.memset(kb[row[h], :, h].bitcast(F32), 1.0).then_inc(kb_set, 1)
                    pool.wait_ge(kb_set, h + 2)

                def step(u, nxt):
                    b, p, g, n = u
                    for t in range(1, KT):
                        w = width(t)
                        pool.wait_ge(probs_ready, n * KT + t + 1 + PRIME)
                        if t == 1:
                            pool.wait_ge(sum_ready, n - 1 + PRIME)
                        else:
                            pool.wait_ge(added, n * (KT - 1) + t - 1 + PRIME)
                        slot = g * KT + t
                        left = probs[:, (slot - 1) % NPB] if t == 1 else acc[0:w, g % 2]
                        nc.gpsimd.tensor_tensor(acc[0:w, g % 2], left, probs[0:w, slot % NPB], ALU.add).then_inc(added, 1)

                units(pool, NP, lambda u: None, step)

            @block.scalar
            def _(act):
                act.preload_act_table_set(EXP_LN)
                prime(act, ka_ready, v_ready, probs_ready, av_copied, ln_ready, rsum_ready)

                def k_chunk(u, i):
                    b, p, g, n = u
                    k0, w = KCH[i]
                    act.wait_ge(kp_ready, n * NC + i + 1 + PRIME)
                    if i == 0:
                        counted(act, s_ready, (n - 1) * KT)
                    for h in range(2):
                        for half_rows in (once[h], other[h]):
                            last = nc.scalar.activation(ka[half_rows, g % 2, h, k0:k0 + w], k_ps[i % 2][once[h], 0:w], ACT.Copy)
                    last.then_inc(ka_ready, 1)

                def v_tile(hb, t):
                    b, p, h = hb
                    w = width(t)
                    n = (b * 2 + h) * KT + t
                    act.wait_ge(vp_ready, n + 1 + PRIME)
                    if t == 0:
                        counted(act, probs_used, (b * 2 + h - 1) * 4 * KT)
                    nc.scalar.activation(v[0:w, h, t], misc_ps[0:w, :], ACT.Copy).then_inc(v_ready, 1)

                def exponentials(of_tile):
                    (b, p, g, n), t, number, buf = of_tile
                    w = width(t)
                    if t == 0 and g == 0:
                        act.wait_ge(bias_ready, b + 1)
                    act.wait_ge(s_ready, number + 1 + PRIME)
                    act.wait_ge(probs_used, number - NPB + 1 + PRIME)
                    act.wait_ge(added, n * (KT - 1) + (t - NPB + 1 if t < NPB else max(t - NPB, 1)) + PRIME)
                    nc.scalar.activation(probs[0:w, buf % NPB], s_ps[buf % 2][0:w].rearrange("p (h s) -> p h s", h=2), ACT.Exp,
                                         scale=XHD ** -0.5, bias=bias[0:w, p, t:t + 1]).then_inc(probs_ready, 1)

                def beside(u, nxt, t):
                    if tile(u, nxt, t):
                        exponentials(tile(u, nxt, t))
                    if nxt and t in k_step:
                        k_chunk(nxt, k_step[t])
                    if value_tile(u, t):
                        v_tile(*value_tile(u, t))

                def ahead(u):
                    for i in range(NC):
                        k_chunk(u, i)
                    for t in range(KT):
                        v_tile((0, 0, 0), t)
                    exponentials(tile(u, None, 0))
                    for t in range(1, 3):
                        beside(u, following(u, NP), t)

                def step(u, nxt):
                    b, p, g, n = u
                    for t in range(3, KT + 1):
                        beside(u, nxt, t)
                    act.wait_ge(probs_used, (n + 1) * KT + PRIME)
                    act.wait_ge(out_ready, n + PRIME)
                    nc.scalar.activation(av[:], av_ps[:, 0:S], ACT.Copy).then_inc(av_copied, 1)
                    if nxt:
                        for t in range(1, 3):
                            beside(nxt, following(nxt, NP), t)
                    act.wait_ge(sum_ready, n + 1 + PRIME)
                    nc.scalar.activation(ln_sum[:], misc_ps[:, 0:S], ACT.Ln).then_inc(ln_ready, 1)
                    act.wait_ge(ln_ready, n + 1 + PRIME)
                    nc.scalar.activation(rsum[:], ln_sum[:], ACT.Exp, scale=-1.0).then_inc(rsum_ready, 1)

                units(act, NP, ahead, step)

            @block.vector
            def _(dve):
                prime(dve, kb_ready, qb_ready, q_ready, maxed, negmax_ready, diag_ready, shifted, out_ready)
                dve.wait_ge(kb_set, 3)
                dve.wait_ge(qb_set, 1)

                def queries(u):
                    b, p, g, n = u
                    q2 = g % 2
                    if g == 0:
                        counted(dve, probs_ready, (b - 1) * NP * KT)
                        nc.vector.tensor_scalar(bias[:, p], c["key_bias"][:, b, :], 1.0, None, ALU.mult).then_inc(bias_ready, 1)
                    dve.wait_ge(q_loaded[q2], (b * (NP // 2) + g // 2 + 1) * 16)
                    counted(dve, s_ready, (n - 1) * KT)
                    for h in range(2):
                        nc.vector.tensor_copy(qb[once[h], q2, h], qp[once[h], q2]).then_inc(qb_ready, 1)
                    dve.wait_ge(qb_ready, (n + 1) * 2 + PRIME)
                    for h in range(2):
                        nc.vector.tensor_copy(qa[once[h], q2, h], qb[once[h], q2, h])
                        last = nc.vector.tensor_tensor(qa[other[h], q2, h], qp[once[h], q2], qb[once[h], q2, h], ALU.subtract)
                    last.then_inc(q_ready, 1)

                def k_chunk(u, i):
                    b, p, g, n = u
                    k0, w = KCH[i]
                    dve.wait_ge(ka_ready, n * NC + i + 1 + PRIME)
                    for h in range(2):
                        last = nc.vector.tensor_tensor(kb[once[h], g % 2, h, k0:k0 + w], k_ps[i % 2][once[h], 0:w],
                                                       ka[once[h], g % 2, h, k0:k0 + w], ALU.subtract)
                    last.then_inc(kb_ready, 1)

                def maxima(u, q):
                    b, p, g, n = u
                    i, m = divmod(q, 4)
                    if q == 0:
                        dve.wait_ge(negmax_ready, n + PRIME)
                    dve.wait_ge(max_ready, n * NM + q + 1 + PRIME)
                    nc.vector.tensor_reduce(partmax[:, m, i:i + 1], max_ps[q % 2][:, 0:KCH[i][1]], AX.X, ALU.max
                                            ).then_inc(maxed, 1)

                def diagonals(u):
                    b, p, g, n = u
                    dve.wait_ge(maxed, (n + 1) * NM + PRIME)
                    dve.wait_ge(diag_ready, n + PRIME)
                    nc.vector.tensor_reduce(negmax[:], partmax[:], AX.X, ALU.max, negate=True).then_inc(negmax_ready, 1)
                    dve.wait_ge(negmax_ready, n + 1 + PRIME)
                    dve.wait_ge(shift_ready, n + PRIME)
                    nc.vector.tensor_tensor(diag[:].rearrange("p j (t s) -> p (j t) s", t=2),
                                            c["ident"][:].unsqueeze(1).to_broadcast([P, 4, P]),
                                            negmax[:].unsqueeze(2).to_broadcast([P, 4, P]), ALU.mult).then_inc(diag_ready, 1)

                def copy_shift(u):
                    b, p, g, n = u
                    dve.wait_ge(shift_ready, n + 1 + PRIME)
                    for h in range(2):
                        last = nc.vector.tensor_copy(qb[row[h], g % 2, h], misc_ps[row[h], h * S:(h + 1) * S])
                    last.then_inc(shifted, 1)

                def beside(nxt, t):
                    if t == 1:
                        queries(nxt)
                    for q in max_step.get(t, ()):
                        maxima(nxt, q)
                    if t - 1 in k_step:
                        k_chunk(nxt, k_step[t - 1])
                    if t == shift_step - 2:
                        diagonals(nxt)
                    if t == shift_step:
                        copy_shift(nxt)

                def ahead(u):
                    queries(u)
                    for i in range(NC):
                        k_chunk(u, i)
                    for q in range(NM):
                        maxima(u, q)
                    diagonals(u)
                    copy_shift(u)
                    for t in range(1, 4):
                        beside(following(u, NP), t)

                def step(u, nxt):
                    b, p, g, n = u
                    if nxt:
                        for t in range(4, KT + 1):
                            beside(nxt, t)
                        if following(nxt, NP):
                            for t in range(1, 4):
                                beside(following(nxt, NP), t)
                    dve.wait_ge(rsum_ready, n + 1 + PRIME)
                    dve.wait_ge(av_copied, n + 1 + PRIME)
                    dve.wait_ge(stored[g % 2], (b * (NP // 2) + g // 2) * 16 + PRIME)
                    nc.vector.tensor_tensor(out[:, g % 2], av[:], rsum[:], ALU.mult).then_inc(out_ready, 1)

                units(dve, NP, ahead, step)

            @block.tensor
            def _(pe):
                prime(pe, kp_ready, vp_ready, max_ready, shift_ready, s_ready, probs_used, sum_ready)
                pe.wait_ge(w_ready, 32)

                def k_chunk(u, i):
                    b, p, g, n = u
                    k0, w = KCH[i]
                    if i == 0:
                        pe.wait_ge(loaded[p], half(b, p) * 32 + 32)
                    pe.wait_ge(kb_ready, n * NC + i - 1 + PRIME)
                    nc.tensor.matmul(k_ps[i % 2][:, 0:w], wk[:, g], cm[:, p, k0:k0 + w], start=True, stop=True).then_inc(kp_ready, 1)

                def v_tile(hb, t, before):
                    b, p, h = hb
                    w = width(t)
                    n = (b * 2 + h) * KT + t
                    pe.wait_ge(loaded[p], half(b, p) * 32 + 32)
                    pe.wait_ge(rsum_ready, before + PRIME)
                    pe.wait_ge(v_ready, n + PRIME)
                    nc.tensor.matmul(misc_ps[0:w, :], ct[:, p, t * P:t * P + w], wv[:, h], start=True, stop=True).then_inc(vp_ready, 1)

                def maxima(u, q):
                    b, p, g, n = u
                    (i, m), (k0, w) = divmod(q, 4), KCH[q // 4]
                    if m == 0:
                        pe.wait_ge(ka_ready, n * NC + i + 1 + PRIME)
                    if q == 0:
                        pe.wait_ge(q_ready, n + 1 + PRIME)
                    pe.wait_ge(maxed, n * NM + q - 1 + PRIME)
                    nc.tensor.matmul(max_ps[q % 2][:, 0:w], qa[:, g % 2, m // 2, m % 2 * P:m % 2 * P + P],
                                     ka[:, g % 2, m // 2, k0:k0 + w], start=True, stop=True).then_inc(max_ready, 1)

                def shift(u, values_made):
                    b, p, g, n = u
                    pe.wait_ge(diag_ready, n + 1 + PRIME)
                    pe.wait_ge(rsum_ready, n - 1 + PRIME)
                    pe.wait_ge(v_ready, values_made + PRIME)
                    nc.tensor.matmul(misc_ps[:], c["ones_r"][:], diag[:], start=True, stop=True).then_inc(shift_ready, 1)

                def scores(of_tile):
                    (b, p, g, n), t, number, buf = of_tile
                    w = width(t)
                    pe.wait_ge(probs_ready, number - 1 + PRIME)
                    if t == 0:
                        pe.wait_ge(shifted, n + 1 + PRIME)
                        pe.wait_ge(kb_ready, (n + 1) * NC + PRIME)
                    for h in range(2):
                        o = s_ps[buf % 2][0:w, h * S:(h + 1) * S]
                        nc.tensor.matmul(o, ka[:, g % 2, h, t * P:t * P + w], qa[:, g % 2, h], start=True, stop=False)
                        last = nc.tensor.matmul(o, kb[:, g % 2, h, t * P:t * P + w], qb[:, g % 2, h], start=False, stop=True)
                    last.then_inc(s_ready, 1)

                def values(of_tile):
                    (b, p, g, n), t, number, buf = of_tile
                    w = width(t)
                    pe.wait_ge(probs_ready, number + 1 + PRIME)
                    if t == 0:
                        pe.wait_ge(v_ready, (b * 2 + g // 4 + 1) * KT + PRIME)
                        pe.wait_ge(av_copied, n + PRIME)
                    for h in range(2):
                        d0 = g % 4 * P + h * XHD
                        last = nc.tensor.matmul(av_ps[h * XHD:(h + 1) * XHD, 0:S], v[0:w, g // 4, t, d0:d0 + XHD],
                                                probs[0:w, buf % NPB, h], start=(t == 0), stop=(t == KT - 1))
                    last.then_inc(probs_used, 1)

                def ahead(u):
                    for i in range(NC):
                        k_chunk(u, i)
                    for t in range(KT):
                        v_tile((0, 0, 0), t, 0)
                    for q in range(NM):
                        maxima(u, q)
                    shift(u, KT)
                    for t in range(2):
                        scores(tile(u, None, t))
                    values(tile(u, None, 0))

                def step(u, nxt):
                    b, p, g, n = u
                    for t in range(1, KT + 1):
                        now = tile(u, nxt, t)
                        soon = tile(u, nxt, t + 1) if t < KT else nxt and tile(nxt, None, 1)
                        items = max_step.get(t, ()) if nxt else ()
                        if soon:
                            scores(soon)
                        if nxt and t == shift_step:
                            made = next_half(u)
                            shift(nxt, (made[0] * 2 + made[2]) * KT + v_share(g)[-1] + 1 if made else 2 * B * KT)
                        if nxt and t in k_step:
                            k_chunk(nxt, k_step[t])
                        if value_tile(u, t):
                            v_tile(*value_tile(u, t), n)
                        for q in items[:1]:
                            maxima(nxt, q)
                        if now:
                            values(now)
                        for q in items[1:]:
                            maxima(nxt, q)
                    if not nxt:
                        pe.wait_ge(rsum_ready, n + PRIME)
                    pe.wait_ge(added, (n + 1) * (KT - 1) + PRIME)
                    for h in range(2):
                        last = nc.tensor.matmul(misc_ps[h * XHD:(h + 1) * XHD, 0:S], c["ones"][:, 0:XHD], acc[:, g % 2, h],
                                                start=True, stop=True)
                    last.then_inc(sum_ready, 1)

                units(pe, NP, ahead, step)


def feed_forward(nc, src, c, name, x_d, normed_d, w_in, w_out, out_d, silu, gate=None, w_proj=None, proj_d=None,
                 masked_d=None):
    NE = 2 if silu else 1
    kh = w_out[0].shape[1]
    with Phase(nc, name) as ph:
        x, xn = ph.sb("x", [P, 2, DC, S]), ph.sb("xn", [P, 2, DC, S])
        xe = ph.sb("xe", [P, 2, 2, DC, S]) if silu else None
        wi = [ph.sb(f"wi{k}", [P, DC, kh * P]) for k in range(len(w_in))]
        wo = ph.sb("wo", [P, NE * kh, D])
        act_g = ph.sb("act_g", [P, 2, S])
        hid = ph.sb("hid", [P, 2, NE * kh, S])
        out = ph.sb("out", [P, 2, DC, S])
        wp = ph.sb("wp", [P, DC, C]) if proj_d is not None else None
        pr = ph.sb("pr", [P, 2, S])
        in_ps, out_ps, pr_ps = ph.banks("in", 4), ph.banks("out", 2), ph.banks("pr", 1)
        loaded, stored, pr_stored, w_ready = ph.sems2("loaded"), ph.sems2("stored"), ph.sems2("pr_stored"), ph.sem("w_ready")
        xe_ready, in_ready, act_ready, hid_ready, down_ready, out_ready, pr_ready, pr_copied = (
            ph.sem(n) for n in ("xe_ready", "in_ready", "act_ready", "hid_ready", "down_ready", "out_ready", "pr_ready", "pr_copied"))
        n_loaded = ph.sems2("n_loaded")
        masked = MaskedContext(nc, ph, src, c, masked_d) if masked_d is not None else None
        NB_ = NE * kh if silu else kh // 2
        n_weights = len(w_in) + NE + (proj_d is not None)

        with nc.Block() as block:
            @block.sync
            def _(sp):
                prime(sp, *stored, *pr_stored)
                for k, w in enumerate(w_in):
                    sp.dma_start(wi[k][:], w).then_inc(w_ready, 16)
                for e, w in enumerate(w_out):
                    sp.dma_start(wo[:, e * kh:(e + 1) * kh], w).then_inc(w_ready, 16)
                if proj_d is not None:
                    sp.dma_start(wp[:], w_proj).then_inc(w_ready, 16)

                if masked:
                    masked.prime_sync(sp)

                def load_x(u):
                    b, p, _, _ = u
                    sp.wait_ge(out_ready, b - 1 + PRIME)
                    sp.dma_start(x[:, p], x_d[b]).then_inc(loaded[p], 16)

                def load_normed(u):
                    b, p, _, _ = u
                    if silu:
                        sp.wait_ge(xe_ready, b * 2 - 2 + PRIME)
                    else:
                        counted(sp, in_ready, (b - 1) * NB_)
                    sp.dma_start(xn[:, p], normed_d[b]).then_inc(n_loaded[p], 16)

                def load(u):
                    load_normed(u)
                    load_x(u)
                    load_normed(following(u, 1))
                    if masked:
                        masked.load(sp, u)

                def step(u, nxt):
                    if nxt and masked:
                        masked.load(sp, nxt)
                    if nxt and following(nxt, 1):
                        load_normed(following(nxt, 1))
                    if nxt:
                        load_x(nxt)
                    b, p, _, _ = u
                    if masked:
                        masked.store(sp, u)
                    sp.wait_ge(out_ready, b + 1 + PRIME)
                    sp.dma_start(out_d[b], out[:, p]).then_inc(stored[p], 16)
                    if proj_d is not None:
                        sp.wait_ge(pr_copied, b + 1 + PRIME)
                        sp.dma_start(proj_d[b], pr[:, p]).then_inc(pr_stored[p], 16)

                units(sp, 1, load, step)
                if masked:
                    masked.finish(sp)
                for p in range(2):
                    sp.wait_ge(stored[p], B // 2 * 16 + PRIME)
                    if proj_d is not None:
                        sp.wait_ge(pr_stored[p], B // 2 * 16 + PRIME)

            @block.scalar
            def _(act):
                prime(act, act_ready, pr_copied)
                if not silu:
                    prime(act, hid_ready)

                def hidden(u):
                    b, p, _, _ = u
                    for m in range(NB_):
                        n = b * NB_ + m
                        act.wait_ge(in_ready, n + 1 + PRIME)
                        if silu:
                            act.wait_ge(hid_ready, n - 1 + PRIME)
                            nc.scalar.activation(act_g[:, m % 2], in_ps[m % 4][:, 0:S], ACT.Silu).then_inc(act_ready, 1)
                        else:
                            if m == 0:
                                act.wait_ge(down_ready, b - 1 + PRIME)
                            nc.scalar.activation(hid[:, p, 2 * m:2 * m + 2], in_ps[m % 4][:].rearrange("p (m s) -> p m s", m=2),
                                                 ACT.Gelu).then_inc(hid_ready, 1)

                def step(u, nxt):
                    b, p, _, _ = u
                    if nxt:
                        hidden(nxt)
                    if proj_d is not None:
                        act.wait_ge(pr_ready, b + 1 + PRIME)
                        act.wait_ge(pr_stored[p], half(b, p) * 16 + PRIME)
                        nc.scalar.activation(pr[:, p], pr_ps[0][:, 0:S], ACT.Copy).then_inc(pr_copied, 1)

                units(act, 1, hidden, step)

            @block.vector
            def _(dve):
                prime(dve, xe_ready, out_ready)
                if silu:
                    prime(dve, hid_ready)
                if masked:
                    masked.prime_vector(dve)

                def split(u):
                    b, p, _, _ = u
                    dve.wait_ge(n_loaded[p], half(b, p) * 16 + 16)
                    counted(dve, in_ready, (b - 1) * NB_)
                    for k in range(DC):
                        last = nc.vector.tensor_tensor(xe[:, p, 0, k], xn[:, p, k], c["vm"][:, b, :], ALU.mult)
                    last.then_inc(xe_ready, 1)
                    dve.wait_ge(xe_ready, b * 2 + 1 + PRIME)
                    nc.vector.tensor_tensor(xe[:, p, 1], xn[:, p], xe[:, p, 0], ALU.subtract).then_inc(xe_ready, 1)

                def hidden(u):
                    b, p, _, _ = u
                    for m in range(NB_):
                        dve.wait_ge(act_ready, b * NB_ + m + 1 + PRIME)
                        if m == 0:
                            dve.wait_ge(down_ready, b - 1 + PRIME)
                        nc.vector.tensor_tensor(hid[:, p, m], in_ps[m % 4][:, S:2 * S], act_g[:, m % 2], ALU.mult
                                                ).then_inc(hid_ready, 1)
                        if masked and m % 2 == 1 and m // 2 < masked.STEPS:
                            masked.vector_step(dve, u, m // 2)

                def step(u, nxt):
                    b, p, _, _ = u
                    if nxt and silu:
                        hidden(nxt)
                        if following(nxt, 1):
                            split(following(nxt, 1))
                    dve.wait_ge(loaded[p], half(b, p) * 16 + 16)
                    dve.wait_ge(stored[p], half(b, p) * 16 + PRIME)
                    dve.wait_ge(pr_ready, b - 1 + PRIME) if proj_d is not None else None
                    dve.wait_ge(down_ready, b + 1 + PRIME)
                    src_ = out_ps[p][:].rearrange("p (m s) -> p m s", m=DC)
                    if gate is not None:
                        nc.vector.scalar_tensor_tensor(out[:, p], src_, gate, x[:, p], ALU.mult, ALU.add).then_inc(out_ready, 1)
                    else:
                        nc.vector.tensor_tensor(out[:, p], src_, x[:, p], ALU.add).then_inc(out_ready, 1)

                def ahead(u):
                    if silu:
                        split(u)
                        split(following(u, 1))
                        hidden(u)

                units(dve, 1, ahead, step)

            @block.tensor
            def _(pe):
                prime(pe, in_ready, down_ready, pr_ready)
                pe.wait_ge(w_ready, n_weights * 16)

                def hidden(u):
                    b, p, _, _ = u
                    if silu:
                        pe.wait_ge(xe_ready, b * 2 + 2 + PRIME)
                    else:
                        pe.wait_ge(n_loaded[p], half(b, p) * 16 + 16)
                    for m in range(NB_):
                        pe.wait_ge(hid_ready, b * NB_ + (m - 3 if m >= 4 or NB_ % 4 == 0 else 0) + PRIME)
                        e, t = divmod(m, kh)
                        for h in range(2):
                            w = wi[2 * e + h] if silu else wi[0]
                            mt = t if silu else 2 * m + h
                            for k in range(DC):
                                rhs = xe[:, p, e, k] if silu else xn[:, p, k]
                                last = nc.tensor.matmul(in_ps[m % 4][:, h * S:(h + 1) * S], w[:, k, mt * P:(mt + 1) * P], rhs,
                                                        start=(k == 0), stop=(k == DC - 1))
                        last.then_inc(in_ready, 1)

                def step(u, nxt):
                    b, p, _, _ = u
                    if nxt:
                        hidden(nxt)
                    pe.wait_ge(hid_ready, (b + 1) * NB_ + PRIME)
                    pe.wait_ge(out_ready, b - 1 + PRIME)
                    for m in range(DC):
                        for k in range(NE * kh):
                            last = nc.tensor.matmul(out_ps[p][:, m * S:(m + 1) * S], wo[:, k, m * P:(m + 1) * P], hid[:, p, k],
                                                    start=(k == 0), stop=(k == NE * kh - 1))
                    last.then_inc(down_ready, 1)
                    if proj_d is not None:
                        pe.wait_ge(out_ready, b + 1 + PRIME)
                        pe.wait_ge(pr_copied, b + PRIME)
                        for k in range(DC):
                            last = nc.tensor.matmul(pr_ps[0][:, 0:S], wp[:, k], out[:, p, k], start=(k == 0), stop=(k == DC - 1))
                        last.then_inc(pr_ready, 1)

                units(pe, 1, hidden, step)


def memory_attention(nc, src, c, name, q_d, out_d):
    with Phase(nc, name) as ph:
        ct, cn = ph.sb("ct", [P, 2, NKP]), ph.sb("cn", [P, 2, KT, C])
        q = ph.sb("q", [P, 2, S])
        ct_r, q_r = ph.sb("ct_r", [P, 2, NKP], F32R), ph.sb("q_r", [P, 2, S], F32R)
        partmax, negmax = ph.sb("partmax", [P, 2, len(KCH)]), ph.sb("negmax", [P, 2])
        diag = ph.sb("diag", [P, 2, S], F32R)
        probs, acc = ph.sb("probs", [P, 2, 4, S]), ph.sb("acc", [P, 4, S])
        av, rsum, out = ph.sb("av", [P, S]), ph.sb("rsum", [P, S]), ph.sb("out", [P, 2, S])
        max_ps, s_ps = ph.banks("max", 2), ph.banks("s", 2, 1024)
        av_ps, sum_ps = ph.banks("av", 1)[0], ph.banks("sum", 1)[0]
        loaded, stored = ph.sems2("loaded"), ph.sems2("stored")
        rounded, max_ready, maxed, negmax_ready, diag_ready = (
            ph.sem(n) for n in ("rounded", "max_ready", "maxed", "negmax_ready", "diag_ready"))
        s_ready, probs_ready, probs_used, added, av_copied, sum_ready, rsum_ready, out_ready = (
            ph.sem(n) for n in ("s_ready", "probs_ready", "probs_used", "added", "av_copied", "sum_ready", "rsum_ready", "out_ready"))
        NM = 2 * NC
        quads = [range(t, min(t + 4, KT)) for t in range(0, KT, 4)]
        NQ = len(quads)

        with nc.Block() as block:
            @block.sync
            def _(sp):
                prime(sp, *stored)
                def load(u):
                    b, p, _, _ = u
                    counted(sp, probs_used, (b - 1) * NQ)
                    sp.dma_start(ct[:, p], src["ctx_t"][b]).then_inc(loaded[p], 16)
                    sp.dma_start(cn[:, p], src["ctx_n"][b]).then_inc(loaded[p], 16)
                    sp.dma_start(q[:, p], q_d[b]).then_inc(loaded[p], 16)

                def step(u, nxt):
                    b, p, _, _ = u
                    if nxt:
                        load(nxt)
                    sp.wait_ge(out_ready, b + 1 + PRIME)
                    sp.dma_start(out_d[b], out[:, p]).then_inc(stored[p], 16)

                units(sp, 1, load, step)
                for s in stored:
                    sp.wait_ge(s, 16 * B // 2 + PRIME)

            @block.gpsimd
            def _(pool):
                prime(pool, added)

                def step(u, nxt):
                    b, p, _, _ = u
                    for i in range(1, NQ):
                        pool.wait_ge(probs_ready, b * NQ + i + 1 + PRIME)
                        if i == 1:
                            pool.wait_ge(sum_ready, b + PRIME)
                        else:
                            pool.wait_ge(added, b * (NQ - 1) + i - 1 + PRIME)
                        if i < NQ - 1:
                            nc.gpsimd.tensor_tensor(acc[:], probs[:, 0] if i == 1 else acc[:], probs[:, i % 2], ALU.add
                                                    ).then_inc(added, 1)
                        else:
                            nc.gpsimd.tensor_tensor(acc[0:KLAST, 0], acc[0:KLAST, 0], probs[0:KLAST, i % 2, 0], ALU.add
                                                    ).then_inc(added, 1)

                units(pool, 1, lambda u: None, step)

            @block.scalar
            def _(act):
                act.preload_act_table_set(EXP_LN)
                prime(act, rounded, probs_ready, av_copied)

                def ahead(u):
                    b, p, _, _ = u
                    act.wait_ge(loaded[p], half(b, p) * 48 + 48)
                    counted(act, max_ready, (b - 1) * NM)
                    nc.scalar.activation(q_r[:, p], q[:, p], ACT.Copy)
                    nc.scalar.activation(ct_r[:, p], ct[:, p], ACT.Copy).then_inc(rounded, 1)

                def step(u, nxt):
                    b, p, _, _ = u
                    if nxt:
                        ahead(nxt)
                    for i, tiles in enumerate(quads):
                        n = b * NQ + i
                        act.wait_ge(s_ready, n + 1 + PRIME)
                        act.wait_ge(probs_used, b * NQ + max(i - 1, 0) + PRIME)
                        act.wait_ge(added, b * (NQ - 1) + (max(i - 2, 1) if i >= 2 else 0) + PRIME)
                        w, m = width(tiles[-1]), len(tiles)
                        nc.scalar.activation(probs[0:w, i % 2, 0:m], s_ps[i % 2][0:w, 0:m * S].rearrange("p (t s) -> p t s", t=m),
                                             ACT.Exp, scale=D ** -0.5).then_inc(probs_ready, 1)
                    act.wait_ge(probs_used, (b + 1) * NQ + PRIME)
                    act.wait_ge(out_ready, b + PRIME)
                    nc.scalar.activation(av[:], av_ps[:, 0:S], ACT.Copy).then_inc(av_copied, 1)

                units(act, 1, ahead, step)

            @block.vector
            def _(dve):
                prime(dve, maxed, negmax_ready, diag_ready, rsum_ready, out_ready)

                def ahead(u):
                    b, p, _, _ = u
                    dve.wait_ge(negmax_ready, b + PRIME)
                    for m in range(NM):
                        w = KCH[m % NC][1]
                        dve.wait_ge(max_ready, b * NM + m + 1 + PRIME)
                        nc.vector.tensor_reduce(partmax[:, m // NC, m % NC:m % NC + 1], max_ps[m % 2][:, 0:w], AX.X, ALU.max
                                                ).then_inc(maxed, 1)
                    dve.wait_ge(maxed, (b + 1) * NM + PRIME)
                    dve.wait_ge(diag_ready, b + PRIME)
                    nc.vector.tensor_reduce(negmax[:], partmax[:], AX.X, ALU.max, negate=True).then_inc(negmax_ready, 1)
                    dve.wait_ge(negmax_ready, b + 1 + PRIME)
                    counted(dve, s_ready, (b - 1) * NQ)
                    for m in range(2):
                        last = nc.vector.tensor_scalar(diag[:, p, m * P:(m + 1) * P], c["ident"][:], negmax[:, m:m + 1], None,
                                                       ALU.mult)
                    last.then_inc(diag_ready, 1)

                def step(u, nxt):
                    b, p, _, _ = u
                    if nxt:
                        ahead(nxt)
                    dve.wait_ge(sum_ready, b + 1 + PRIME)
                    dve.wait_ge(out_ready, b + PRIME)
                    nc.vector.reciprocal(rsum[:], sum_ps[:, 0:S]).then_inc(rsum_ready, 1)
                    dve.wait_ge(rsum_ready, b + 1 + PRIME)
                    dve.wait_ge(av_copied, b + 1 + PRIME)
                    dve.wait_ge(stored[p], half(b, p) * 16 + PRIME)
                    nc.vector.tensor_tensor(out[:, p], av[:], rsum[:], ALU.mult).then_inc(out_ready, 1)

                units(dve, 1, ahead, step)

            @block.tensor
            def _(pe):
                prime(pe, max_ready, s_ready, probs_used, sum_ready)

                def maxima(u, m):
                    b, p, _, _ = u
                    k0, w = KCH[m % NC]
                    pe.wait_ge(rounded, b + 1 + PRIME)
                    pe.wait_ge(maxed, b * NM + m - 1 + PRIME)
                    nc.tensor.matmul(max_ps[m % 2][:, 0:w], q_r[:, p, m // NC * P:(m // NC + 1) * P], ct_r[:, p, k0:k0 + w],
                                     start=True, stop=True).then_inc(max_ready, 1)

                def scores(u, i):
                    b, p, _, _ = u
                    pe.wait_ge(probs_ready, b * NQ + i - (i > 0) + PRIME)
                    for k, t in enumerate(quads[i]):
                        w = width(t)
                        o = s_ps[i % 2][0:w, k * S:(k + 1) * S]
                        nc.tensor.matmul(o, ct[:, p, t * P:t * P + w], q[:, p], start=True, stop=False)
                        last = nc.tensor.matmul(o, c["ones_r"][:, 0:w], diag[:, p], start=False, stop=True)
                    last.then_inc(s_ready, 1)

                def values(u, nxt, i):
                    b, p, _, _ = u
                    pe.wait_ge(probs_ready, b * NQ + i + 1 + PRIME)
                    if i == 0:
                        pe.wait_ge(av_copied, b + PRIME)
                    for k, t in enumerate(quads[i]):
                        w = width(t)
                        last = nc.tensor.matmul(av_ps[:, 0:S], cn[0:w, p, t], probs[0:w, i % 2, k], start=(t == 0), stop=(t == KT - 1))
                        if nxt and i and k < 3:
                            maxima(nxt, 3 * i - 3 + k)
                    last.then_inc(probs_used, 1)

                def ahead(u):
                    for m in range(NM):
                        maxima(u, m)

                def step(u, nxt):
                    b, p, _, _ = u
                    pe.wait_ge(diag_ready, b + 1 + PRIME)
                    pe.wait_ge(loaded[p], half(b, p) * 48 + 48)
                    scores(u, 0)
                    for i in range(NQ):
                        if i + 1 < NQ:
                            scores(u, i + 1)
                        if nxt and i == NQ - 1:
                            maxima(nxt, 6)
                            maxima(nxt, 7)
                        values(u, nxt if i < NQ - 1 else None, i)
                    pe.wait_ge(added, (b + 1) * (NQ - 1) + PRIME)
                    pe.wait_ge(rsum_ready, b + PRIME)
                    for k in range(4):
                        last = nc.tensor.matmul(sum_ps[:, 0:S], c["ones"][:], acc[:, k], start=(k == 0), stop=(k == 3))
                    last.then_inc(sum_ready, 1)

                units(pe, 1, ahead, step)


def gated_memory(nc, src, c, name, layer, x_d, mem_d, out_d, w_proj=None, proj_d=None):
    with Phase(nc, name) as ph:
        x, mem = ph.sb("x", [P, 2, DC, S]), ph.sb("mem", [P, 2, S])
        wm, wg = ph.sb("wm", [P, D]), ph.sb("wg", [P, 2 * DC, D])
        wp = ph.sb("wp", [P, DC, C])
        neg_b = ph.sb("neg_b", [P, DC])
        mc, e = ph.sb("mc", [P, 2, DC, S]), ph.sb("e", [P, DC, S])
        e1, g, gm = ph.sb("e1", [P, DC, S]), ph.sb("g", [P, DC, S]), ph.sb("gm", [P, DC, S])
        f, sq, ln, rs = ph.sb("f", [P, DC, S]), ph.sb("sq", [P, DC, S]), ph.sb("ln", [P, S]), ph.sb("rs", [P, S])
        out, pr = ph.sb("out", [P, 2, DC, S]), ph.sb("pr", [P, 2, S])
        mc_ps, g_ps, var_ps, pr_ps = ph.banks("mc", 2), ph.banks("g", 2), ph.banks("var", 1), ph.banks("pr", 1)
        loaded, stored, pr_stored, w_ready = ph.sems2("loaded"), ph.sems2("stored"), ph.sems2("pr_stored"), ph.sem("w_ready")
        b_ready, mcp_ready, mc_ready, gp_ready, e_ready, steps, f_ready = (
            ph.sem(n) for n in ("b_ready", "mcp_ready", "mc_ready", "gp_ready", "e_ready", "steps", "f_ready"))
        sq_ready, var_ready, ln_ready, rs_ready, out_ready, pr_ready, pr_copied = (
            ph.sem(n) for n in ("sq_ready", "var_ready", "ln_ready", "rs_ready", "out_ready", "pr_ready", "pr_copied"))
        project = proj_d is not None
        with nc.Block() as block:
            @block.sync
            def _(sp):
                prime(sp, *stored, *pr_stored)
                sp.dma_start(wm[:], src[layer + "_mem_t"]).then_inc(w_ready, 16)
                sp.dma_start(wg[:], src[layer + "_gate"]).then_inc(w_ready, 16)
                if project:
                    sp.dma_start(wp[:], w_proj).then_inc(w_ready, 16)

                def load(u):
                    b, p, _, _ = u
                    sp.wait_ge(out_ready, b - 1 + PRIME)
                    sp.dma_start(x[:, p], x_d[b]).then_inc(loaded[p], 16)
                    sp.dma_start(mem[:, p], mem_d[b]).then_inc(loaded[p], 16)

                def step(u, nxt):
                    if nxt:
                        load(nxt)
                    b, p, _, _ = u
                    sp.wait_ge(out_ready, b + 1 + PRIME)
                    sp.dma_start(out_d[b], out[:, p]).then_inc(stored[p], 16)
                    if project:
                        sp.wait_ge(pr_copied, b + 1 + PRIME)
                        sp.dma_start(proj_d[b], pr[:, p]).then_inc(pr_stored[p], 16)

                units(sp, 1, load, step)
                for p in range(2):
                    sp.wait_ge(stored[p], B // 2 * 16 + PRIME)
                    if project:
                        sp.wait_ge(pr_stored[p], B // 2 * 16 + PRIME)

            @block.scalar
            def _(act):
                act.preload_act_table_set(EXP_LN)
                prime(act, mc_ready, e_ready, sq_ready, ln_ready, rs_ready, pr_copied)
                act.wait_ge(b_ready, 1)

                def ahead(u):
                    b, p, _, _ = u
                    act.wait_ge(mcp_ready, b + 1 + PRIME)
                    act.wait_ge(gp_ready, b - 1 + PRIME)
                    act.wait_ge(f_ready, b - 1 + PRIME)
                    nc.scalar.activation(mc[:, p], mc_ps[p][:].rearrange("p (m s) -> p m s", m=DC), ACT.Copy).then_inc(mc_ready, 1)

                def step(u, nxt):
                    b, p, _, _ = u
                    act.wait_ge(gp_ready, b + 1 + PRIME)
                    act.wait_ge(f_ready, b + PRIME)
                    for m in range(DC):
                        last = nc.scalar.activation(e[:, m], g_ps[p][:, m * S:(m + 1) * S], ACT.Exp, scale=-1.0,
                                                    bias=neg_b[:, m:m + 1])
                    last.then_inc(e_ready, 1)
                    if nxt:
                        ahead(nxt)
                    act.wait_ge(f_ready, b + 1 + PRIME)
                    act.wait_ge(var_ready, b + PRIME)
                    nc.scalar.activation(sq[:], f[:], ACT.Square).then_inc(sq_ready, 1)
                    act.wait_ge(var_ready, b + 1 + PRIME)
                    nc.scalar.activation(ln[:], var_ps[0][:, 0:S], ACT.Ln, bias=c["eps6"][:, 0:1]).then_inc(ln_ready, 1)
                    act.wait_ge(ln_ready, b + 1 + PRIME)
                    act.wait_ge(out_ready, b + PRIME)
                    nc.scalar.activation(rs[:], ln[:], ACT.Exp, scale=-0.5).then_inc(rs_ready, 1)
                    if project:
                        act.wait_ge(pr_ready, b + 1 + PRIME)
                        act.wait_ge(pr_stored[p], half(b, p) * 16 + PRIME)
                        nc.scalar.activation(pr[:, p], pr_ps[0][:, 0:S], ACT.Copy).then_inc(pr_copied, 1)

                units(act, 1, ahead, step)

            @block.vector
            def _(dve):
                prime(dve, f_ready, out_ready)
                nc.vector.tensor_scalar(neg_b[:], c[layer + "_bgate"][:], -1.0, None, ALU.mult).then_inc(b_ready, 1)

                def step(u, nxt):
                    b, p, _, _ = u
                    ch = Chain(dve, steps, b * 3)
                    dve.wait_ge(e_ready, b + 1 + PRIME)
                    ch.link(nc.vector.tensor_scalar(e1[:], e[:], BIG, 1.0, ALU.min, ALU.add))
                    ch.link(nc.vector.reciprocal(g[:], e1[:]))
                    dve.wait_ge(mc_ready, b + 1 + PRIME)
                    ch.link(nc.vector.tensor_tensor(gm[:], g[:], mc[:, p], ALU.mult))
                    dve.wait_ge(loaded[p], half(b, p) * 32 + 32)
                    dve.wait_ge(sq_ready, b + PRIME)
                    nc.vector.tensor_tensor(f[:], gm[:], x[:, p], ALU.add).then_inc(f_ready, 1)
                    dve.wait_ge(f_ready, b + 1 + PRIME)
                    dve.wait_ge(rs_ready, b + 1 + PRIME)
                    dve.wait_ge(stored[p], half(b, p) * 16 + PRIME)
                    if project:
                        dve.wait_ge(pr_ready, b - 1 + PRIME)
                    for k in range(DC):
                        last = nc.vector.scalar_tensor_tensor(out[:, p, k], f[:, k], c[layer + "_norm"][:, k:k + 1], rs[:],
                                                              ALU.mult, ALU.mult)
                    last.then_inc(out_ready, 1)

                units(dve, 1, lambda u: None, step)

            @block.tensor
            def _(pe):
                prime(pe, mcp_ready, gp_ready, var_ready, pr_ready)
                pe.wait_ge(w_ready, (2 + project) * 16)

                def ahead(u):
                    b, p, _, _ = u
                    pe.wait_ge(loaded[p], half(b, p) * 32 + 32)
                    pe.wait_ge(mc_ready, b - 1 + PRIME)
                    for m in range(DC):
                        last = nc.tensor.matmul(mc_ps[p][:, m * S:(m + 1) * S], wm[:, m * P:(m + 1) * P], mem[:, p],
                                                start=True, stop=True)
                    last.then_inc(mcp_ready, 1)
                    pe.wait_ge(mc_ready, b + 1 + PRIME)
                    pe.wait_ge(e_ready, b - 1 + PRIME)
                    for m in range(DC):
                        for k in range(2 * DC):
                            rhs = x[:, p, k] if k < DC else mc[:, p, k - DC]
                            last = nc.tensor.matmul(g_ps[p][:, m * S:(m + 1) * S], wg[:, k, m * P:(m + 1) * P], rhs,
                                                    start=(k == 0), stop=(k == 2 * DC - 1))
                    last.then_inc(gp_ready, 1)

                def step(u, nxt):
                    b, p, _, _ = u
                    if nxt:
                        ahead(nxt)
                    pe.wait_ge(sq_ready, b + 1 + PRIME)
                    pe.wait_ge(ln_ready, b + PRIME)
                    for k in range(DC):
                        last = nc.tensor.matmul(var_ps[0][:, 0:S], c["mean"][:], sq[:, k], start=(k == 0), stop=(k == DC - 1))
                    last.then_inc(var_ready, 1)
                    if project:
                        pe.wait_ge(out_ready, b + 1 + PRIME)
                        pe.wait_ge(pr_copied, b + PRIME)
                        for k in range(DC):
                            last = nc.tensor.matmul(pr_ps[0][:, 0:S], wp[:, k], out[:, p, k], start=(k == 0), stop=(k == DC - 1))
                        last.then_inc(pr_ready, 1)

                units(pe, 1, ahead, step)


def build(nc, src, out):
    def scratch(name, shape, dt=F32):
        return nc.dram_tensor("d_" + name, shape, dt, kind="Internal").ap()

    with ExitStack() as ctx:
        def keep(name, shape, dt=F32):
            return ctx.enter_context(nc.sbuf_tensor("c_" + name, shape, dt))

        c = {"ident": keep("ident", [P, P]), "ones": keep("ones", [P, P]), "rot": keep("rot", [P, P]),
             "headmask": keep("headmask", [P, P // SHD]), "causal_t": keep("causal_t", [P, 2, S]),
             "sum16": keep("sum16", [P, P]), "sum8": keep("sum8", [P, P]), "low": keep("low", [P, 5])}
        c["loads"] = {k: src["c_" + k] for k in c}
        vectors = {"ln_in_w": DC, "ln_post_attn_w": DC, "ln_post_cross_w": DC, "ln_q_g": DC, "ln_q_b": DC,
                   "ln_ff_g": DC, "ln_ff_b": DC, "L2_bgate": DC, "L2_norm": DC, "L3_bgate": DC, "L3_norm": DC}
        for k, n in vectors.items():
            c[k] = keep(k, [P, n])
            c["loads"][k] = src[k]
        for k in ("attn_gate", "ff_gate"):
            c[k] = keep(k, [P, 1])
            c["loads"][k] = src[k][0].partition_broadcast(P)
        for k, shape, dt in (("mean", [P, P], F32), ("cos", [P, S], F32), ("sin", [P, S], F32), ("vm", [P, B, S], F32),
                             ("ident_b", [P, P], BF16), ("ones_r", [P, P], F32R), ("sel_r", [P, 4, P], F32R),
                             ("causal", [P, 2, S], BF16), ("causal_tb", [P, 2, S], BF16), ("key_bias", [P, B, KT], F32),
                             ("eps6", [P, 1], F32), ("eps5", [P, 1], F32), ("tanh_gate", [P, 2], F32)):
            c[k] = keep(k, shape, dt)
        load_constants(nc, src, c)
        masked_d = scratch("masked_ctx", [B, P, NKP])
        q_d, k_d = (scratch(n, [B, P, 2, S]) for n in ("self_q", "self_k"))
        v_d = scratch("self_v", [B, P, 2, NH, 32])
        self_projections(nc, src, c, q_d, k_d, v_d)
        self_d = scratch("self_out", [B, P, NG, S])
        self_attention(nc, c, q_d, k_d, v_d, self_d)
        x1_d = scratch("x1", [B, P, DC, S])
        cross = scratch("cross", [B, P, 2, NG, S])
        cq_d, cross_d = cross[:, :, 0], cross[:, :, 1]
        residual_norm(nc, c, "selfout", src["x_t"], "rms", c["ln_post_cross_w"], attn_d=self_d,
                      w_attn=(src["v_dense"], src["l_dense"]), experts=True, x_out_d=x1_d,
                      w_proj=src["cq_stack"], proj_d=cq_d, split=True)
        cross_attention_0(nc, src, c, cq_d, cross_d)
        x2_d, n2_d, x3_d = (scratch(n, [B, P, DC, S]) for n in ("x2", "n2", "x3"))
        residual_norm(nc, c, "crossout", x1_d, "rms", c["ln_post_attn_w"], attn_d=cross_d, w_attn=(src["cdense"],),
                      x_out_d=x2_d, normed_d=n2_d)
        feed_forward(nc, src, c, "ffn0", x2_d, n2_d, [src[k] for k in ("v_gate", "v_up", "l_gate", "l_up")],
                     [src["v_down"], src["l_down"]], x3_d, silu=True, masked_d=masked_d)
        cross1 = scratch("cross1", [B, P, 2, NP, S])
        q1_d, out1_d = cross1[:, :, 0], cross1[:, :, 1]
        residual_norm(nc, c, "query1", x3_d, "layer", c["ln_q_g"], c["ln_q_b"], w_proj=src["Wq"], proj_d=q1_d)
        cross_attention_1(nc, src, c, masked_d, q1_d, out1_d)
        x4_d, n4_d, x5_d, x6_d = (scratch(n, [B, P, DC, S]) for n in ("x4", "n4", "x5", "x6"))
        q2_d, q3_d, m2_d, m3_d = (scratch(n, [B, P, S]) for n in ("q2", "q3", "m2", "m3"))
        residual_norm(nc, c, "out1", x3_d, "layer", c["ln_ff_g"], c["ln_ff_b"], attn_d=out1_d, w_attn=(src["Wo"],),
                      gate=c["tanh_gate"][:, 0:1], x_out_d=x4_d, normed_d=n4_d)
        feed_forward(nc, src, c, "ffn1", x4_d, n4_d, [src["W1"]], [src["W2"]], x5_d, silu=False,
                     gate=c["tanh_gate"][:, 1:2], w_proj=src["L2_mem"], proj_d=q2_d)
        memory_attention(nc, src, c, "mem2", q2_d, m2_d)
        gated_memory(nc, src, c, "gated2", "L2", x5_d, m2_d, x6_d, w_proj=src["L3_mem"], proj_d=q3_d)
        memory_attention(nc, src, c, "mem3", q3_d, m3_d)
        gated_memory(nc, src, c, "gated3", "L3", x6_d, m3_d, out)


def _inputs(inputs):
    n = {k: np.asarray(v) for k, v in inputs.items()}
    f32 = np.float32
    x, ctx = n["x"], n["ctx_1024"]
    mask = n["mask_BxS2_bk0"].view(np.uint8)

    def rows(w):
        return np.ascontiguousarray(w.reshape(-1, P, w.shape[-1]).transpose(1, 0, 2))

    def cols(w):
        return np.ascontiguousarray(w.reshape(-1, P).T)

    a = {
        "x_t": x.reshape(B, S, DC, P).transpose(0, 3, 2, 1),
        "ctx_t": np.concatenate([ctx, ctx[:, NK - 1:NK]], axis=1)[:, :NKP].transpose(0, 2, 1),
        "ctx_n": np.concatenate([ctx, np.zeros((B, KT * P - NK, C), f32)], axis=1).reshape(B, KT, P, C).transpose(0, 2, 1, 3),
        "tok_mask": n["mask_BxS_ik0"], "pos": n["pos_1xS"],
        "key_mask": np.concatenate([mask, mask[:, NK - 1:NK], np.zeros((B, 4 * MW - NK - 1), np.uint8)], axis=1).view(np.int32),
        "key_mask_t": np.ascontiguousarray(np.concatenate([mask, np.zeros((B, KT * P - NK), np.uint8)], axis=1).reshape(
            B, KT, P).transpose(2, 0, 1)).reshape(P, B * KT).view(np.int32),
        "ln_in_w": cols(n["L0_xattn_ln_in_w"]), "ln_post_attn_w": cols(n["L0_xattn_ln_post_attn_w"]),
        "ln_post_cross_w": cols(n["L0_xattn_ln_post_cross_w"]),
        "v_qkv": rows(n["L0_xattn_v_qkv"]), "l_qkv": rows(n["L0_xattn_l_qkv"]),
    }
    def spread(w, width):
        out = np.zeros((NG, 4, 32, w.shape[1]), f32)
        out[:, :, :width] = w.reshape(NG, 4, width, w.shape[1])
        return rows(out.reshape(NG * P, -1))

    a["v_dense"], a["l_dense"] = spread(n["L0_xattn_v_dense"], SHD), spread(n["L0_xattn_l_dense"], SHD)
    a["cdense"] = spread(n["L0_xattn_cdense_w"], CHD)

    def stacked(w):
        out = np.zeros((w.shape[0], NH, 4, CHD), f32)
        out[:, :, 1:] = w.reshape(w.shape[0], NH, 1, CHD)
        return out.reshape(w.shape[0], NH * 32)

    a["cq_stack"] = rows(stacked(n["L0_xattn_cq_w"]))
    a["ck_stack"] = stacked(n["L0_xattn_ckv_w"][:, :C])
    a["cv"] = n["L0_xattn_ckv_w"][:, C:]
    for k in ("v_gate", "v_up", "l_gate", "l_up"):
        w = n["L0_xattn_" + k]
        a[k] = rows(np.concatenate([w, np.zeros((D, -FF0 % P), f32)], axis=1))
    for k in ("v_down", "l_down"):
        w = n["L0_xattn_" + k]
        a[k] = rows(np.concatenate([w, np.zeros((-FF0 % P, D), f32)]))
    for k in ("ln_q_g", "ln_q_b", "ln_ff_g", "ln_ff_b"):
        a[k] = cols(n["L1_xattn_" + k])
    a["attn_gate"], a["ff_gate"] = n["L1_xattn_attn_gate"].reshape(1, 1), n["L1_xattn_ff_gate"].reshape(1, 1)
    a["Wq"], a["W1"], a["W2"], a["Wo"] = (rows(n["L1_xattn_" + k]) for k in ("Wq", "W1", "W2", "Wo"))
    a["Wkv"] = n["L1_xattn_Wkv"]
    for layer in ("L2", "L3"):
        a[layer + "_mem"] = rows(n[layer + "_xattn_W_mem"])
        a[layer + "_mem_t"] = n[layer + "_xattn_W_mem"].T
        a[layer + "_gate"] = rows(n[layer + "_xattn_W_gate"].T)
        a[layer + "_bgate"], a[layer + "_norm"] = cols(n[layer + "_xattn_b_gate"]), cols(n[layer + "_xattn_norm_w"])

    eye = np.eye(P, dtype=f32)
    a["c_ident"], a["c_ones"] = eye, np.ones((P, P), f32)
    a["c_iota"] = (np.arange(P)[:, None] + P * np.arange(2)[None, :]).astype(f32)
    inv = (f32(1) / f32(10000) ** (np.arange(0, SHD, 2, dtype=f32) / f32(SHD))).astype(f32)
    angle = np.outer(np.arange(S, dtype=f32), inv).astype(f32)
    table = np.stack([np.tile(np.concatenate([f(angle), f(angle)], axis=1), (1, P // SHD)) for f in (np.cos, np.sin)])
    a["c_rope"] = table.astype(f32).reshape(2, 2, P, P).transpose(2, 0, 1, 3)
    rot = np.zeros((P, P), f32)
    for m in range(P):
        if m % SHD < SHD // 2:
            rot[m + SHD // 2, m] = -1
        else:
            rot[m - SHD // 2, m] = 1
    a["c_rot"] = rot
    key, query = np.arange(S)[None, :], np.arange(S)[:, None]
    bias = np.where(key > query, -BIG, 0.0).astype(f32)
    a["c_causal"] = bias.reshape(2, P, S).transpose(1, 0, 2)
    a["c_causal_t"] = bias.T.reshape(2, P, S).transpose(1, 0, 2)
    a["c_headmask"] = (np.arange(P)[:, None] // SHD == np.arange(P // SHD)[None, :]).astype(f32)
    sel = np.zeros((P, 4, P), f32)
    for j in range(4):
        sel[:, j, 32 * j] = 1
    a["c_sel"] = sel
    for width in (SHD, CHD):
        m = np.zeros((P, P), f32)
        for j in range(P):
            m[j // 32 * 32 + width, j] = 1
        a[f"c_sum{width}"] = m
    low = np.zeros((P, 5), f32)
    block = np.arange(P) % 32 // CHD
    low[:, 0] = np.where(block == 2, 1, 0)
    low[:, 1] = np.where(block == 3, 1, 0)
    low[:, 2] = np.arange(P) % 32 == 0
    low[:, 3:5] = 1 - 2 * low[:, 0:2]
    a["c_low"] = low
    return {k: np.ascontiguousarray(v) for k, v in a.items()}


def kernel(**inputs):
    from concourse import bacc
    from concourse.bass_utils import run_bass_kernel_spmd

    nc = bacc.Bacc("TRN2", target_bir_lowering=False, num_devices=1)
    arrays = _inputs(inputs)
    src = {k: nc.dram_tensor("in_" + k, v.shape, mybir.dt.from_np(v.dtype), kind="ExternalInput").ap()
           for k, v in arrays.items()}
    out = nc.dram_tensor("out_t", (B, P, DC, S), F32, kind="ExternalOutput").ap()
    build(nc, src, out)
    r = run_bass_kernel_spmd(nc, [{"in_" + k: v for k, v in arrays.items()}], core_ids=[0])
    return np.ascontiguousarray(r.results[0]["out_t"].transpose(0, 3, 2, 1).reshape(B, S, D))
```
